# Optimizing a Trainium2 kernel written in Bass

```python
import numpy as np
import jax
import jax.numpy as jnp

def _softmax(x, axis=-1):
    return jax.nn.softmax(x, axis=axis)

def _gelu(x):
    return jax.nn.gelu(x, approximate=True)

def _silu(x):
    return jax.nn.silu(x)

def _sigmoid(x):
    return jax.nn.sigmoid(x)

def _layernorm(x, axis=-1, eps=1e-05):
    m = jnp.mean(x, axis=axis, keepdims=True)
    v = jnp.var(x, axis=axis, keepdims=True)
    return (x - m) / jnp.sqrt(v + eps)

def _scatter_add(tgt, idx, src, axis=0):
    return tgt.at[idx].add(src)

def _segment_sum(src, seg, n):
    return jax.ops.segment_sum(src, seg, n)
kernel_name = 'mk_vit_tower_postln_d1_tok_img256_r4_00bbb9'

def setup_inputs(seed: int=0):
    np.random.seed(seed)
    _w = jnp.asarray

    def _rec_inputs():
        import jax
        import jax.numpy as jnp
        _rk = jax.random.key(seed)
        x = -0.000928989 + 1.00043 * jax.random.normal(jax.random.fold_in(_rk, 1), (64, 64, 64, 1), jnp.float32)
        return x
    x = _rec_inputs()

    def _L0_tok_setup():
        import jax, jax.numpy as jnp
        import numpy as np
        B, S, D_A, D_V, D_U, L, M1, M2 = (16, 64, 3, 32, 1, 4, 12, 12)
        MID = 4 * D_U

        def conv1x1(x, w, b):
            return jnp.einsum('bixy,oi->boxy', x, w) + b[None, :, None, None]

        def fourier_layer(x, fw_i):
            Bm, C, M, N = x.shape
            x_ft = jnp.fft.rfft2(x, s=(M, N), norm='ortho')
            w_lo = fw_i[0, ..., 0] + 1j * fw_i[0, ..., 1]
            w_hi = fw_i[1, ..., 0] + 1j * fw_i[1, ..., 1]
            lo = jnp.einsum('bixy,ioxy->boxy', x_ft[:, :, :M1, :M2], w_lo)
            hi = jnp.einsum('bixy,ioxy->boxy', x_ft[:, :, -M1:, :M2], w_hi)
            out_ft = jnp.zeros(x_ft.shape, dtype=x_ft.dtype)
            out_ft = out_ft.at[:, :, :M1, :M2].set(lo)
            out_ft = out_ft.at[:, :, -M1:, :M2].set(hi)
            return jnp.fft.irfft2(out_ft, s=(M, N), norm='ortho')

        def make_grid(b, sx, sy):
            gx = jnp.broadcast_to(jnp.linspace(0.0, 1.0, sx)[None, :, None], (b, sx, sy))
            gy = jnp.broadcast_to(jnp.linspace(0.0, 1.0, sy)[None, None, :], (b, sx, sy))
            return jnp.stack([gx, gy], axis=-1)
        key = jax.random.key(seed)
        ks = jax.random.split(key, 12)
        sc_v = 1.0 / np.sqrt(D_V)
        inp = {'x': jax.random.normal(ks[0], (B, S, S, D_A - 2), dtype=jnp.float32), 'p_w': jax.random.normal(ks[1], (D_V, D_A), dtype=jnp.float32) / np.sqrt(D_A), 'p_b': jnp.zeros((D_V,), dtype=jnp.float32), 'fw': jax.random.normal(ks[2], (L, 2, D_V, D_V, M1, M2, 2), dtype=jnp.float32) * sc_v, 'w1_w': jax.random.normal(ks[3], (L, D_V, D_V), dtype=jnp.float32) * sc_v, 'w1_b': jnp.zeros((L, D_V), dtype=jnp.float32), 'w2_w': jax.random.normal(ks[4], (L, D_V, D_V), dtype=jnp.float32) * sc_v, 'w2_b': jnp.zeros((L, D_V), dtype=jnp.float32), 'q1_w': jax.random.normal(ks[5], (MID, D_V), dtype=jnp.float32) * sc_v, 'q1_b': jnp.zeros((MID,), dtype=jnp.float32), 'q2_w': jax.random.normal(ks[6], (D_U, MID), dtype=jnp.float32) / np.sqrt(MID), 'q2_b': jnp.zeros((D_U,), dtype=jnp.float32)}
        return inp
    _L0_tok_all = _L0_tok_setup()
    _L0_tok_in = {k: v for k, v in _L0_tok_all.items() if k in ('p_w', 'p_b', 'fw', 'w1_w', 'w1_b', 'w2_w', 'w2_b', 'q1_w', 'q1_b', 'q2_w', 'q2_b')}
    del _L0_tok_all

    def _L0_attn_setup():
        import jax, jax.numpy as jnp
        import numpy as np
        HEAD_SIZE = 64
        HEAD_SIZE_R = HEAD_SIZE // 4
        HEAD_SIZE_C = HEAD_SIZE - HEAD_SIZE_R
        N_EMBD = 64

        def rope(x, start_pos=0):
            B, T, d = x.shape
            half = d // 2
            theta = 1.0 / 10000.0 ** (jnp.arange(half, dtype=x.dtype) / half)
            idx = jnp.arange(start_pos, start_pos + T, dtype=x.dtype)[:, None] * theta[None, :]
            sin, cos = (jnp.sin(idx), jnp.cos(idx))
            xs = x.reshape(B, T, half, 2)
            x1, x2 = (xs[..., 0], xs[..., 1])
            rot = jnp.stack([x1 * cos - x2 * sin, x1 * sin + x2 * cos], axis=-1)
            return rot.reshape(B, T, d)

        def _reference_tuple_inner(x, Wq_comp, Wkv_comp, Wqc, Wqr, Wkc, Wkr, Wv):
            c_q = x @ Wq_comp
            c_kv = x @ Wkv_comp
            q_c = c_q @ Wqc
            q_r = rope(c_q @ Wqr, start_pos=0)
            q = jnp.concatenate([q_c, q_r], axis=-1)
            k_c = c_kv @ Wkc
            k_r = rope(c_kv @ Wkr, start_pos=0)
            k = jnp.concatenate([k_c, k_r], axis=-1)
            v = c_kv @ Wv
            scale = 1.0 / jnp.sqrt(jnp.asarray(HEAD_SIZE, dtype=x.dtype))
            wei = jnp.einsum('bqd,bkd->bqk', q, k) * scale
            T_q = q.shape[1]
            mask = jnp.tril(jnp.ones((T_q, T_q), dtype=bool))
            wei = jnp.where(mask, wei, jnp.asarray(-jnp.inf, dtype=wei.dtype))
            wei = jax.nn.softmax(wei, axis=-1)
            out = jnp.einsum('bqk,bkd->bqd', wei, v)
            return (out, (k, v))
        key = jax.random.key(seed)
        ks = jax.random.split(key, 8)
        B, T = (32, 512)
        s = 0.05
        return {'x': jax.random.normal(ks[0], (B, T, N_EMBD), dtype=jnp.float32), 'Wq_comp': jax.random.normal(ks[1], (N_EMBD, N_EMBD), dtype=jnp.float32) * s, 'Wkv_comp': jax.random.normal(ks[2], (N_EMBD, N_EMBD), dtype=jnp.float32) * s, 'Wqc': jax.random.normal(ks[3], (N_EMBD, HEAD_SIZE_C), dtype=jnp.float32) * s, 'Wqr': jax.random.normal(ks[4], (N_EMBD, HEAD_SIZE_R), dtype=jnp.float32) * s, 'Wkc': jax.random.normal(ks[5], (N_EMBD, HEAD_SIZE_C), dtype=jnp.float32) * s, 'Wkr': jax.random.normal(ks[6], (N_EMBD, HEAD_SIZE_R), dtype=jnp.float32) * s, 'Wv': jax.random.normal(ks[7], (N_EMBD, HEAD_SIZE), dtype=jnp.float32) * s}
    _L0_attn_all = _L0_attn_setup()
    _L0_attn_in = {k: v for k, v in _L0_attn_all.items() if k in ('Wq_comp', 'Wkv_comp', 'Wqc', 'Wqr', 'Wkc', 'Wkr', 'Wv')}
    del _L0_attn_all

    def _L0_ffn_setup():
        import jax, jax.numpy as jnp
        import numpy as np
        E, D, H, TOP_K = (6, 64, 64, 2)
        ROUTER_H = D // 2
        key = jax.random.key(seed)
        ks = jax.random.split(key, 12)
        s = 1.0 / np.sqrt(D)
        sh = 1.0 / np.sqrt(H)
        sr = 1.0 / np.sqrt(ROUTER_H)
        return {'features': jax.random.normal(ks[0], (8, 1024, D), dtype=jnp.float32), 'router_w1': jax.random.uniform(ks[1], (D, ROUTER_H), jnp.float32, -s, s), 'router_b1': jnp.zeros((ROUTER_H,), jnp.float32), 'router_w2': jax.random.uniform(ks[2], (ROUTER_H, E), jnp.float32, -sr, sr), 'router_b2': jnp.zeros((E,), jnp.float32), 'expert_w1': jax.random.uniform(ks[3], (E, D, H), jnp.float32, -s, s), 'expert_b1': jnp.zeros((E, H), jnp.float32), 'expert_w2': jax.random.uniform(ks[4], (E, H, H), jnp.float32, -sh, sh), 'expert_b2': jnp.zeros((E, H), jnp.float32), 'expert_w3': jax.random.uniform(ks[5], (E, H, D), jnp.float32, -sh, sh), 'expert_b3': jnp.zeros((E, D), jnp.float32)}
    _L0_ffn_all = _L0_ffn_setup()
    _L0_ffn_in = {k: v for k, v in _L0_ffn_all.items() if k in ('router_w1', 'router_b1', 'router_w2', 'router_b2', 'expert_w1', 'expert_b1', 'expert_w2', 'expert_b2', 'expert_w3', 'expert_b3')}
    del _L0_ffn_all
    return {'x': x, 'L0_tok_p_w': _L0_tok_in['p_w'], 'L0_tok_p_b': _L0_tok_in['p_b'], 'L0_tok_fw': _L0_tok_in['fw'], 'L0_tok_w1_w': _L0_tok_in['w1_w'], 'L0_tok_w1_b': _L0_tok_in['w1_b'], 'L0_tok_w2_w': _L0_tok_in['w2_w'], 'L0_tok_w2_b': _L0_tok_in['w2_b'], 'L0_tok_q1_w': _L0_tok_in['q1_w'], 'L0_tok_q1_b': _L0_tok_in['q1_b'], 'L0_tok_q2_w': _L0_tok_in['q2_w'], 'L0_tok_q2_b': _L0_tok_in['q2_b'], 'L0_attn_Wq_comp': _L0_attn_in['Wq_comp'], 'L0_attn_Wkv_comp': _L0_attn_in['Wkv_comp'], 'L0_attn_Wqc': _L0_attn_in['Wqc'], 'L0_attn_Wqr': _L0_attn_in['Wqr'], 'L0_attn_Wkc': _L0_attn_in['Wkc'], 'L0_attn_Wkr': _L0_attn_in['Wkr'], 'L0_attn_Wv': _L0_attn_in['Wv'], 'L0_ffn_router_w1': _L0_ffn_in['router_w1'], 'L0_ffn_router_b1': _L0_ffn_in['router_b1'], 'L0_ffn_router_w2': _L0_ffn_in['router_w2'], 'L0_ffn_router_b2': _L0_ffn_in['router_b2'], 'L0_ffn_expert_w1': _L0_ffn_in['expert_w1'], 'L0_ffn_expert_b1': _L0_ffn_in['expert_b1'], 'L0_ffn_expert_w2': _L0_ffn_in['expert_w2'], 'L0_ffn_expert_b2': _L0_ffn_in['expert_b2'], 'L0_ffn_expert_w3': _L0_ffn_in['expert_w3'], 'L0_ffn_expert_b3': _L0_ffn_in['expert_b3']}

def reference(x, L0_tok_p_w, L0_tok_p_b, L0_tok_fw, L0_tok_w1_w, L0_tok_w1_b, L0_tok_w2_w, L0_tok_w2_b, L0_tok_q1_w, L0_tok_q1_b, L0_tok_q2_w, L0_tok_q2_b, L0_attn_Wq_comp, L0_attn_Wkv_comp, L0_attn_Wqc, L0_attn_Wqr, L0_attn_Wkc, L0_attn_Wkr, L0_attn_Wv, L0_ffn_router_w1, L0_ffn_router_b1, L0_ffn_router_w2, L0_ffn_router_b2, L0_ffn_expert_w1, L0_ffn_expert_b1, L0_ffn_expert_w2, L0_ffn_expert_b2, L0_ffn_expert_w3, L0_ffn_expert_b3):
    import jax
    import jax.numpy as jnp

    def _L0_tok_ref(x, p_w, p_b, fw, w1_w, w1_b, w2_w, w2_b, q1_w, q1_b, q2_w, q2_b):
        import jax, jax.numpy as jnp
        import numpy as np
        B, S, D_A, D_V, D_U, L, M1, M2 = (16, 64, 3, 32, 1, 4, 12, 12)
        MID = 4 * D_U

        def conv1x1(x, w, b):
            return jnp.einsum('bixy,oi->boxy', x, w) + b[None, :, None, None]

        def fourier_layer(x, fw_i):
            Bm, C, M, N = x.shape
            x_ft = jnp.fft.rfft2(x, s=(M, N), norm='ortho')
            w_lo = fw_i[0, ..., 0] + 1j * fw_i[0, ..., 1]
            w_hi = fw_i[1, ..., 0] + 1j * fw_i[1, ..., 1]
            lo = jnp.einsum('bixy,ioxy->boxy', x_ft[:, :, :M1, :M2], w_lo)
            hi = jnp.einsum('bixy,ioxy->boxy', x_ft[:, :, -M1:, :M2], w_hi)
            out_ft = jnp.zeros(x_ft.shape, dtype=x_ft.dtype)
            out_ft = out_ft.at[:, :, :M1, :M2].set(lo)
            out_ft = out_ft.at[:, :, -M1:, :M2].set(hi)
            return jnp.fft.irfft2(out_ft, s=(M, N), norm='ortho')

        def make_grid(b, sx, sy):
            gx = jnp.broadcast_to(jnp.linspace(0.0, 1.0, sx)[None, :, None], (b, sx, sy))
            gy = jnp.broadcast_to(jnp.linspace(0.0, 1.0, sy)[None, None, :], (b, sx, sy))
            return jnp.stack([gx, gy], axis=-1)
        b, sx, sy = (x.shape[0], x.shape[1], x.shape[2])
        grid = make_grid(b, sx, sy)
        h = jnp.concatenate([x, grid], axis=-1)
        h = jnp.transpose(h, (0, 3, 1, 2))
        h = conv1x1(h, p_w, p_b)
        for i in range(L):
            x1 = fourier_layer(h, fw[i])
            x1 = jax.nn.relu(conv1x1(x1, w1_w[i], w1_b[i]))
            x1 = conv1x1(x1, w2_w[i], w2_b[i])
            h = h + x1
        h = conv1x1(h, q1_w, q1_b)
        h = jax.nn.relu(h)
        h = conv1x1(h, q2_w, q2_b)
        return jnp.squeeze(h)

    def _L0_attn_ref(x, Wq_comp, Wkv_comp, Wqc, Wqr, Wkc, Wkr, Wv):
        import jax, jax.numpy as jnp
        import numpy as np
        HEAD_SIZE = 64
        HEAD_SIZE_R = HEAD_SIZE // 4
        HEAD_SIZE_C = HEAD_SIZE - HEAD_SIZE_R
        N_EMBD = 64

        def rope(x, start_pos=0):
            B, T, d = x.shape
            half = d // 2
            theta = 1.0 / 10000.0 ** (jnp.arange(half, dtype=x.dtype) / half)
            idx = jnp.arange(start_pos, start_pos + T, dtype=x.dtype)[:, None] * theta[None, :]
            sin, cos = (jnp.sin(idx), jnp.cos(idx))
            xs = x.reshape(B, T, half, 2)
            x1, x2 = (xs[..., 0], xs[..., 1])
            rot = jnp.stack([x1 * cos - x2 * sin, x1 * sin + x2 * cos], axis=-1)
            return rot.reshape(B, T, d)

        def _reference_tuple_inner(x, Wq_comp, Wkv_comp, Wqc, Wqr, Wkc, Wkr, Wv):
            c_q = x @ Wq_comp
            c_kv = x @ Wkv_comp
            q_c = c_q @ Wqc
            q_r = rope(c_q @ Wqr, start_pos=0)
            q = jnp.concatenate([q_c, q_r], axis=-1)
            k_c = c_kv @ Wkc
            k_r = rope(c_kv @ Wkr, start_pos=0)
            k = jnp.concatenate([k_c, k_r], axis=-1)
            v = c_kv @ Wv
            scale = 1.0 / jnp.sqrt(jnp.asarray(HEAD_SIZE, dtype=x.dtype))
            wei = jnp.einsum('bqd,bkd->bqk', q, k) * scale
            T_q = q.shape[1]
            mask = jnp.tril(jnp.ones((T_q, T_q), dtype=bool))
            wei = jnp.where(mask, wei, jnp.asarray(-jnp.inf, dtype=wei.dtype))
            wei = jax.nn.softmax(wei, axis=-1)
            out = jnp.einsum('bqk,bkd->bqd', wei, v)
            return (out, (k, v))
        return _reference_tuple_inner(x, Wq_comp, Wkv_comp, Wqc, Wqr, Wkc, Wkr, Wv)[0]

    def _L0_ffn_ref(features, router_w1, router_b1, router_w2, router_b2, expert_w1, expert_b1, expert_w2, expert_b2, expert_w3, expert_b3):
        import jax, jax.numpy as jnp
        import numpy as np
        E, D, H, TOP_K = (6, 64, 64, 2)
        ROUTER_H = D // 2
        rh = jax.nn.relu(features @ router_w1 + router_b1)
        expert_logits = jax.nn.softmax(rh @ router_w2 + router_b2, axis=-1)
        top_w, top_i = jax.lax.top_k(expert_logits, TOP_K)
        routing_weights = jax.nn.softmax(top_w, axis=-1)
        h1 = jax.nn.relu(jnp.einsum('bsd,edh->bseh', features, expert_w1) + expert_b1)
        h2 = jax.nn.relu(jnp.einsum('bseh,ehf->bsef', h1, expert_w2) + expert_b2)
        expert_out = jnp.einsum('bsef,efo->bseo', h2, expert_w3) + expert_b3
        sel = jnp.take_along_axis(expert_out, top_i[:, :, :, None], axis=2)
        combined = jnp.sum(sel * routing_weights[..., None], axis=2)
        return combined
    h = _L0_tok_ref(x, L0_tok_p_w, L0_tok_p_b, L0_tok_fw, L0_tok_w1_w, L0_tok_w1_b, L0_tok_w2_w, L0_tok_w2_b, L0_tok_q1_w, L0_tok_q1_b, L0_tok_q2_w, L0_tok_q2_b)
    h = _layernorm(h + _L0_attn_ref(h, L0_attn_Wq_comp, L0_attn_Wkv_comp, L0_attn_Wqc, L0_attn_Wqr, L0_attn_Wkc, L0_attn_Wkr, L0_attn_Wv), axis=-1)
    h = _layernorm(h + _L0_ffn_ref(h, L0_ffn_router_w1, L0_ffn_router_b1, L0_ffn_router_w2, L0_ffn_router_b2, L0_ffn_expert_w1, L0_ffn_expert_b1, L0_ffn_expert_w2, L0_ffn_expert_b2, L0_ffn_expert_w3, L0_ffn_expert_b3), axis=-1)
    return h

_drawn_inputs = setup_inputs


def setup_inputs(seed=0):
    import zlib

    import numpy as np

    out = dict(_drawn_inputs(seed))
    spreads = {'L0_tok_p_b': (0.0, 0.1),
     'L0_tok_w1_b': (0.0, 0.1),
     'L0_tok_w2_b': (0.0, 0.1),
     'L0_tok_q1_b': (0.0, 0.1),
     'L0_ffn_router_b1': (0.0, 0.1),
     'L0_ffn_router_b2': (0.0, 0.1),
     'L0_ffn_expert_b1': (0.0, 0.695),
     'L0_ffn_expert_b2': (0.0, 0.29),
     'L0_ffn_expert_b3': (0.0, 0.1)}
    factors = {'L0_attn_Wq_comp': 8.0,
     'L0_attn_Wqc': 8.0,
     'L0_attn_Wqr': 8.0,
     'L0_attn_Wkc': 8.0,
     'L0_attn_Wkr': 8.0}
    for name, (base, spread) in spreads.items():
        noise = np.random.default_rng([zlib.crc32(name.encode()), seed]).standard_normal(out[name].shape)
        drawn = base * np.exp(spread * noise) if base else spread * noise
        out[name] = jnp.asarray(drawn.astype(out[name].dtype))
    for name, factor in factors.items():
        out[name] = (out[name] * factor).astype(out[name].dtype)
    return out
```

```python
from contextlib import ExitStack

import numpy as np

import concourse.bass as bass
from concourse import mybir

F32 = mybir.dt.float32
ALU = mybir.AluOpType
ACT = mybir.ActivationFunctionType
AX = mybir.AxisListType

B, S, C, L, NQ = 64, 64, 32, 4, 4
NKX, NKY = 24, 12
BP = B // 2
OG = C // 4
K6 = NKY // 2
PM = K6 * 2 * NKX
D, E, HID, RH = 64, 6, 64, 32
HR = 16
GROUP = 4
NEG = -3.0e38

LAYOUT = [("ident", 128), ("row_inv", 128), ("col_inv", 256), ("col_fwd", 64), ("row_fwd", 224),
          ("gx_cols", 64), ("gy_part", 1), ("one", 128), ("gx_part", 2), ("gy_row", 64),
          ("same8", 8), ("pick_row", 64), ("rep", 256), ("pick_out", 32),
          ("cos_q", 64), ("sin_q", 64), ("cos_k", 64), ("sin_k", 64), ("causal", 64), ("rank", 6)]
AT = {}
for _name, _width in LAYOUT:
    AT[_name] = (sum(w for n, w in LAYOUT[:len(AT)]), _width)
NCONST = sum(w for _, w in LAYOUT)


def constants():
    f = {n: np.zeros((128, w), np.float64) for n, w in LAYOUT}
    kx = np.array(list(range(12)) + list(range(-12, 0)))
    ky = np.arange(NKY)
    pos = np.arange(S)
    tx = 2 * np.pi * np.outer(kx, pos) / S
    ty = 2 * np.pi * np.outer(ky, pos) / S
    f["ident"][:] = np.eye(128)
    for b in range(2):
        f["row_inv"][b * 24:b * 24 + 24, b * 64:b * 64 + 64] = np.cos(tx) / 8
        f["row_inv"][48 + b * 24:72 + b * 24, b * 64:b * 64 + 64] = -np.sin(tx) / 8
    v = np.zeros((K6, 2, 2, 4, 2, 2, S))
    for k in range(NKY):
        w = (1.0 if k == 0 else 2.0) / 8
        for o in range(4):
            v[k % K6, k // K6, 0, o, o // 2, o % 2] = w * np.cos(ty[k])
            v[k % K6, k // K6, 1, o, o // 2, o % 2] = w * np.sin(ty[k])
    f["col_inv"][:96] = v.reshape(96, 256)
    c = np.zeros((2, S, 2, 2, NKY))
    order = [K6 * (m % 2) + m // 2 for m in range(NKY)]
    for o in range(2):
        c[o, :, o, 0] = np.cos(ty[order]).T / 8
        c[o, :, o, 1] = -np.sin(ty[order]).T / 8
    f["col_fwd"][:, :48] = c.reshape(128, 48)
    d = np.zeros((2, 128, 112))
    for b in range(2):
        r = slice(b * 64, b * 64 + 64)
        re, im = slice(b * 24, b * 24 + 24), slice(64 + b * 24, 88 + b * 24)
        d[0, r, re], d[0, r, im] = np.cos(tx).T / 8, -np.sin(tx).T / 8
        d[1, r, re], d[1, r, im] = np.sin(tx).T / 8, np.cos(tx).T / 8
    f["row_fwd"][:] = d.transpose(1, 0, 2).reshape(128, 224)
    grid = np.linspace(0.0, 1.0, S, dtype=np.float32)
    p = np.arange(128)
    f["gx_cols"][:] = grid
    f["gy_part"][:, 0] = grid[p % 64]
    f["one"][:] = 1
    f["gx_part"][:] = np.stack([grid[p // 4], grid[32 + p // 4]], 1)
    f["gy_row"][:] = grid
    f["same8"][:] = (p[:, None] % 8) == np.arange(8)
    f["pick_row"][:] = (p[:, None] % 64) == np.arange(64)
    r = np.zeros((32, 2, 2, OG, 8))
    for ch in range(C):
        r[ch, ch % 2, (ch // 2) % 2, ch // 4] = 1
    f["rep"][:32] = r.reshape(32, 256)
    f["pick_out"][:] = (p[:, None] // 4) == np.arange(32)
    half = HR // 2
    theta = (1.0 / (np.float32(10000.0) ** (np.arange(half, dtype=np.float32) / np.float32(half)))).astype(np.float32)
    ang = (pos.astype(np.float32)[:, None] * theta[None]).astype(np.float32)
    cos, sin = np.ones((64, S)), np.zeros((64, S))
    for i in range(half):
        for s in range(2):
            cos[48 + 2 * i + s] = np.cos(ang[:, i])
            sin[48 + 2 * i + s] = (-1, 1)[s] * np.sin(ang[:, i])
    for n, m in (("cos", cos), ("sin", sin)):
        f[n + "_k"][:] = np.tile(m, (2, 1))
        f[n + "_q"][:] = np.tile(m, (2, 1)) / np.sqrt(D)
    f["causal"][:] = np.where(np.arange(64)[None] > (p % 64)[:, None], NEG, 0)
    f["rank"][:] = np.arange(E, 0, -1)
    return np.concatenate([f[n] for n, _ in LAYOUT], 1).astype(np.float32)


SMALL = [("q1T", 4), ("w2n", L * 32), ("comps", 8), ("q1b", 1), ("q2", 1), ("q2b", 1),
         ("b1", L * 2), ("w2b", L), ("WqcT", 64), ("WkvcT", 64), ("Wq", 64), ("Wqs", 64),
         ("Wk", 64), ("Wks", 64), ("Wv", 64), ("rw1", 32), ("rw2", 6), ("rb1", 1), ("rb2", 6),
         ("eb1", 3), ("eb2", 3), ("eb3", 384)]
SAT = {}
for _name, _width in SMALL:
    SAT[_name] = (sum(w for n, w in SMALL[:len(SAT)]), _width)
NSMALL = sum(w for _, w in SMALL)


def program(nc, x, fw, w12, pT, small, ew, const, out):
    with ExitStack() as ctx:
        def sb(name, *shape):
            return ctx.enter_context(nc.sbuf_tensor(name, [128, *shape], F32))

        def sem(name):
            return ctx.enter_context(nc.semaphore(name))

        ps = ctx.enter_context(nc.psum_tensor("ps", [128, 8, 512], F32))
        cs = sb("cs", NCONST)
        sm = sb("sm", NSMALL)

        def K(name):
            a, w = AT[name]
            return cs[:, a:a + w]

        def W(name):
            a, w = SAT[name]
            return sm[:, a:a + w]

        H = sb("H", BP, K6, 2, NKX)
        Z = sb("Z", K6, NKX, BP, 2)
        G = sb("G", BP, 2, 2, S)
        fws = sb("fws", K6 * NKX, 2, C)
        w1c = sb("w1c", 2, 128)
        w2c = sb("w2c", 128)
        pbd = sb("pbd", 128)
        dc = sb("dc", 2, K6, 2, NKX)
        qs_all = sb("qs_all", L, 2, 8, NQ)
        qs = sb("qs", 2, 8, NQ)
        Z1 = sb("Z1", K6, 2, 2, NKX)
        Zt = sb("Zt", OG, K6 * 2 * 2, 4)
        V = sb("V", OG, 128)
        R = sb("R", 2, 8, 2, OG, 8)
        RT = sb("RT", 4, 2, 2, 2, S)
        US = sb("US", OG, 128)
        U = sb("U", 2 * NKY, C)
        XS = sb("XS", NKY, 2, C)
        XT = sb("XT", PM)
        q1w2 = U[0:32, 0, 0:L * NQ]
        comp = sb("comp", 12)
        pab = sb("pab", NQ)
        selx = V[:, 0:2, :].rearrange("p a b -> p (a b)")
        S0 = sb("S0", 2, S)
        Xst = sb("Xst", GROUP, S)
        rin = R[:].rearrange("p a b c d e -> p (a b c d e)")[:, 0:1024].rearrange("p (h a) -> p h a", h=2)
        USe = US[:, 0:GROUP, :]
        Ue = U[:].rearrange("p a b -> p (a b)")[:, 0:384]
        zero_bias = sb("zero_bias", 1)

        load_s = sem("load_s")
        load_fw = sem("load_fw")
        load_w12 = sem("load_w12")
        load_p = sem("load_p")
        load_x = sem("load_x")
        wr_zero = sem("wr_zero")
        w_neg = sem("w_neg")
        w1_neg = sem("w1_neg")
        setup_pe = sem("setup_pe")
        setup_dve = sem("setup_dve")
        q_cur = sem("q_cur")
        e_pe = sem("e_pe"); e_act = sem("e_act"); e_dve = sem("e_dve"); h0_done = sem("h0_done")
        mix_pe = sem("mix_pe")
        z_act = sem("z_act"); z_dve = sem("z_dve")
        dc_ready = sem("dc_ready")
        h_whole = sem("h_whole")
        pe_w1 = sem("pe_w1"); pe_t = sem("pe_t"); pe_a = sem("pe_a"); pe_b = sem("pe_b")
        pe_c = sem("pe_c"); pe_tr = sem("pe_tr"); pe_tu = sem("pe_tu"); pe_d = sem("pe_d")
        pe_t2 = sem("pe_t2"); pe_w2 = sem("pe_w2"); pe_g = sem("pe_g")
        z1_re = sem("z1_re"); z1_im = sem("z1_im"); zt_0 = sem("zt_0"); zt_1 = sem("zt_1")
        v_ready = sem("v_ready")
        r_even = sem("r_even"); r_odd = sem("r_odd"); us_0 = sem("us_0"); us_1 = sem("us_1")
        rt_even = sem("rt_even"); rt_odd = sem("rt_odd"); u_ready = sem("u_ready")
        x_re = sem("x_re"); x_im = sem("x_im"); xt_ready = sem("xt_ready"); h_add = sem("h_add"); g_add = sem("g_add")
        stored = sem("stored")
        waited = sem("waited")
        tail_load = sem("tail_load")

        def r_part(h, q):
            return R[:].rearrange("p i g h o x -> p h o (i g) x")[:, h, 4 * q:4 * q + 4]

        def zt_copy(copy, half):
            src = ps[0:96, 4 + half, 0:384].rearrange("p (a g o) -> p g a o", g=OG, o=4)
            return copy(Zt[0:96, :, 12 * half:12 * half + 12, :], src)

        def xs_copy(copy, ri):
            return copy(XS[0:48, :, ri, :], ps[64 * ri:64 * ri + 48, 6, 0:384].rearrange("p (a c) -> p a c", c=C))

        block = ctx.enter_context(nc.Block())
        xd = x.rearrange("(g p i) x y o -> g (i x) p (y o)", p=GROUP, i=2)
        NG = BP // GROUP
        NB = K6 * NKX // 8 * 1
        Zf = Z[:].rearrange("p a b c d -> p (a b c d)")
        Hf = H[:].rearrange("p a b c d -> p (a b c d)")
        Ff = fws[:].rearrange("p a b c -> p (a b c)")
        NT = 16 * 128
        TOK, XTT, QT, KT = [Zf[:, NT * i:NT * i + NT] for i in range(4)]
        VT, PR, PT, Y1 = [Hf[:, NT * i:NT * i + NT] for i in range(4)]
        N1, N1T, T0, T1 = [Ff[:, NT * i:NT * i + NT] for i in range(4)]
        RHS = QT
        H1 = [KT[:, 512 * i:512 * i + 512] for i in range(3)]
        H2 = [VT[:, 512 * i:512 * i + 512] for i in range(3)]
        GP = PR[:, 0:1536]
        fo = sb("fo", 32)
        wb = sb("wb", 5, 128)
        wr1 = sb("wr1", 64)
        wr2 = sb("wr2", 2, E)
        ew1 = R[:].rearrange("p a b c d e -> p (a b c d e)")[:, 0:384]
        ew2 = R[:].rearrange("p a b c d e -> p (a b c d e)")[:, 384:768]
        ew3 = R[:].rearrange("p a b c d e -> p (a b c d e)")[:, 768:1152]
        st = sb("st", 4, 32)
        gt = sb("gt", 6, 32, E)
        gm = sb("gm", 6, 32)
        names = ["t_load", "w_ps", "w_rdy", "relu_a", "relu_d", "fo_rdy", "h_ps", "h_sb", "xt_ps", "xt_sb",
                 "qk_ps", "qk_mul", "qk_sb", "v_ps", "v_sb", "s_ps", "s_sh", "p_exp", "p_sb", "pt_ps", "pt_sb", "o_ps",
                 "ln_c", "ln_sq", "ln_v", "ln_std", "n1_sb", "nt_ps", "nt_sb", "rh_ps", "rh_sb", "lg_ps",
                 "lg_sh", "lg_exp", "g_dif", "g_exp", "gate", "l1_ps", "l1_sb", "l2_ps", "l2_sb", "l3_ps", "l3_rd", "y_sb"]
        T = {n: sem("t_" + n) for n in names}

        @block.sync
        def _(sp):
            sp.dma_start(cs[:], const).then_inc(load_s, 16)
            sp.dma_start(sm[:], small).then_inc(load_s, 16)
            sp.wait_ge(wr_zero, 1)
            for b in range(4):
                sp.dma_start(pbd[4 * b:4 * b + 4, 32 * b:32 * b + 32], pT).then_inc(load_p, 16)

            def layer_w12(l):
                for kyp in range(2):
                    for ri in range(2):
                        r = 64 * kyp + 32 * ri
                        sp.dma_start(w1c[r:r + 32, 0, r:r + 32], w12[bass.ds(l, 1), 0, :, :].rearrange("a i o -> (a i) o")).then_inc(load_w12, 16)
                        q = 64 * kyp + 32 * (1 - ri)
                        sp.dma_start(w1c[r:r + 32, 1, q:q + 32], w12[bass.ds(l, 1), 0, :, :].rearrange("a i o -> (a i) o")).then_inc(load_w12, 16)
                        sp.dma_start(w2c[r:r + 32, r:r + 32], w12[bass.ds(l, 1), 1, :, :].rearrange("a i o -> (a i) o")).then_inc(load_w12, 16)

            sp.dma_start(fws[:].rearrange("p a b c -> p (a b c)"), fw[0]).then_inc(load_fw, 16)
            layer_w12(0)
            sp.dma_start(Xst[:], xd[0]).then_inc(load_x, 16)
            with sp.Fori(1, NG) as g:
                sp.wait_ge(e_pe, g * 7)
                sp.dma_start(Xst[:], xd[bass.ds(g, 1)].rearrange("a p b y -> (a p) b y")).then_inc(load_x, 16)
            with sp.Fori(0, L - 1) as l:
                sp.wait_ge(mix_pe, (l + 1) * 18)
                sp.dma_start(fws[:].rearrange("p a b c -> p (a b c)"), fw[bass.ds(l + 1, 1)].rearrange("a p n -> (a p) n")).then_inc(load_fw, 16)
                sp.wait_ge(pe_w2, (l + 1) * BP)
                layer_w12(l + 1)
            sp.wait_ge(pe_g, L * BP)
            sp.wait_ge(T["w_rdy"], 1)
            sp.dma_start(ew1, ew[:, 0:384]).then_inc(T["t_load"], 16)
            for e in range(E):
                r, q = slice(64 * (e % 2), 64 * (e % 2) + 64), 128 * (e // 2) + 64 * (e % 2)
                sp.dma_start(ew2[r, q:q + 64], ew[r, 384 + 64 * (e // 2):448 + 64 * (e // 2)]).then_inc(T["t_load"], 16)
                sp.dma_start(ew3[r, q:q + 64], ew[r, 576 + 64 * (e // 2):640 + 64 * (e // 2)]).then_inc(T["t_load"], 16)
            sp.wait_ge(T["y_sb"], 1)
            od = out.rearrange("(h p i) x d -> p i x h d", p=2, i=2)
            for p in range(2):
                for i in range(2):
                    sp.dma_start(od[p, i], N1[64 * p:64 * p + 64, :].rearrange("p (h i d) -> p i h d", i=2, d=D)[:, i]).then_inc(stored, 16)
            sp.wait_ge(stored, 64)

        @block.tensor
        def _(pe):
            mm = pe.matmul

            def own_wait():
                pe.sem_inc(waited, 1)

            pe.wait_ge(load_s, 32)
            for l in range(L):
                a = mm(ps[0:32, 0, 4 * l:4 * l + 4], W("w2n")[0:32, 32 * l:32 * l + 32], W("q1T")[0:32, :], start=True, stop=True)
            a.then_inc(setup_pe, 1)
            pe.wait_ge(setup_dve, 1)
            for o2 in range(2):
                mm(ps[:, 1, 16 * o2:16 * o2 + 16], K("rep")[0:32, 128 * o2:128 * o2 + 128], q1w2, start=True, stop=True)
            mm(ps[:, 2, 0:8], XT[0:32, 0:128], W("comps")[0:32, :], start=True, stop=True)
            mm(ps[:, 3, 0:4], XT[0:32, 128:256], W("q1T")[0:32, :], start=True, stop=True).then_inc(setup_pe, 1)

            pe.wait_ge(load_p, 64)
            with pe.Fori(0, NG) as g:
                pe.wait_ge(load_x, g * 16 + 16)
                pe.wait_ge(e_dve, g * 8 + 1)
                own_wait()
                for p in range(GROUP):
                    a = pe.transpose(ps[0:64, 0, 128 * p:128 * p + 128], Xst[:, p, :], K("ident"))
                a.then_inc(e_pe, 1)
                for half in range(2):
                    for i in range(2):
                        a = mm(ps[:, 1 + i, 256 * half:256 * half + 256],
                               selx[64 * i:64 * i + 64, 128 * half:128 * half + 128],
                               Xst[64 * i:64 * i + 64, :, :], start=True, stop=True)
                a.then_inc(e_pe, 1)
                pe.wait_ge(e_act, g * 3 + 1)
                own_wait()
                for h in range(2):
                    a = mm(ps[64 * h:64 * h + 64, 3, :], K("col_fwd"), rin[:, h], start=True, stop=True)
                a.then_inc(e_pe, 1)
                pe.wait_ge(e_dve, g * 8 + 4)
                for p in range(GROUP):
                    a = pe.transpose(ps[:, 4, 128 * p:128 * p + 128], USe[:, p, :], K("ident"))
                a.then_inc(e_pe, 1)
                pe.wait_ge(e_dve, g * 8 + 6)
                for j in range(2):
                    a = mm(ps[0:112, 5, 0:192], K("row_fwd")[:, 112 * j:112 * j + 112], Ue[:, 192 * j:192 * j + 192],
                           start=(j == 0), stop=(j == 1))
                a.then_inc(e_pe, 1)
                pe.wait_ge(e_act, g * 3 + 3)
                own_wait()
                for p in range(GROUP):
                    for k in range(K6):
                        src = XS[0:48].rearrange("p a b c -> p (a b c)")[:, 96 * p:96 * p + 96].rearrange("p (k b) -> p k b", k=K6)
                        a = pe.transpose(ps[0:16, (6, 7, 0, 4)[p], 48 * k:48 * k + 48], src[:, k], K("ident")[0:48, 0:48])
                a.then_inc(e_pe, 1)
                pe.wait_ge(e_dve, g * 8 + 8)
                for p in range(GROUP):
                    a = mm(ps[:, (6, 7, 0, 4)[p], 0:PM], pbd[0:16, :], RT[0:16].rearrange("p a b c d e -> p (a b c d e)")[:, PM * p:PM * p + PM], start=True, stop=True)
                a.then_inc(e_pe, 1)

            def front(n, t):
                src = Z[:, :, :, bass.ds(t, 1), :]
                for ri in range(2):
                    a = mm(ps[:, 4 + ri, 0:PM], w1c[:, ri, :], src.rearrange("p k x a b -> p k (a b) x"), start=True, stop=True)
                a.then_inc(pe_w1, 1)

            def front_t(n):
                pe.wait_ge(z1_re, n + 1)
                pe.wait_ge(z1_im, n + 1)
                for k in range(K6):
                    a = pe.transpose(ps[0:96, 4 + k // 3, 128 * (k % 3):128 * (k % 3) + 128],
                                     Z1[:, k].rearrange("p a b c -> p (a b c)"), K("ident"))
                a.then_inc(pe_t, 1)

            def front_a(n):
                pe.wait_ge(zt_0, n + 1)
                pe.wait_ge(zt_1, n + 1)
                for og in range(OG):
                    a = mm(ps[0:96, 4 + og // 4, 128 * (og % 4):128 * (og % 4) + 128],
                           Zt[0:96, og].rearrange("p a b -> p (a b)"), K("row_inv")[0:96, :], start=True, stop=True)
                    if og % 4 == 3:
                        a.then_inc(pe_a, 1)

            def back1(n):
                pe.wait_ge(v_ready, 2 * n + 2)
                for q in range(2):
                    for h in range(2):
                        if q == 1 and h == 1:
                            pe.wait_ge(g_add, n + 1)
                        mm(ps[:, 2 * q + h, :], K("col_inv")[0:96, 128 * h:128 * h + 128],
                           V[0:96, 4 * q:4 * q + 4, :].rearrange("p a b -> p (a b)"), start=True, stop=True).then_inc(pe_b, 1)

            def back2(n):
                pe.wait_ge(h_add, n + 1)
                for q in range(2):
                    pe.wait_ge(r_even, 2 * n + q + 1)
                    pe.wait_ge(r_odd, 2 * n + q + 1)
                    own_wait()
                    for h in range(2):
                        a = mm(ps[64 * h:64 * h + 64, 6 + q, :], K("col_fwd"),
                               r_part(h, q), start=True, stop=True)
                    a.then_inc(pe_c, 1)
                for quarter in range(4):
                    for half in range(2):
                        for i in range(2):
                            s = 128 * (2 * half + i)
                            a = pe.transpose(ps[:, quarter, s:s + 128], R[:, i, 4 * half + quarter].rearrange("p a b c -> p (a b c)"), K("ident"))
                    a.then_inc(pe_tr, 1)

            def back3(n):
                for q in range(2):
                    pe.wait_ge((us_0, us_1)[q], n + 1)
                    for og in range(4):
                        a = pe.transpose(ps[:, 6 + q, 128 * og:128 * og + 128], US[:, 4 * q + og, :], K("ident"))
                    a.then_inc(pe_tu, 1)

            def grow(n, o2):
                if o2 == 0:
                    pe.wait_ge(rt_even, 2 * n + 2)
                    pe.wait_ge(rt_odd, 2 * n + 2)
                for quarter in range(4):
                    a = mm(ps[32 * quarter:32 * quarter + 32, 3, 0:256], qs[:, o2].rearrange("p a b -> p (a b)"),
                           RT[:, quarter, :, :, o2, :].rearrange("p a b y -> p (a b) y"), start=(o2 == 0), stop=(o2 == 1))
                if o2 == 1:
                    a.then_inc(pe_g, 1)

            def back4(n):
                pe.wait_ge(u_ready, n + 1)
                for j in range(2):
                    a = mm(ps[0:112, 6, 0:384], K("row_fwd")[:, 112 * j:112 * j + 112],
                           U[:, NKY * j:NKY * j + NKY, :].rearrange("p a b -> p (a b)"), start=(j == 0), stop=(j == 1))
                a.then_inc(pe_d, 1)
                grow(n, 0)
                pe.wait_ge(x_re, n + 1)
                pe.wait_ge(x_im, n + 1)
                own_wait()
                xs = XS[0:48].rearrange("p (k a) b c -> p k (a b c)", a=2)
                for k in range(K6):
                    a = pe.transpose(ps[:, 7, 48 * k:48 * k + 48], xs[:, k], K("ident")[0:48, 0:48])
                a.then_inc(pe_t2, 1)
                grow(n, 1)
                pe.wait_ge(xt_ready, n + 1)
                mm(ps[:, 6, 0:PM], w2c[:, :], XT[:, :], start=True, stop=True).then_inc(pe_w2, 1)

            with pe.Fori(0, L) as l:
                pe.wait_ge(h_whole, l + 1)
                pe.wait_ge(load_fw, l * 16 + 16)
                pe.wait_ge(w_neg, l * 2 + 2)
                pe.wait_ge(q_cur, l + 1)
                pe.wait_ge(load_w12, l * 192 + 192)
                pe.wait_ge(w1_neg, l * 2 + 2)
                for m in range(18):
                    if m >= 4:
                        pe.wait_ge((z_act, z_dve)[m % 2], l * 9 + (m - 4) // 2 + 1)
                    own_wait()
                    for s in range(8):
                        k, kxi = divmod(8 * m + s, NKX)
                        for kyp in range(2):
                            r = slice(64 * kyp, 64 * kyp + 64)
                            a = mm(ps[r, m % 4, 64 * s:64 * s + 64], fws[r, 8 * m + s].rearrange("p a b -> p (a b)"),
                                   H[r, :, k, :, kxi], start=True, stop=True)
                    a.then_inc(mix_pe, 1)
                pe.wait_ge(z_act, l * 9 + 9)
                pe.wait_ge(z_dve, l * 9 + 9)
                front(l * BP, 0)
                front_t(l * BP)
                front_a(l * BP)
                with pe.Fori(0, BP - 1) as t:
                    n = l * BP + t
                    back1(n)
                    front(n + 1, t + 1)
                    back2(n)
                    front_t(n + 1)
                    back3(n)
                    front_a(n + 1)
                    back4(n)
                n = l * BP + (BP - 1)
                back1(n)
                back2(n)
                back3(n)
                back4(n)

            pe.wait_ge(h_whole, L + 1)
            for w, name in enumerate(("Wq", "Wqs", "Wk", "Wks", "Wv")):
                for i in range(2):
                    a = mm(ps[64 * i:64 * i + 64, 0, 64 * w:64 * w + 64], W("WqcT" if w < 2 else "WkvcT")[0:64, :], W(name)[0:64, :], start=True, stop=True)
            a.then_inc(T["w_ps"], 1)
            pe.wait_ge(T["fo_rdy"], 1)
            pe.wait_ge(T["relu_a"], 1)
            pe.wait_ge(T["relu_d"], 1)
            g5 = G[:].rearrange("p (h r) a i y -> p h r a (i y)", r=2)
            for j in range(4):
                for bpp in range(2):
                    for half in range(2):
                        r = 64 * bpp + 32 * half
                        a = mm(ps[r:r + 32, 4 + j, :], fo[:, :], g5[:, 4 * j:4 * j + 4, bpp, half], start=True, stop=True)
                a.then_inc(T["h_ps"], 1)

            def turn(bank0, src, ready, done, free=None):
                for j in range(4):
                    if free is not None:
                        pe.wait_ge(*free)
                    pe.wait_ge(ready, j + 1)
                    for k in range(4):
                        c = 512 * j + 128 * k
                        a = pe.transpose(ps[:, bank0 + j, 128 * k:128 * k + 128], src[:, c:c + 128], K("ident"))
                    a.then_inc(done, 1)

            pe.wait_ge(T["w_rdy"], 1)
            turn(0, TOK, T["h_sb"], T["xt_ps"])
            pe.wait_ge(T["xt_sb"], 4)
            for j in range(4):
                if j >= 2:
                    pe.wait_ge(T["qk_mul"], 4 * j - 4)
                for w in range(4):
                    mm(ps[:, 4 * (j % 2) + w, :], wb[:, w, :], XTT[:, 512 * j:512 * j + 512], start=True, stop=True).then_inc(T["qk_ps"], 1)
            for j in range(4):
                pe.wait_ge(T["qk_mul"], 9 + j)
                for k in range(4):
                    c = 512 * j + 128 * k
                    a = mm(ps[:, j, 128 * k:128 * k + 128], XTT[:, c:c + 128], wb[:, 4, :], start=True, stop=True)
                a.then_inc(T["v_ps"], 1)
            pe.wait_ge(T["qk_sb"], 8)
            pe.wait_ge(T["qk_mul"], 16)
            for j in range(4):
                for k in range(8):
                    c = 512 * j + 64 * k
                    for i in range(2):
                        r = slice(64 * i, 64 * i + 64)
                        a = mm(ps[r, 4 + j, 64 * k:64 * k + 64], QT[r, c:c + 64], KT[r, c:c + 64], start=True, stop=True)
                a.then_inc(T["s_ps"], 1)
            pe.wait_ge(T["v_sb"], 4)
            turn(0, PR, T["p_sb"], T["pt_ps"])
            for j in range(4):
                pe.wait_ge(T["pt_sb"], j + 1)
                for k in range(4):
                    for i in range(2):
                        c = 512 * j + 128 * k + 64 * i
                        for p in range(2):
                            r = slice(64 * p, 64 * p + 64)
                            a = mm(ps[r, 4 + j, 128 * k + 64 * i:128 * k + 64 * i + 64], PT[r, c:c + 64], VT[r, c:c + 64], start=True, stop=True)
                a.then_inc(T["o_ps"], 1)
            pe.wait_ge(T["n1_sb"], 1)
            for j in range(4):
                for k in range(4):
                    c = 512 * j + 128 * k
                    a = pe.transpose(ps[:, j, 128 * k:128 * k + 128], N1[:, c:c + 128], K("ident"))
                a.then_inc(T["nt_ps"], 1)
            for j in range(4):
                pe.wait_ge(T["nt_sb"], j + 1)
                mm(ps[0:64, 4 + j, :], wr1[:, :], N1T[:, 512 * j:512 * j + 512], start=True, stop=True).then_inc(T["rh_ps"], 1)
            pe.wait_ge(T["rh_sb"], 4)
            for g in range(16):
                a = mm(ps[:, 0, 12 * g:12 * g + 12], RHS[0:64, 128 * g:128 * g + 128], wr2[0:64].rearrange("p a b -> p (a b)"), start=True, stop=True)
            a.then_inc(T["lg_ps"], 1)
            pe.wait_ge(T["t_load"], 16 * 13)
            pe.wait_ge(T["gate"], 1)
            for n in range(8):
                i, j = n // 4, n % 4
                r = slice(64 * i, 64 * i + 64)
                for p in range(3):
                    m = 3 * n + p
                    if m >= 2:
                        pe.wait_ge(T["l1_sb"], m - 1)
                    mm(ps[:, m % 2, :], ew1[r, 128 * p:128 * p + 128], N1T[r, 512 * j:512 * j + 512], start=True, stop=True).then_inc(T["l1_ps"], 1)
                for p in range(3):
                    m = 3 * n + p
                    pe.wait_ge(T["l1_sb"], m + 1)
                    if m >= 2:
                        pe.wait_ge(T["l2_sb"], m - 1)
                    mm(ps[:, 2 + m % 2, :], ew2[:, 128 * p:128 * p + 128], H1[p], start=True, stop=True).then_inc(T["l2_ps"], 1)
                for p in range(3):
                    pe.wait_ge(T["l2_sb"], 3 * n + p + 1)
                    if n:
                        pe.wait_ge(T["l3_rd"], 3 * n - 2 + p)
                    mm(ps[:, 4 + p, :], K("one")[0:1, :], W("eb3")[0:1, 128 * p:128 * p + 128].unsqueeze(1).to_broadcast([1, 4, 128]),
                       start=True, stop=False, skip_group_check=True)
                    for k in range(4):
                        a = mm(ps[:, 4 + p, 128 * k:128 * k + 128], H2[p][:, 128 * k:128 * k + 128], ew3[:, 128 * p:128 * p + 128],
                               start=False, stop=True, skip_group_check=True)
                    a.then_inc(T["l3_ps"], 1)

        @block.scalar
        def _(act):
            cp = act.copy
            rin0 = rin[0:64, 0]
            act.wait_ge(setup_dve, 2)
            with act.Fori(0, NG) as g:
                act.wait_ge(e_pe, g * 7 + 1)
                cp(rin0, ps[0:64, 0, :]).then_inc(e_act, 1)
                act.wait_ge(e_pe, g * 7 + 5)
                xe = XS[0:48].rearrange("p a b c -> p (a b c)")[:, 0:384].rearrange("p (q y r c) -> p (q y) r c", q=GROUP, r=2, c=4)
                for ri in range(2):
                    cp(xe[:, :, ri, :], ps[64 * ri:64 * ri + 48, 5, 0:192].rearrange("p (a c) -> p a c", c=4)).then_inc(e_act, 1)

            def back_a(n):
                for q in range(2):
                    act.wait_ge(pe_b, 4 * n + 2 * q + 1)
                    act.activation(r_part(0, q), ps[:, 2 * q, :].rearrange("p (g a x) -> p g a x", g=4, x=8), ACT.Relu).then_inc(r_even, 1)

            def back_b(n):
                act.wait_ge(pe_c, 2 * n + 1)
                cp(US[:, 0:4, :].rearrange("p a b -> p (a b)"), ps[:, 6, :]).then_inc(us_0, 1)
                for q in range(2):
                    act.wait_ge(pe_tr, 4 * n + 2 * q + 1)
                    cp(RT[:, 2 * q].rearrange("p a b c d -> p (a b c d)"), ps[:, 2 * q, :]).then_inc(rt_even, 1)

            def front_z(n):
                act.wait_ge(pe_t, n + 1)
                zt_copy(act.copy, 0).then_inc(zt_0, 1)

            def front_v(n):
                for q in range(2):
                    act.wait_ge(pe_a, 2 * n + q + 1)
                    cp(V[0:96, 4 * q:4 * q + 4, :].rearrange("p a b -> p (a b)"), ps[0:96, 4 + q, :]).then_inc(v_ready, 1)

            def back_c(n):
                act.wait_ge(pe_d, n + 1)
                xs_copy(act.copy, 1).then_inc(x_im, 1)
                act.wait_ge(pe_t2, n + 1)
                cp(XT[:, :], ps[:, 7, 0:PM]).then_inc(xt_ready, 1)

            with act.Fori(0, L) as l:
                for m in range(0, 18, 2):
                    act.wait_ge(mix_pe, l * 18 + m + 1)
                    cp(Z[:].rearrange("p a b c d -> p (a b c d)")[:, 512 * m:512 * m + 512], ps[:, m % 4, :]).then_inc(z_act, 1)
                front_z(l * BP)
                front_v(l * BP)
                with act.Fori(0, BP - 1) as t:
                    n = l * BP + t
                    back_a(n)
                    back_b(n)
                    front_z(n + 1)
                    front_v(n + 1)
                    back_c(n)
                n = l * BP + (BP - 1)
                back_a(n)
                back_b(n)
                back_c(n)

            act.wait_ge(h_whole, L + 1)
            gf = G[:].rearrange("p a b c d -> p (a b c d)")
            act.activation(gf[:, 0:4096], gf[:, 0:4096], ACT.Relu).then_inc(T["relu_a"], 1)
            for j in range(4):
                act.wait_ge(T["h_ps"], j + 1)
                act.activation(TOK[:, 512 * j:512 * j + 512], ps[:, 4 + j, :], ACT.Identity, bias=W("q2b")).then_inc(T["h_sb"], 1)
            for j in range(4):
                act.wait_ge(T["xt_ps"], j + 1)
                cp(XTT[:, 512 * j:512 * j + 512], ps[:, j, :]).then_inc(T["xt_sb"], 1)
            for j in range(4):
                act.wait_ge(T["v_ps"], j + 1)
                cp(VT[:, 512 * j:512 * j + 512], ps[:, j, :]).then_inc(T["v_sb"], 1)
            for j in range(4):
                act.wait_ge(T["s_sh"], j + 1)
                c = slice(512 * j, 512 * j + 512)
                act.activation(PR[:, c], T0[:, c], ACT.Exp).then_inc(T["p_exp"], 1)
            for j in range(4):
                act.wait_ge(T["pt_ps"], j + 1)
                cp(PT[:, 512 * j:512 * j + 512], ps[:, j, :]).then_inc(T["pt_sb"], 1)

            def ln_act(k):
                act.wait_ge(T["ln_c"], k + 1)
                act.activation(T1, T0, ACT.Square).then_inc(T["ln_sq"], 1)
                act.wait_ge(T["ln_v"], k + 1)
                act.activation(st[:, 2, :], st[:, 1, :], ACT.Sqrt).then_inc(T["ln_std"], 1)

            ln_act(0)
            for j in range(4):
                act.wait_ge(T["nt_ps"], j + 1)
                cp(N1T[:, 512 * j:512 * j + 512], ps[:, j, :]).then_inc(T["nt_sb"], 1)
            for j in range(4):
                act.wait_ge(T["rh_ps"], j + 1)
                act.activation(RHS[0:64, 512 * j:512 * j + 512], ps[0:64, 4 + j, :], ACT.Relu, bias=W("rb1")[0:64, :]).then_inc(T["rh_sb"], 1)
            act.wait_ge(T["lg_sh"], 1)
            act.activation(gt[:, 1], gt[:, 0], ACT.Exp).then_inc(T["lg_exp"], 1)
            act.wait_ge(T["g_dif"], 1)
            act.activation(gm[:, 3], gm[:, 2], ACT.Exp).then_inc(T["g_exp"], 1)
            for n in range(8):
                for p in range(3):
                    act.wait_ge(T["l1_ps"], 3 * n + p + 1)
                    act.activation(H1[p], ps[:, (3 * n + p) % 2, :], ACT.Relu, bias=W("eb1")[:, p:p + 1]).then_inc(T["l1_sb"], 1)
                for p in range(3):
                    act.wait_ge(T["l2_ps"], 3 * n + p + 1)
                    act.activation(H2[p], ps[:, 2 + (3 * n + p) % 2, :], ACT.Relu, bias=W("eb2")[:, p:p + 1]).then_inc(T["l2_sb"], 1)
            ln_act(1)

        @block.vector
        def _(ve):
            chain = [0]
            step = sem("ve_step")

            def then(ins):
                chain[0] += 1
                ins.then_inc(step, 1)
                ve.wait_ge(step, chain[0])

            tt, ts, cp = ve.tensor_tensor, ve.tensor_scalar, ve.tensor_copy
            ve.wait_ge(load_s, 32)
            cp(XT[0:32, 0:128].rearrange("p (a q) -> p a q", q=4), W("q1T")[0:32, :].unsqueeze(1).to_broadcast([32, 32, 4]))
            cp(XT[0:32, 128:256], W("comps")[0:32, 0:1].to_broadcast([32, 128]))
            ve.wait_ge(setup_pe, 1)
            cp(q1w2, ps[0:32, 0, 0:16]).then_inc(setup_dve, 1)
            rflat = rin.rearrange("p h (a x) -> p h a x", x=S)
            cp(rflat[64:128, 0], K("gx_cols")[64:128, :].unsqueeze(1).to_broadcast([64, 8, 64]))
            cp(rflat[0:64, 1], K("gy_part")[0:64, :].unsqueeze(1).to_broadcast([64, 8, 64]))
            ve.memset(rflat[64:128, 1], 1.0)
            ve.memset(dc[:], 0.0)
            ve.wait_ge(setup_pe, 2)
            for o2 in range(2):
                for l in range(L):
                    tt(qs_all[:, l, o2], ps[:, 1, 16 * o2 + 4 * l:16 * o2 + 4 * l + 4].unsqueeze(1).to_broadcast([128, 8, 4]),
                       K("same8").unsqueeze(2).to_broadcast([128, 8, 4]), ALU.mult)
            cp(comp[:, 0:8], ps[:, 2, 0:8])
            then(cp(pab[:, :], ps[:, 3, 0:4]))
            ve.reduce_sum(comp[:, 8:9], comp[:, 3:8], AX.X)
            then(tt(selx.rearrange("p (a q) -> p a q", q=4), K("pick_row").unsqueeze(2).to_broadcast([128, 64, 4]),
                    pab[:, :].unsqueeze(1).to_broadcast([128, 64, 4]), ALU.mult))
            then(tt(comp[:, 9:10], comp[:, 8:9], W("q1b"), ALU.add))
            for half in range(2):
                then(ts(comp[:, 10 + half:11 + half], K("gx_part")[:, half:half + 1], comp[:, 1:2], comp[:, 9:10], ALU.mult, ALU.add))
                then(ts(S0[:, half, :], K("gy_row"), comp[:, 2:3], comp[:, 10 + half:11 + half], ALU.mult, ALU.add))
            ve.memset(zero_bias[:], 0.0).then_inc(setup_dve, 1)
            ve.memset(comp[:, 11:12], 0.0).then_inc(e_dve, 1)

            with ve.Fori(0, NG) as g:
                ve.wait_ge(e_pe, g * 7 + 2)
                for half in range(2):
                    gd = G[:, bass.ds(g * GROUP, GROUP), half].rearrange("p a i y -> p i a y")
                    tt(gd, ps[:, 1:3, 256 * half:256 * half + 256].rearrange("p i (a y) -> p i a y", a=GROUP),
                       S0[:, half].unsqueeze(1).unsqueeze(1).to_broadcast([128, 2, GROUP, S]), ALU.add).then_inc(e_dve, 1)
                ve.wait_ge(e_pe, g * 7 + 3)
                cp(USe.rearrange("p a b -> p (a b)"), ps[:, 3, :]).then_inc(e_dve, 1)
                ve.wait_ge(e_pe, g * 7 + 4)
                uv = Ue.rearrange("p (r a k c) -> p r a k c", r=2, a=GROUP, c=4)
                pv = ps[:, 4, :].rearrange("p (a h m) -> p a h m", a=GROUP, h=2)
                for r in range(2):
                    src = pv[:, :, :, 0:48].rearrange("p a h (o r k) -> p a h o r k", o=2, r=2)
                    for h in range(2):
                        ins = cp(uv[:, r, :, :, 2 * h:2 * h + 2].rearrange("p a k c -> p a c k"), src[:, :, h, :, r, :])
                    ins.then_inc(e_dve, 1)
                ve.wait_ge(e_pe, g * 7 + 6)
                rte = RT[0:16].rearrange("p a b c d e -> p (a b c d e)")
                for p in range(GROUP):
                    ins = cp(rte[:, PM * p:PM * p + PM], ps[0:16, (6, 7, 0, 4)[p], 0:PM])
                    if p % 2:
                        ins.then_inc(e_dve, 1)
                ve.wait_ge(e_pe, g * 7 + 7)
                for p in range(GROUP):
                    ins = cp(H[:, bass.ds(g * GROUP + p, 1)].rearrange("p a k i x -> p (a k i x)"), ps[:, (6, 7, 0, 4)[p], 0:PM])
                ins.then_inc(e_dve, 1)

            ve.wait_ge(e_dve, 8 * NG + 1)
            ve.sem_inc(g_add, 1)
            ve.sem_inc(h_add, 1)
            ve.sem_inc(h_whole, 1)

            def z1(n):
                for ri in range(2):
                    tgt = Z1[:, :, ri].rearrange("p k i x -> p k (i x)")
                    if ri == 0:
                        ve.wait_ge(pe_w1, n + 1)
                    tt(tgt, ps[:, 4 + ri, 0:PM].rearrange("p (k m) -> p k m", k=K6), dc[:, ri].rearrange("p k i x -> p k (i x)"),
                       ALU.add).then_inc((z1_re, z1_im)[ri], 1)

            def back_a(n):
                for q in range(2):
                    ve.wait_ge(pe_b, 4 * n + 2 * q + 2)
                    ts(r_part(1, q), ps[:, 2 * q + 1, :].rearrange("p (g a x) -> p g a x", g=4, x=8), 0.0, None, ALU.max).then_inc(r_odd, 1)

            def back_b(n):
                ve.wait_ge(pe_c, 2 * n + 2)
                cp(US[:, 4:8, :].rearrange("p a b -> p (a b)"), ps[:, 7, :]).then_inc(us_1, 1)
                for q in range(2):
                    ve.wait_ge(pe_tr, 4 * n + 2 * q + 2)
                    cp(RT[:, 2 * q + 1].rearrange("p a b c d -> p (a b c d)"), ps[:, 2 * q + 1, :]).then_inc(rt_odd, 1)

            def front_z(n):
                ve.wait_ge(pe_t, n + 1)
                zt_copy(cp, 1).then_inc(zt_1, 1)

            def back_u(n):
                for q in range(2):
                    ve.wait_ge(pe_tu, 2 * n + q + 1)
                    src = ps[:, 6 + q, :].rearrange("p (g h m) -> p g h m", g=4, h=2)
                    dst = U[:].rearrange("p m (g h o) -> p g h o m", g=OG, h=2)
                    for h in range(2):
                        ins = cp(dst[:, 4 * q:4 * q + 4, h], src[:, :, h, 0:48].rearrange("p g (o m) -> p g o m", o=2))
                ins.then_inc(u_ready, 1)

            def back_c(n, t):
                ve.wait_ge(pe_d, n + 1)
                xs_copy(cp, 0).then_inc(x_re, 1)
                ve.wait_ge(pe_g, n + 1)
                gd = G[:, bass.ds(t, 1)].rearrange("p a i j y -> p (a i j y)")
                tt(gd, gd, ps[:, 3, 0:256], ALU.add).then_inc(g_add, 1)
                ve.wait_ge(pe_w2, n + 1)
                hd = H[:, bass.ds(t, 1)].rearrange("p a k i x -> p (a k i x)")
                tt(hd, hd, ps[:, 6, 0:PM], ALU.add).then_inc(h_add, 1)

            with ve.Fori(0, L) as l:
                ve.wait_ge(h_whole, l + 1)
                b1v = W("b1")[:, bass.ds(l * 2, 2)]
                ts(dc[:, :, 0, :, 0], b1v.unsqueeze(2).to_broadcast([128, 2, 2]), float(S), None, ALU.mult).then_inc(dc_ready, 1)
                for m in range(1, 18, 2):
                    ve.wait_ge(mix_pe, l * 18 + m + 1)
                    cp(Z[:].rearrange("p a b c d -> p (a b c d)")[:, 512 * m:512 * m + 512], ps[:, m % 4, :]).then_inc(z_dve, 1)
                ve.wait_ge(dc_ready, l + 1)
                z1(l * BP)
                front_z(l * BP)
                with ve.Fori(0, BP - 1) as t:
                    n = l * BP + t
                    back_a(n)
                    z1(n + 1)
                    back_b(n)
                    front_z(n + 1)
                    back_u(n)
                    back_c(n, t)
                n = l * BP + (BP - 1)
                back_a(n)
                back_b(n)
                back_u(n)
                back_c(n, BP - 1)
                ve.wait_ge(h_add, l * BP + BP + 1)
                hdc = H[0:32, :, 0, :, 0]
                ve.scalar_tensor_tensor(out=hdc, in0=W("w2b")[0:32, bass.ds(l, 1)].unsqueeze(2).to_broadcast([32, BP, 2]), scalar=float(S), in1=hdc,
                                        op0=ALU.mult, op1=ALU.add).then_inc(h_whole, 1)

            ve.wait_ge(h_whole, L + 1)
            gf = G[:].rearrange("p a b c d -> p (a b c d)")
            ts(fo[:, :], K("pick_out"), W("q2"), None, ALU.mult).then_inc(T["fo_rdy"], 1)
            ts(gf[:, 4096:8192], gf[:, 4096:8192], 0.0, None, ALU.max).then_inc(T["relu_d"], 1)
            ve.wait_ge(pe_g, L * BP)
            ve.memset(wb[:], 0.0)
            ve.memset(wr1[:], 0.0)
            ve.memset(R[:], 0.0)
            then(ve.memset(wr2[:], 0.0))
            for i in range(2):
                r = slice(64 * i, 64 * i + 64)
                cp(wr1[r, 32 * i:32 * i + 32], W("rw1")[r, :])
                cp(wr2[32 * i:32 * i + 32, i, :], W("rw2")[32 * i:32 * i + 32, :])
            ve.wait_ge(T["w_ps"], 1)
            for i in range(2):
                r = slice(64 * i, 64 * i + 64)
                a = cp(wb[r, :, 64 * i:64 * i + 64], ps[r, 0, 0:320].rearrange("p (a b) -> p a b", a=5))
            a.then_inc(T["w_rdy"], 1)
            b8 = [128, 8, 64]
            for j in range(4):
                c = slice(512 * j, 512 * j + 512)
                for w in range(4):
                    dst = (QT, T0, KT, T1)[w][:, c].rearrange("p (a b) -> p a b", b=64)
                    ve.wait_ge(T["qk_ps"], 4 * j + w + 1)
                    tt(dst, ps[:, 4 * (j % 2) + w, :].rearrange("p (a b) -> p a b", b=64),
                       K(("cos_q", "sin_q", "cos_k", "sin_k")[w]).unsqueeze(1).to_broadcast(b8), ALU.mult).then_inc(T["qk_mul"], 1)
            ve.wait_ge(T["qk_sb"], 8)
            for j in range(4):
                c = slice(512 * j, 512 * j + 512)
                t0 = T0[:, c].rearrange("p (a b) -> p a b", b=64)
                ve.wait_ge(T["s_ps"], j + 1)
                then(tt(t0, ps[:, 4 + j, :].rearrange("p (a b) -> p a b", b=64), K("causal").unsqueeze(1).to_broadcast(b8), ALU.add))
                then(ve.reduce_max(st[:, 0, 8 * j:8 * j + 8], t0, AX.X))
                tt(t0, t0, st[:, 0, 8 * j:8 * j + 8].unsqueeze(2).to_broadcast(b8), ALU.subtract).then_inc(T["s_sh"], 1)
            for j in range(4):
                c = slice(512 * j, 512 * j + 512)
                pj = PR[:, c].rearrange("p (a b) -> p a b", b=64)
                ve.wait_ge(T["p_exp"], j + 1)
                then(ve.reduce_sum(st[:, 1, 8 * j:8 * j + 8], pj, AX.X))
                then(ve.reciprocal(st[:, 2, 8 * j:8 * j + 8], st[:, 1, 8 * j:8 * j + 8]))
                tt(pj, pj, st[:, 2, 8 * j:8 * j + 8].unsqueeze(2).to_broadcast(b8), ALU.mult).then_inc(T["p_sb"], 1)
            for j in range(4):
                c = slice(512 * j, 512 * j + 512)
                ve.wait_ge(T["o_ps"], j + 1)
                a = tt(Y1[:, c], ps[:, 4 + j, :], TOK[:, c], ALU.add)
            then(a)
            b32 = [128, 32, 64]

            def layernorm(k, y, n):
                y3, t3, q3, n3 = [v.rearrange("p (a b) -> p a b", b=64) for v in (y, T0, T1, n)]
                then(ve.reduce_sum(st[:, 0, :], y3, AX.X))
                then(ts(st[:, 0, :], st[:, 0, :], 1.0 / D, None, ALU.mult))
                tt(t3, y3, st[:, 0, :].unsqueeze(2).to_broadcast(b32), ALU.subtract).then_inc(T["ln_c"], 1)
                ve.wait_ge(T["ln_sq"], k + 1)
                then(ve.reduce_sum(st[:, 1, :], q3, AX.X))
                ts(st[:, 1, :], st[:, 1, :], 1.0 / D, 1e-5, ALU.mult, ALU.add).then_inc(T["ln_v"], 1)
                ve.wait_ge(T["ln_std"], k + 1)
                then(ve.reciprocal(st[:, 3, :], st[:, 2, :]))
                return tt(n3, t3, st[:, 3, :].unsqueeze(2).to_broadcast(b32), ALU.mult)

            layernorm(0, Y1, N1).then_inc(T["n1_sb"], 1)
            b6 = [128, 32, E]
            lg, ex, pr, sel1, sel2, tmp = [gt[:, i] for i in range(6)]

            def per_token(v):
                return v.unsqueeze(2).to_broadcast(b6)

            rank = K("rank").unsqueeze(1).to_broadcast(b6)
            ve.wait_ge(T["lg_ps"], 1)
            then(tt(lg, ps[:, 0, 0:192].rearrange("p (a b) -> p a b", b=E), W("rb2").unsqueeze(1).to_broadcast(b6), ALU.add))
            then(ve.reduce_max(gm[:, 0], lg, AX.X))
            tt(lg, lg, per_token(gm[:, 0]), ALU.subtract).then_inc(T["lg_sh"], 1)
            ve.wait_ge(T["lg_exp"], 1)
            then(ve.reduce_sum(gm[:, 0], ex, AX.X))
            then(ve.reciprocal(gm[:, 1], gm[:, 0]))
            then(tt(pr, ex, per_token(gm[:, 1]), ALU.mult))

            def pick(p, best, sel):
                then(ve.reduce_max(best, p, AX.X))
                then(tt(tmp, p, per_token(best), ALU.is_equal))
                then(tt(tmp, tmp, rank, ALU.mult))
                then(ve.reduce_max(gm[:, 5], tmp, AX.X))
                then(tt(sel, tmp, per_token(gm[:, 5]), ALU.is_equal))

            pick(pr, gm[:, 0], sel1)
            then(ve.scalar_tensor_tensor(out=pr, in0=sel1, scalar=-2.0, in1=pr, op0=ALU.mult, op1=ALU.add))
            pick(pr, gm[:, 1], sel2)
            tt(gm[:, 2], gm[:, 1], gm[:, 0], ALU.subtract).then_inc(T["g_dif"], 1)
            ve.wait_ge(T["g_exp"], 1)
            then(ts(gm[:, 4], gm[:, 3], 1.0, None, ALU.add))
            then(ve.reciprocal(gm[:, 4], gm[:, 4]))
            then(tt(gm[:, 5], gm[:, 3], gm[:, 4], ALU.mult))
            then(tt(sel1, sel1, per_token(gm[:, 4]), ALU.mult))
            then(tt(sel2, sel2, per_token(gm[:, 5]), ALU.mult))
            tt(lg, sel1, sel2, ALU.add).then_inc(T["gate"], 1)
            ve.wait_ge(T["gate"], 1)
            gate = lg.rearrange("p (h i) e -> p h i e", i=2)
            n1v = N1.rearrange("p (h i d) -> p h i d", i=2, d=D)
            y1v = Y1.rearrange("p (h i d) -> p h i d", i=2, d=D)
            gp = GP.rearrange("p (e h d) -> p e h d", e=E, h=4)
            for n in range(8):
                i, j = n // 4, n % 4
                for p in range(3):
                    ve.wait_ge(T["l3_ps"], 3 * n + p + 1)
                    pv = ps[:, 4 + p, :].rearrange("p (h e d) -> p e h d", e=2, d=D)
                    for e in range(2):
                        a = tt(gp[:, 2 * p + e], pv[:, e], gate[:, 4 * j:4 * j + 4, i, 2 * p + e].unsqueeze(2).to_broadcast([128, 4, 64]), ALU.mult)
                    a.then_inc(T["l3_rd"], 1)
                ve.wait_ge(T["l3_rd"], 3 * n + 3)
                yv = y1v[:, 4 * j:4 * j + 4, i]
                then(ve.reduce_sum(yv, gp.rearrange("p e h d -> p h d e"), AX.X))
                then(tt(yv, yv, n1v[:, 4 * j:4 * j + 4, i], ALU.add))
            layernorm(1, Y1, N1).then_inc(T["y_sb"], 1)

        @block.gpsimd
        def _(po):
            po.memset(w1c[:], 0.0)
            po.memset(w2c[:], 0.0)
            po.memset(pbd[:], 0.0).then_inc(wr_zero, 1)
            with po.Fori(0, L) as l:
                po.wait_ge(load_fw, l * 16 + 16)
                po.sem_inc(waited, 1)
                for kyp in range(2):
                    r = slice(64 * kyp + 32, 64 * kyp + 64)
                    po.tensor_scalar(fws[r, :, 0, :], fws[r, :, 0, :], -1.0, None, ALU.mult).then_inc(w_neg, 1)
                    po.wait_ge(w_neg, l * 2 + kyp + 1)
                    po.sem_inc(waited, 1)
                po.wait_ge(load_w12, l * 192 + 192)
                po.sem_inc(waited, 1)
                for kyp in range(2):
                    r = slice(64 * kyp + 32, 64 * kyp + 64)
                    po.tensor_scalar(w1c[r, 0, :], w1c[r, 0, :], -1.0, None, ALU.mult).then_inc(w1_neg, 1)
                    po.wait_ge(w1_neg, l * 2 + kyp + 1)
                    po.sem_inc(waited, 1)
                po.wait_ge(setup_dve, 2)
                po.wait_ge(h_whole, l + 1)
                po.sem_inc(waited, 1)
                po.tensor_copy(qs[:].rearrange("p a b c -> p (a b c)"), qs_all[:, bass.ds(l, 1)].rearrange("p a b c d -> p (a b c d)")).then_inc(q_cur, 1)
                po.wait_ge(q_cur, l + 1)
                po.sem_inc(waited, 1)
            for j in range(4):
                c = slice(512 * j, 512 * j + 512)
                po.wait_ge(T["qk_mul"], 4 * j + 2)
                po.tensor_tensor(QT[:, c], QT[:, c], T0[:, c], ALU.add).then_inc(T["qk_sb"], 1)
                po.wait_ge(T["qk_mul"], 4 * j + 4)
                po.tensor_tensor(KT[:, c], KT[:, c], T1[:, c], ALU.add).then_inc(T["qk_sb"], 1)


def kernel(**inputs):
    import concourse.bacc as bacc
    from concourse.bass_utils import run_bass_kernel_spmd as run

    a = {k: np.asarray(v) for k, v in inputs.items()}
    t = {k[7:]: v for k, v in a.items() if k.startswith("L0_tok_")}
    at = {k[8:]: v for k, v in a.items() if k.startswith("L0_attn_")}
    ff = {k[7:]: v for k, v in a.items() if k.startswith("L0_ffn_")}
    w = t["fw"].transpose(0, 5, 2, 1, 4, 6, 3).reshape(L, 2, K6, C, 2 * 12, 2, C)
    w = w.transpose(0, 1, 3, 2, 4, 5, 6)
    fw = np.stack([w, w[:, :, :, :, :, ::-1]], 2).reshape(L, 128, K6 * NKX * 2 * C)
    w12 = np.stack([t["w1_w"].transpose(0, 2, 1), t["w2_w"].transpose(0, 2, 1)], 1)
    pT = np.concatenate([t["p_w"].T, t["p_b"][None]], 0)
    small = np.zeros((128, NSMALL), np.float32)

    def put(name, v, r0=0):
        c, width = SAT[name]
        v = np.asarray(v).reshape(-1, width)
        small[r0:r0 + v.shape[0], c:c + width] = v

    put("q1T", t["q1_w"].T)
    put("w2n", t["w2_w"].transpose(1, 0, 2))
    put("comps", np.concatenate([t["p_w"], t["p_b"][:, None], t["w2_b"].T], 1))
    put("q1b", np.tile(t["q1_b"], 32))
    put("q2", np.tile(t["q2_w"][0], 32))
    put("q2b", np.tile(t["q2_b"], 128))
    for ri in range(2):
        small[32 * ri:32 * ri + 32, SAT["b1"][0] + ri:SAT["b1"][0] + 2 * L:2] = t["w1_b"].T
    put("w2b", t["w2_b"].T)
    put("WqcT", at["Wq_comp"].T)
    put("WkvcT", at["Wkv_comp"].T)
    swap = np.arange(HR) ^ 1
    for n in "qk":
        put("W" + n, np.concatenate([at[f"W{n}c"], at[f"W{n}r"]], 1))
        put("W" + n + "s", np.concatenate([at[f"W{n}c"], at[f"W{n}r"][:, swap]], 1))
    put("Wv", at["Wv"])
    for i in range(2):
        put("rw1", ff["router_w1"], 64 * i)
        put("rw2", ff["router_w2"], 32 * i)
        put("rb1", ff["router_b1"], 32 * i)
    put("rb2", np.tile(ff["router_b2"], (128, 1)))
    put("eb1", ff["expert_b1"].reshape(3, 128).T)
    put("eb2", ff["expert_b2"].reshape(3, 128).T)
    put("eb3", ff["expert_b3"].reshape(1, 384))
    e1 = np.tile(ff["expert_w1"].transpose(1, 0, 2).reshape(D, E * HID), (2, 1))
    e2 = ff["expert_w2"].reshape(3, 128, HID).transpose(1, 0, 2).reshape(128, 192)
    e3 = ff["expert_w3"].reshape(3, 128, D).transpose(1, 0, 2).reshape(128, 192)
    arrays = {"x": a["x"], "fw": fw, "w12": w12, "pT": pT, "small": small,
              "ew": np.concatenate([e1, e2, e3], 1), "const": constants()}
    nc = bacc.Bacc("TRN2", target_bir_lowering=False, num_devices=1)
    maps, args = {}, []
    for name, v in arrays.items():
        v = np.ascontiguousarray(v)
        maps["in_" + name] = v
        args.append(nc.dram_tensor("in_" + name, v.shape, mybir.dt.from_np(v.dtype), kind="ExternalInput").ap())
    o = nc.dram_tensor("out_0", (B, S, S), F32, kind="ExternalOutput").ap()
    program(nc, *args, o)
    r = run(nc, [maps], core_ids=[0])
    return r.results[0]["out_0"]
```

```python
from contextlib import ExitStack

import numpy as np

import concourse.bass as bass
from concourse import mybir

F32 = mybir.dt.float32
F32R = mybir.dt.float32r
ALU = mybir.AluOpType
ACT = mybir.ActivationFunctionType
AX = mybir.AxisListType

B, S, C, L, NQ = 64, 64, 32, 4, 4
NKX, NKY = 24, 12
BP = B // 2
OG = C // 4
K6 = NKY // 2
PM = K6 * 2 * NKX
D, E, HID, RH = 64, 6, 64, 32
HR = 16
NEG = -3.0e38

LAYOUT = [("ident", 128), ("row_inv", 128), ("col_inv", 128), ("col_fwd", 64), ("row_fwd", 224),
          ("one", 128), ("gx_part", 4), ("gy_row", 32), ("same", 16), ("rep", 128), ("pick_out", 128),
          ("gmodes", PM), ("quarter", 4), ("of_pair", BP),
          ("cos_q", 64), ("sin_q", 64), ("cos_k", 64), ("sin_k", 64), ("causal", 64), ("rank", 6)]
AT = {}
for _name, _width in LAYOUT:
    AT[_name] = (sum(w for n, w in LAYOUT[:len(AT)]), _width)
NCONST = sum(w for _, w in LAYOUT)


def constants():
    f = {n: np.zeros((128, w), np.float64) for n, w in LAYOUT}
    kx = np.array(list(range(12)) + list(range(-12, 0)))
    ky = np.arange(NKY)
    pos = np.arange(S)
    tx = 2 * np.pi * np.outer(kx, pos) / S
    ty = 2 * np.pi * np.outer(ky, pos) / S
    f["ident"][:] = np.eye(128)
    for b in range(2):
        f["row_inv"][b * 24:b * 24 + 24, b * 64:b * 64 + 64] = np.cos(tx) / 8
        f["row_inv"][48 + b * 24:72 + b * 24, b * 64:b * 64 + 64] = -np.sin(tx) / 8
    v = np.zeros((K6, 2, 2, 2, 2, S))
    for k in range(NKY):
        w = (1.0 if k == 0 else 2.0) / 8
        for o in range(2):
            v[k % K6, k // K6, 0, o, o] = w * np.cos(ty[k])
            v[k % K6, k // K6, 1, o, o] = w * np.sin(ty[k])
    f["col_inv"][:48] = f["col_inv"][64:112] = v.reshape(48, 128)
    c = np.zeros((2, S, 2, 2, NKY))
    order = [K6 * (m % 2) + m // 2 for m in range(NKY)]
    for o in range(2):
        c[o, :, o, 0] = np.cos(ty[order]).T / 8
        c[o, :, o, 1] = -np.sin(ty[order]).T / 8
    f["col_fwd"][:, :48] = c.reshape(128, 48)
    d = np.zeros((2, 128, 112))
    for b in range(2):
        r = slice(b * 64, b * 64 + 64)
        re, im = slice(b * 24, b * 24 + 24), slice(64 + b * 24, 88 + b * 24)
        d[0, r, re], d[0, r, im] = np.cos(tx).T / 8, -np.sin(tx).T / 8
        d[1, r, re], d[1, r, im] = np.sin(tx).T / 8, np.cos(tx).T / 8
    f["row_fwd"][:] = d.transpose(1, 0, 2).reshape(128, 224)
    grid = np.linspace(0.0, 1.0, S, dtype=np.float32)
    p = np.arange(128)
    f["one"][:] = 1
    xt, xv, yh, x0 = p // 32, p // 16 % 2, p // 8 % 2, p // 4 % 2
    xr = np.arange(4)
    xg = 32 * (xr // 2) + 2 * (xr % 2) + (8 * xt + 4 * xv + x0)[:, None]
    f["gx_part"][:] = grid[xg]
    f["gy_row"][:] = grid[32 * yh[:, None] + np.arange(32)]
    k_yh, k_x0 = p // 32 % 2, p % 2
    e = np.zeros((128, 2, 2, 2, 2))
    for v in range(2):
        e[p, v, v, k_yh, k_x0] = 1
    f["same"][:] = e.reshape(128, 16)
    r = np.zeros((C, 2, 2, 2, OG, 2))
    for ch in range(C):
        r[ch, ch % 2, :, ch // 2 % 2, ch // 4, :] = 1
    f["rep"][:C] = r.reshape(C, 128)
    fields = np.stack([np.tile(grid[:, None], (1, S)), np.tile(grid[None], (S, 1)), np.ones((S, S))])
    m = np.fft.fft2(fields.astype(np.float64))[:, kx][:, :, ky] / S
    g = np.zeros((2, 2, 3, K6, 2, NKX))
    for kyp in range(2):
        for k in range(K6):
            g[kyp, 0, :, k] = m[:, None, :, K6 * kyp + k].real
            g[kyp, 1, :, k] = m[:, None, :, K6 * kyp + k].imag
    f["gmodes"][:12] = g.reshape(12, PM)
    f["quarter"][:] = (p[:, None] // 32) == np.arange(4)
    f["of_pair"][:] = (p[:, None] % 32) == np.arange(32)
    g = np.zeros((128, 2, 2, 32))
    for xl in range(2):
        g[p, yh, xl, 8 * xt + 4 * xv + 2 * xl + x0] = 1
    f["pick_out"][:] = g.reshape(128, 128)
    half = HR // 2
    theta = (1.0 / (np.float32(10000.0) ** (np.arange(half, dtype=np.float32) / np.float32(half)))).astype(np.float32)
    ang = (pos.astype(np.float32)[:, None] * theta[None]).astype(np.float32)
    cos, sin = np.ones((64, S)), np.zeros((64, S))
    for i in range(half):
        for s in range(2):
            cos[48 + 2 * i + s] = np.cos(ang[:, i])
            sin[48 + 2 * i + s] = (-1, 1)[s] * np.sin(ang[:, i])
    for n, m in (("cos", cos), ("sin", sin)):
        f[n + "_k"][:] = np.tile(m, (2, 1))
        f[n + "_q"][:] = np.tile(m, (2, 1)) / np.sqrt(D)
    f["causal"][:] = np.where(np.arange(64)[None] > (p % 64)[:, None], NEG, 0)
    f["rank"][:] = np.arange(E, 0, -1)
    return np.concatenate([f[n] for n, _ in LAYOUT], 1).astype(np.float32)


SMALL = [("px", 32), ("q1T", 4), ("w2n", L * 32), ("comps", 8), ("q1b", 1), ("q2", 1), ("q2b", 1),
         ("b1", L), ("w2b", L), ("WqcT", 64), ("WkvcT", 64), ("Wq", 64), ("Wqs", 64),
         ("Wk", 64), ("Wks", 64), ("Wv", 64), ("rw1", 32), ("rw2", 6), ("rb1", 1), ("rb2", 6),
         ("eb1", 3), ("eb2", 3), ("eb3", 384)]
SAT = {}
for _name, _width in SMALL:
    SAT[_name] = (sum(w for n, w in SMALL[:len(SAT)]), _width)
NSMALL = sum(w for _, w in SMALL)


def program(nc, x, fw, w12, pT, small, ew, const, out):
    with ExitStack() as ctx:
        def sb(name, *shape, dtype=F32):
            return ctx.enter_context(nc.sbuf_tensor(name, [128, *shape], dtype))

        def sem(name):
            return ctx.enter_context(nc.semaphore(name))

        ps = ctx.enter_context(nc.psum_tensor("ps", [128, 8, 512], F32))
        cs = sb("cs", NCONST)
        sm = sb("sm", NSMALL)

        def K(name):
            a, w = AT[name]
            return cs[:, a:a + w]

        def W(name):
            a, w = SAT[name]
            return sm[:, a:a + w]

        H = sb("H", BP, K6, 2, NKX)
        Z = sb("Z", K6, NKX, BP, 2)
        G = sb("G", BP, 2, 4, 32)
        fws = sb("fws", K6 * NKX, 2, C)
        w1c = sb("w1c", 128)
        w2c = sb("w2c", 128)
        pbd = sb("pbd", 128)
        dc = sb("dc", K6, 2, NKX)
        qs_all = sb("qs_all", L, 2, 8, NQ)
        qs = sb("qs", 2, 8, NQ)
        Z1 = sb("Z1", K6, 2, 2, NKX)
        Zt = sb("Zt", OG, 2, 32, 2)
        V = sb("V", 2, OG, 128, dtype=F32R)
        ci = sb("ci", 2, 128, dtype=F32R)
        R = sb("R", 2, 32, 2, OG, 2)
        RT = sb("RT", 2, 2, 4, 2, 64)
        US = sb("US", OG, 128)
        U = sb("U", 2 * NKY, C)
        XS = sb("XS", NKY, 2, C)
        XT = sb("XT", PM)
        q1w2 = U[0:32, 0, 0:L * NQ]
        comp = sb("comp", 12)
        gxp = sb("gxp", 4)
        S0 = sb("S0", 4, 32)
        XN = R[:].rearrange("p a b c d e -> p (a b c d e)")
        XNT = RT[:].rearrange("p a b c d e -> p (a b c d e)")
        HC = Z1[:].rearrange("p a b c d -> p (a b c d)")[:, 0:PM]
        pb = Z1[:].rearrange("p a b c d -> p (a b c d)")[:, PM:PM + 128]
        PSEL = Z[:].rearrange("p a b c d -> p (a b c d)")[:, 0:BP * 128]
        load_s = sem("load_s")
        load_fw = sem("load_fw")
        load_w12 = sem("load_w12")
        load_p = sem("load_p")
        load_x = sem("load_x")
        load_xg = sem("load_xg")
        wr_zero = sem("wr_zero")
        w_neg = sem("w_neg")
        w1_neg = sem("w1_neg")
        setup_pe = sem("setup_pe")
        setup_dve = sem("setup_dve")
        q_cur = sem("q_cur")
        e_pe = sem("e_pe")
        e_act = sem("e_act"); e_dve = sem("e_dve")
        hc_ps = sem("hc_ps"); psel_ready = sem("psel_ready"); h0_ps = sem("h0_ps"); h0_sb = sem("h0_sb")
        g_init = sem("g_init")
        mix_pe = sem("mix_pe")
        z_act = sem("z_act"); z_dve = sem("z_dve")
        dc_ready = sem("dc_ready")
        h_whole = sem("h_whole")
        pe_w1 = sem("pe_w1"); pe_t = sem("pe_t"); pe_a = sem("pe_a"); pe_b = sem("pe_b")
        pe_c = sem("pe_c"); pe_tu = sem("pe_tu"); pe_d = sem("pe_d")
        pe_t2 = sem("pe_t2"); pe_w2 = sem("pe_w2"); pe_g = sem("pe_g")
        z1_re = sem("z1_re"); z1_im = sem("z1_im"); zt_0 = sem("zt_0"); zt_1 = sem("zt_1")
        v_first = sem("v_first"); v_rest = sem("v_rest")
        ci_first = sem("ci_first"); ci_rest = sem("ci_rest")
        r_ready = sem("r_ready"); us_ready = sem("us_ready"); rt_ready = sem("rt_ready"); u_ready = sem("u_ready")
        x_re = sem("x_re"); x_im = sem("x_im"); xt_ready = sem("xt_ready"); h_add = sem("h_add"); g_add = sem("g_add")
        stored = sem("stored")
        waited = sem("waited")
        tail_load = sem("tail_load")

        def r_part(h, q):
            return R[:].rearrange("p i g h o x -> p h o (i g) x")[:, h, 4 * q:4 * q + 4]

        def zt_copy(copy, half):
            src = ps[0:96, 4 + half, 0:384].rearrange("p (a g o) -> p g a o", g=2 * OG, o=2)
            return copy(Zt[0:96].rearrange("p g h a o -> p (g h) a o")[:, :, 12 * half:12 * half + 12, :], src)

        HB = (slice(0, 48), slice(64, 112))

        def xs_copy(copy, ri):
            return copy(XS[0:48, :, ri, :], ps[64 * ri:64 * ri + 48, 6, 0:384].rearrange("p (a c) -> p a c", c=C))

        block = ctx.enter_context(nc.Block())
        xg = x.rearrange("b (h t l z) (u y) o -> u z h l t b (y o)", h=2, t=8, l=2, u=2)
        Zf = Z[:].rearrange("p a b c d -> p (a b c d)")
        Hf = H[:].rearrange("p a b c d -> p (a b c d)")
        Ff = fws[:].rearrange("p a b c -> p (a b c)")
        NT = 16 * 128
        TOK, XTT, QT, KT = [Zf[:, NT * i:NT * i + NT] for i in range(4)]
        VT, PR, PT, Y1 = [Hf[:, NT * i:NT * i + NT] for i in range(4)]
        N1, N1T, T0, T1 = [Ff[:, NT * i:NT * i + NT] for i in range(4)]
        RHS = QT
        H1 = [KT[:, 512 * i:512 * i + 512] for i in range(3)]
        H2 = [VT[:, 512 * i:512 * i + 512] for i in range(3)]
        GP = PR[:, 0:1536]
        fo = sb("fo", 2, 2, 32)
        wb = sb("wb", 5, 128)
        wr1 = sb("wr1", 64)
        wr2 = sb("wr2", 2, E)
        ew1 = R[:].rearrange("p a b c d e -> p (a b c d e)")[:, 0:384]
        ew2 = R[:].rearrange("p a b c d e -> p (a b c d e)")[:, 384:768]
        ew3 = R[:].rearrange("p a b c d e -> p (a b c d e)")[:, 768:1152]
        st = sb("st", 4, 32)
        gt = RT[:].rearrange("p a b c d e -> p (a b c d e)")[:, 0:6 * 32 * E].rearrange("p (a b c) -> p a b c", a=6, b=32)
        gm = sb("gm", 6, 32)
        names = ["t_load", "w_ps", "w_rdy", "relu_a", "relu_d", "fo_rdy", "h_ps", "h_sb", "xt_ps", "xt_sb",
                 "qk_ps", "qk_mul", "qk_sb", "v_ps", "v_sb", "s_ps", "s_sh", "p_exp", "p_sb", "pt_ps", "pt_sb", "o_ps",
                 "ln_c", "ln_sq", "ln_v", "ln_std", "n1_sb", "nt_ps", "nt_sb", "rh_ps", "rh_sb", "lg_ps",
                 "lg_sh", "lg_exp", "g_dif", "g_exp", "gate", "l1_ps", "l1_sb", "l2_ps", "l2_sb", "l3_ps", "l3_rd", "y_sb"]
        T = {n: sem("t_" + n) for n in names}

        @block.sync
        def _(sp):
            sp.dma_start(XN.rearrange("p (b y) -> p b y", y=S), x.rearrange("(b i) x y o -> (i x) b (y o)", i=2)).then_inc(load_x, 16)
            sp.dma_start(cs[:], const).then_inc(load_s, 16)
            sp.dma_start(sm[:], small).then_inc(load_s, 16)
            sp.wait_ge(wr_zero, 1)
            for b in range(4):
                sp.dma_start(pbd[3 * b:3 * b + 3, 32 * b:32 * b + 32], pT).then_inc(load_p, 16)

            def layer_w12(l):
                for kyp in range(2):
                    for ri in range(2):
                        r = 64 * kyp + 32 * ri
                        sp.dma_start(w1c[r:r + 32, r:r + 32], w12[bass.ds(l, 1), 0, :, :].rearrange("a i o -> (a i) o")).then_inc(load_w12, 16)
                        sp.dma_start(w2c[r:r + 32, r:r + 32], w12[bass.ds(l, 1), 1, :, :].rearrange("a i o -> (a i) o")).then_inc(load_w12, 16)

            sp.dma_start(fws[:].rearrange("p a b c -> p (a b c)"), fw[0]).then_inc(load_fw, 16)
            layer_w12(0)
            with sp.Fori(0, L - 1) as l:
                sp.wait_ge(mix_pe, (l + 1) * 18)
                sp.dma_start(fws[:].rearrange("p a b c -> p (a b c)"), fw[bass.ds(l + 1, 1)].rearrange("a p n -> (a p) n")).then_inc(load_fw, 16)
                sp.wait_ge(pe_w2, (l + 1) * BP)
                layer_w12(l + 1)
            sp.wait_ge(mix_pe, L * 18)
            XG = fws[:].rearrange("p a b c -> p (a b c)")[:, 0:BP * 256].rearrange("p (b h l y) -> p h l b y", h=2, l=2, y=32)
            for q in range(NQ):
                for u in range(2):
                    for z in range(2):
                        for xh in range(2):
                            for xl in range(2):
                                r = 8 * u + 4 * z + q
                                sp.dma_start(XG[r:r + 113:16, xh, xl], xg[u, z, xh, xl]).then_inc(load_xg, 16)
            sp.wait_ge(pe_g, L * BP)
            sp.wait_ge(T["w_rdy"], 1)
            sp.dma_start(ew1, ew[:, 0:384]).then_inc(T["t_load"], 16)
            for e in range(E):
                r, q = slice(64 * (e % 2), 64 * (e % 2) + 64), 128 * (e // 2) + 64 * (e % 2)
                sp.dma_start(ew2[r, q:q + 64], ew[r, 384 + 64 * (e // 2):448 + 64 * (e // 2)]).then_inc(T["t_load"], 16)
                sp.dma_start(ew3[r, q:q + 64], ew[r, 576 + 64 * (e // 2):640 + 64 * (e // 2)]).then_inc(T["t_load"], 16)
            sp.wait_ge(T["y_sb"], 1)
            od = out.rearrange("(h p i) x d -> p i x h d", p=2, i=2)
            for p in range(2):
                for i in range(2):
                    sp.dma_start(od[p, i], N1[64 * p:64 * p + 64, :].rearrange("p (h i d) -> p i h d", i=2, d=D)[:, i]).then_inc(stored, 16)
            sp.wait_ge(stored, 64)

        @block.tensor
        def _(pe):
            mm = pe.matmul

            def own_wait():
                pe.sem_inc(waited, 1)

            pe.wait_ge(load_s, 32)
            for l in range(L):
                a = mm(ps[0:32, 0, 4 * l:4 * l + 4], W("w2n")[0:32, 32 * l:32 * l + 32], W("q1T")[0:32, :], start=True, stop=True)
            a.then_inc(setup_pe, 1)
            pe.wait_ge(setup_dve, 1)
            mm(ps[:, 1, 0:16], K("rep")[0:32, :], q1w2, start=True, stop=True)
            mm(ps[:, 2, 0:8], XT[0:32, 0:128], W("comps")[0:32, :], start=True, stop=True).then_inc(setup_pe, 1)

            pe.wait_ge(load_x, 16)
            pe.wait_ge(setup_dve, 2)
            for j in range(4):
                for k in range(4):
                    c = 512 * j + 128 * k
                    a = pe.transpose(ps[:, j, 128 * k:128 * k + 128], XN[:, c:c + 128], K("ident"))
                a.then_inc(e_pe, 1)
            for j in range(4):
                pe.wait_ge((e_act, e_dve)[j % 2], j // 2 + 1)
                a = mm(ps[64 * (j % 2):64 * (j % 2) + 64, 4 + j // 2, :], K("col_fwd"), XNT[:, 512 * j:512 * j + 512], start=True, stop=True)
                if j % 2:
                    a.then_inc(e_pe, 1)
            for j in range(2):
                pe.wait_ge((e_act, e_dve)[j], 3)
                for k in range(4):
                    a = pe.transpose(ps[:, 6 + j, 128 * k:128 * k + 128], US[:, 4 * j + k, :], K("ident"))
                a.then_inc(e_pe, 1)
            pe.wait_ge(load_p, 64)
            mm(ps[:, 4, 0:PM], pbd[0:12, :], K("gmodes")[0:12, :], start=True, stop=True).then_inc(hc_ps, 1)
            pe.wait_ge(e_dve, 4)
            for j in range(2):
                a = mm(ps[0:112, 6, 0:384], K("row_fwd")[:, 112 * j:112 * j + 112],
                       U[:, NKY * j:NKY * j + NKY, :].rearrange("p a b -> p (a b)"), start=(j == 0), stop=(j == 1))
            a.then_inc(e_pe, 1)
            pe.wait_ge(e_dve, 5)
            pe.wait_ge(e_act, 4)
            xs = XS[0:48].rearrange("p (k a) b c -> p k (a b c)", a=2)
            for k in range(K6):
                a = pe.transpose(ps[:, 7, 48 * k:48 * k + 48], xs[:, k], K("ident")[0:48, 0:48])
            a.then_inc(e_pe, 1)
            pe.wait_ge(e_act, 5)
            pe.wait_ge(psel_ready, 1)
            for t in range(BP):
                if t >= 4:
                    pe.wait_ge(h0_sb, t - 3)
                mm(ps[:, t % 4, 0:PM], PSEL[:, 128 * t:128 * t + 128], XT[:, :], start=True, stop=True).then_inc(h0_ps, 1)

            def front(n, t):
                src = Z[:, :, :, bass.ds(t, 1), :]
                mm(ps[:, 4, 0:PM], w1c[:, :], src.rearrange("p k x a b -> p k (a b) x"), start=True, stop=True).then_inc(pe_w1, 1)

            def front_t(n):
                pe.wait_ge(z1_im, 4 * n + 4)
                for k in range(K6):
                    a = pe.transpose(ps[0:96, 4 + k // 3, 128 * (k % 3):128 * (k % 3) + 128],
                                     Z1[:, k].rearrange("p a b c -> p (a b c)"), K("ident"))
                a.then_inc(pe_t, 1)

            def front_a(n):
                pe.wait_ge(zt_0, n + 1)
                pe.wait_ge(zt_1, n + 1)
                for og in range(OG):
                    a = mm(ps[0:112, 4 + og // 4, 128 * (og % 4):128 * (og % 4) + 128],
                           Zt[0:96, og].rearrange("p h a b -> p (h a b)")[:, 0:112], K("row_inv")[0:96, :], start=True, stop=True)
                    if og % 4 == 3:
                        a.then_inc(pe_a, 1)

            def back1(n, q):
                for h in range(2):
                    pe.wait_ge(v_rest, 4 * n + 2 * q + h + 1)
                    if q == 1 and h == 1:
                        pe.wait_ge(g_add, n + 1)
                    for part in range(2):
                        a = mm(ps[:, 2 * q + h, :], ci[0:112, part, :],
                               V[0:112, h, 4 * q:4 * q + 4, :].rearrange("p a b -> p (a b)"), start=(part == 0), stop=(part == 1))
                    a.then_inc(pe_b, 1)

            def back2(n):
                pe.wait_ge(h_add, n + 1)
                for q in range(2):
                    pe.wait_ge(r_ready, 4 * n + 2 * q + 2)
                    own_wait()
                    for h in range(2):
                        a = mm(ps[64 * h:64 * h + 64, 6 + q, :], K("col_fwd"),
                               r_part(h, q), start=True, stop=True)
                    a.then_inc(pe_c, 1)

            def back3(n):
                for q in range(2):
                    pe.wait_ge(us_ready, 2 * n + q + 1)
                    for og in range(4):
                        a = pe.transpose(ps[:, 6 + q, 128 * og:128 * og + 128], US[:, 4 * q + og, :], K("ident"))
                    a.then_inc(pe_tu, 1)

            def back4(n):
                pe.wait_ge(u_ready, n + 1)
                for j in range(2):
                    a = mm(ps[0:112, 6, 0:384], K("row_fwd")[:, 112 * j:112 * j + 112],
                           U[:, NKY * j:NKY * j + NKY, :].rearrange("p a b -> p (a b)"), start=(j == 0), stop=(j == 1))
                a.then_inc(pe_d, 1)

            def grow(n):
                pe.wait_ge(rt_ready, 2 * n + 2)
                for v in range(2):
                    for xt in range(4):
                        a = mm(ps[32 * xt:32 * xt + 32, 3, 0:256], qs[:, v].rearrange("p a b -> p (a b)"),
                               RT[:, :, :, xt, v, :], start=(v == 0), stop=(v == 1))
                a.then_inc(pe_g, 1)

            def back5(n):
                pe.wait_ge(x_re, n + 1)
                pe.wait_ge(x_im, n + 1)
                own_wait()
                xs = XS[0:48].rearrange("p (k a) b c -> p k (a b c)", a=2)
                for k in range(K6):
                    a = pe.transpose(ps[:, 7, 48 * k:48 * k + 48], xs[:, k], K("ident")[0:48, 0:48])
                a.then_inc(pe_t2, 1)

            def back6(n):
                pe.wait_ge(xt_ready, n + 1)
                mm(ps[:, 6, 0:PM], w2c[:, :], XT[:, :], start=True, stop=True).then_inc(pe_w2, 1)

            with pe.Fori(0, L) as l:
                pe.wait_ge(h_whole, l + 1)
                pe.wait_ge(load_fw, l * 16 + 16)
                pe.wait_ge(w_neg, l * 2 + 2)
                for m in range(18):
                    if m >= 4:
                        pe.wait_ge((z_act, z_dve)[m % 2], l * 9 + (m - 4) // 2 + 1)
                    own_wait()
                    for s in range(8):
                        k, kxi = divmod(8 * m + s, NKX)
                        for kyp in range(2):
                            r = slice(64 * kyp, 64 * kyp + 64)
                            a = mm(ps[r, m % 4, 64 * s:64 * s + 64], fws[r, 8 * m + s].rearrange("p a b -> p (a b)"),
                                   H[r, :, k, :, kxi], start=True, stop=True)
                    a.then_inc(mix_pe, 1)
                pe.wait_ge(z_act, l * 9 + 9)
                pe.wait_ge(z_dve, l * 9 + 9)
                pe.wait_ge(q_cur, l + 1)
                pe.wait_ge(ci_rest, 1)
                pe.wait_ge(load_w12, l * 128 + 128)
                pe.wait_ge(w1_neg, l * 2 + 2)
                front(l * BP, 0)
                front_t(l * BP)
                front_a(l * BP)
                back1(l * BP, 0)
                with pe.Fori(0, BP - 1) as t:
                    n = l * BP + t
                    back1(n, 1)
                    front(n + 1, t + 1)
                    back2(n)
                    front_t(n + 1)
                    back3(n)
                    front_a(n + 1)
                    back4(n)
                    grow(n)
                    back5(n)
                    back1(n + 1, 0)
                    back6(n)
                n = l * BP + (BP - 1)
                back1(n, 1)
                back2(n)
                back3(n)
                back4(n)
                grow(n)
                back5(n)
                back6(n)

            pe.wait_ge(h_whole, L + 1)
            for w, name in enumerate(("Wq", "Wqs", "Wk", "Wks", "Wv")):
                for i in range(2):
                    a = mm(ps[64 * i:64 * i + 64, 0, 64 * w:64 * w + 64], W("WqcT" if w < 2 else "WkvcT")[0:64, :], W(name)[0:64, :], start=True, stop=True)
            a.then_inc(T["w_ps"], 1)
            pe.wait_ge(T["fo_rdy"], 1)
            g6 = G[:].rearrange("p (h r) i (a b) y -> p h r i a b y", r=2, a=2)
            for j in range(4):
                pe.wait_ge(T["relu_a"], j + 1)
                for bpp in range(2):
                    for xh in range(2):
                        r = 64 * bpp + 32 * xh
                        o = ps[r:r + 32, 4 + j, :].rearrange("p (h i z y) -> p h i z y", h=4, i=2, z=2)
                        for yh in range(2):
                            for xl in range(2):
                                a = mm(o[:, :, :, yh, :], fo[:, yh, xl, :], g6[:, 4 * j:4 * j + 4, bpp, :, xh, xl, :],
                                       start=(xl == 0), stop=(xl == 1))
                a.then_inc(T["h_ps"], 1)

            def turn(bank0, src, ready, done, free=None):
                for j in range(4):
                    if free is not None:
                        pe.wait_ge(*free)
                    pe.wait_ge(ready, j + 1)
                    for k in range(4):
                        c = 512 * j + 128 * k
                        a = pe.transpose(ps[:, bank0 + j, 128 * k:128 * k + 128], src[:, c:c + 128], K("ident"))
                    a.then_inc(done, 1)

            pe.wait_ge(T["w_rdy"], 1)
            turn(0, TOK, T["h_sb"], T["xt_ps"])
            pe.wait_ge(T["xt_sb"], 4)
            for j in range(4):
                if j >= 2:
                    pe.wait_ge(T["qk_mul"], 4 * j - 4)
                for w in range(4):
                    mm(ps[:, 4 * (j % 2) + w, :], wb[:, w, :], XTT[:, 512 * j:512 * j + 512], start=True, stop=True).then_inc(T["qk_ps"], 1)
            for j in range(4):
                pe.wait_ge(T["qk_mul"], 9 + j)
                for k in range(4):
                    c = 512 * j + 128 * k
                    a = mm(ps[:, j, 128 * k:128 * k + 128], XTT[:, c:c + 128], wb[:, 4, :], start=True, stop=True)
                a.then_inc(T["v_ps"], 1)
            pe.wait_ge(T["qk_sb"], 8)
            pe.wait_ge(T["qk_mul"], 16)
            for j in range(4):
                for k in range(8):
                    c = 512 * j + 64 * k
                    for i in range(2):
                        r = slice(64 * i, 64 * i + 64)
                        a = mm(ps[r, 4 + j, 64 * k:64 * k + 64], QT[r, c:c + 64], KT[r, c:c + 64], start=True, stop=True)
                a.then_inc(T["s_ps"], 1)
            pe.wait_ge(T["v_sb"], 4)
            turn(0, PR, T["p_sb"], T["pt_ps"])
            for j in range(4):
                pe.wait_ge(T["pt_sb"], j + 1)
                for k in range(4):
                    for i in range(2):
                        c = 512 * j + 128 * k + 64 * i
                        for p in range(2):
                            r = slice(64 * p, 64 * p + 64)
                            a = mm(ps[r, 4 + j, 128 * k + 64 * i:128 * k + 64 * i + 64], PT[r, c:c + 64], VT[r, c:c + 64], start=True, stop=True)
                a.then_inc(T["o_ps"], 1)
            pe.wait_ge(T["n1_sb"], 1)
            for j in range(4):
                for k in range(4):
                    c = 512 * j + 128 * k
                    a = pe.transpose(ps[:, j, 128 * k:128 * k + 128], N1[:, c:c + 128], K("ident"))
                a.then_inc(T["nt_ps"], 1)
            for j in range(4):
                pe.wait_ge(T["nt_sb"], j + 1)
                mm(ps[0:64, 4 + j, :], wr1[:, :], N1T[:, 512 * j:512 * j + 512], start=True, stop=True).then_inc(T["rh_ps"], 1)
            pe.wait_ge(T["rh_sb"], 4)
            for g in range(16):
                a = mm(ps[:, 0, 12 * g:12 * g + 12], RHS[0:64, 128 * g:128 * g + 128], wr2[0:64].rearrange("p a b -> p (a b)"), start=True, stop=True)
            a.then_inc(T["lg_ps"], 1)
            pe.wait_ge(T["t_load"], 16 * 13)
            pe.wait_ge(T["gate"], 1)
            for n in range(8):
                i, j = n // 4, n % 4
                r = slice(64 * i, 64 * i + 64)
                for p in range(3):
                    m = 3 * n + p
                    if m >= 2:
                        pe.wait_ge(T["l1_sb"], m - 1)
                    mm(ps[:, m % 2, :], ew1[r, 128 * p:128 * p + 128], N1T[r, 512 * j:512 * j + 512], start=True, stop=True).then_inc(T["l1_ps"], 1)
                for p in range(3):
                    m = 3 * n + p
                    pe.wait_ge(T["l1_sb"], m + 1)
                    if m >= 2:
                        pe.wait_ge(T["l2_sb"], m - 1)
                    mm(ps[:, 2 + m % 2, :], ew2[:, 128 * p:128 * p + 128], H1[p], start=True, stop=True).then_inc(T["l2_ps"], 1)
                for p in range(3):
                    pe.wait_ge(T["l2_sb"], 3 * n + p + 1)
                    if n:
                        pe.wait_ge(T["l3_rd"], 3 * n - 2 + p)
                    mm(ps[:, 4 + p, :], K("one")[0:1, :], W("eb3")[0:1, 128 * p:128 * p + 128].unsqueeze(1).to_broadcast([1, 4, 128]),
                       start=True, stop=False, skip_group_check=True)
                    for k in range(4):
                        a = mm(ps[:, 4 + p, 128 * k:128 * k + 128], H2[p][:, 128 * k:128 * k + 128], ew3[:, 128 * p:128 * p + 128],
                               start=False, stop=True, skip_group_check=True)
                    a.then_inc(T["l3_ps"], 1)

        @block.scalar
        def _(act):
            cp = act.copy
            act.wait_ge(load_s, 32)
            cp(ci[:, 0, :], K("col_inv")).then_inc(ci_first, 1)
            for j in range(2):
                act.wait_ge(e_pe, 2 * j + 1)
                cp(XNT[:, 1024 * j:1024 * j + 512], ps[:, 2 * j, :]).then_inc(e_act, 1)
            act.wait_ge(e_pe, 5)
            cp(US[:, 0:4, :].rearrange("p a b -> p (a b)"), ps[:, 4, :]).then_inc(e_act, 1)
            act.wait_ge(e_pe, 9)
            xs_copy(act.copy, 1).then_inc(e_act, 1)
            act.wait_ge(e_pe, 10)
            cp(XT[:, :], ps[:, 7, 0:PM]).then_inc(e_act, 1)
            act.wait_ge(setup_dve, 2)
            cp(G[:].rearrange("p b i x y -> p (b i) (x y)"), S0[:].rearrange("p x y -> p (x y)").unsqueeze(1).to_broadcast([128, 2 * BP, 128])).then_inc(g_init, 1)
            act.wait_ge(load_fw, 16)
            for kyp in range(2):
                r = slice(64 * kyp + 32, 64 * kyp + 64)
                act.mul(fws[r, :, 0, :], fws[r, :, 0, :], -1.0).then_inc(w_neg, 1)

            def back_a(n):
                for q in range(2):
                    for h in range(2):
                        act.wait_ge(pe_b, 4 * n + 2 * q + h + 1)
                        act.activation(r_part(h, q), ps[:, 2 * q + h, :].rearrange("p (g a x) -> p g a x", g=4, x=2), ACT.Relu).then_inc(r_ready, 1)

            def back_b(n):
                for q in range(2):
                    act.wait_ge(pe_c, 2 * n + q + 1)
                    cp(US[:, 4 * q:4 * q + 4, :].rearrange("p a b -> p (a b)"), ps[:, 6 + q, :]).then_inc(us_ready, 1)

            def front_z(n):
                act.wait_ge(pe_t, n + 1)
                zt_copy(act.copy, 0).then_inc(zt_0, 1)

            def front_v(n):
                for q in range(2):
                    act.wait_ge(pe_a, 2 * n + q + 1)
                    for h in range(2):
                        cp(V[HB[h], h, 4 * q:4 * q + 4, :].rearrange("p a b -> p (a b)"), ps[HB[h], 4 + q, :]).then_inc(v_first, 1)

            def back_c(n):
                act.wait_ge(pe_d, n + 1)
                xs_copy(act.copy, 1).then_inc(x_im, 1)
                act.wait_ge(pe_t2, n + 1)
                cp(XT[:, :], ps[:, 7, 0:PM]).then_inc(xt_ready, 1)

            with act.Fori(0, L) as l:
                for m in range(0, 18, 2):
                    act.wait_ge(mix_pe, l * 18 + m + 1)
                    cp(Z[:].rearrange("p a b c d -> p (a b c d)")[:, 512 * m:512 * m + 512], ps[:, m % 4, :]).then_inc(z_act, 1)
                front_z(l * BP)
                front_v(l * BP)
                with act.Fori(0, BP - 1) as t:
                    n = l * BP + t
                    back_a(n)
                    back_b(n)
                    front_z(n + 1)
                    front_v(n + 1)
                    back_c(n)
                n = l * BP + (BP - 1)
                back_a(n)
                back_b(n)
                back_c(n)

            act.wait_ge(h_whole, L + 1)
            gf = G[:].rearrange("p a b c d -> p (a b c d)")
            for j in range(4):
                c = slice(2048 * j, 2048 * j + 2048)
                act.wait_ge(T["relu_d"], j + 1)
                act.activation(gf[:, c], gf[:, c], ACT.Relu).then_inc(T["relu_a"], 1)
            for j in range(4):
                act.wait_ge(T["h_ps"], j + 1)
                act.activation(TOK[:, 512 * j:512 * j + 512], ps[:, 4 + j, :], ACT.Identity, bias=W("q2b")).then_inc(T["h_sb"], 1)
            for j in range(4):
                act.wait_ge(T["xt_ps"], j + 1)
                cp(XTT[:, 512 * j:512 * j + 512], ps[:, j, :]).then_inc(T["xt_sb"], 1)
            for j in range(4):
                act.wait_ge(T["v_ps"], j + 1)
                cp(VT[:, 512 * j:512 * j + 512], ps[:, j, :]).then_inc(T["v_sb"], 1)
            for j in range(4):
                act.wait_ge(T["s_sh"], j + 1)
                c = slice(512 * j, 512 * j + 512)
                act.activation(PR[:, c], T0[:, c], ACT.Exp).then_inc(T["p_exp"], 1)
            for j in range(4):
                act.wait_ge(T["pt_ps"], j + 1)
                cp(PT[:, 512 * j:512 * j + 512], ps[:, j, :]).then_inc(T["pt_sb"], 1)

            def ln_act(k):
                act.wait_ge(T["ln_c"], k + 1)
                act.activation(T1, T0, ACT.Square).then_inc(T["ln_sq"], 1)
                act.wait_ge(T["ln_v"], k + 1)
                act.activation(st[:, 2, :], st[:, 1, :], ACT.Sqrt).then_inc(T["ln_std"], 1)

            ln_act(0)
            for j in range(4):
                act.wait_ge(T["nt_ps"], j + 1)
                cp(N1T[:, 512 * j:512 * j + 512], ps[:, j, :]).then_inc(T["nt_sb"], 1)
            for j in range(4):
                act.wait_ge(T["rh_ps"], j + 1)
                act.activation(RHS[0:64, 512 * j:512 * j + 512], ps[0:64, 4 + j, :], ACT.Relu, bias=W("rb1")[0:64, :]).then_inc(T["rh_sb"], 1)
            act.wait_ge(T["lg_sh"], 1)
            act.activation(gt[:, 1], gt[:, 0], ACT.Exp).then_inc(T["lg_exp"], 1)
            act.wait_ge(T["g_dif"], 1)
            act.activation(gm[:, 3], gm[:, 2], ACT.Exp).then_inc(T["g_exp"], 1)
            for n in range(8):
                for p in range(3):
                    act.wait_ge(T["l1_ps"], 3 * n + p + 1)
                    act.activation(H1[p], ps[:, (3 * n + p) % 2, :], ACT.Relu, bias=W("eb1")[:, p:p + 1]).then_inc(T["l1_sb"], 1)
                for p in range(3):
                    act.wait_ge(T["l2_ps"], 3 * n + p + 1)
                    act.activation(H2[p], ps[:, 2 + (3 * n + p) % 2, :], ACT.Relu, bias=W("eb2")[:, p:p + 1]).then_inc(T["l2_sb"], 1)
            ln_act(1)

        @block.vector
        def _(ve):
            chain = [0]
            step = sem("ve_step")

            def then(ins):
                chain[0] += 1
                ins.then_inc(step, 1)
                ve.wait_ge(step, chain[0])

            tt, ts, cp = ve.tensor_tensor, ve.tensor_scalar, ve.tensor_copy
            ve.wait_ge(load_s, 32)
            cp(XT[0:32, 0:128].rearrange("p (a q) -> p a q", q=4), W("q1T")[0:32, :].unsqueeze(1).to_broadcast([32, 32, 4]))
            ve.wait_ge(ci_first, 1)
            tt(ci[:, 1, :], K("col_inv"), ci[:, 0, :], ALU.subtract)
            ve.memset(Zt[:], 0.0)
            ve.memset(V[:].bitcast(F32), 0.0).then_inc(ci_rest, 1)
            ve.wait_ge(setup_pe, 1)
            cp(q1w2, ps[0:32, 0, 0:16]).then_inc(setup_dve, 1)
            ve.memset(dc[:], 0.0)
            ve.wait_ge(setup_pe, 2)
            for l in range(L):
                tt(qs_all[:, l].rearrange("p v m q -> p (v m) q"), ps[:, 1, 4 * l:4 * l + 4].unsqueeze(1).to_broadcast([128, 16, 4]),
                   K("same").unsqueeze(2).to_broadcast([128, 16, 4]), ALU.mult)
            then(cp(comp[:, 0:8], ps[:, 2, 0:8]))
            then(ve.reduce_sum(comp[:, 8:9], comp[:, 3:8], AX.X))
            then(tt(comp[:, 9:10], comp[:, 8:9], W("q1b"), ALU.add))
            then(ts(gxp[:, :], K("gx_part"), comp[:, 1:2], comp[:, 9:10], ALU.mult, ALU.add))
            for xr in range(4):
                a = ts(S0[:, xr, :], K("gy_row"), comp[:, 2:3], gxp[:, xr:xr + 1], ALU.mult, ALU.add)
            a.then_inc(setup_dve, 1)
            for j in range(2):
                ve.wait_ge(e_pe, 2 * j + 2)
                cp(XNT[:, 1024 * j + 512:1024 * j + 1024], ps[:, 2 * j + 1, :]).then_inc(e_dve, 1)
            ve.wait_ge(e_pe, 6)
            cp(US[:, 4:8, :].rearrange("p a b -> p (a b)"), ps[:, 5, :]).then_inc(e_dve, 1)
            dst = U[:].rearrange("p m (j h k o) -> p j h k o m", j=2, h=2, o=2)
            for j in range(2):
                ve.wait_ge(e_pe, 7 + j)
                src = ps[:, 6 + j, :].rearrange("p (k h m) -> p k h m", k=4, h=2)
                for h in range(2):
                    a = cp(dst[:, j, h], src[:, :, h, 0:48].rearrange("p k (o m) -> p k o m", o=2))
            a.then_inc(e_dve, 1)
            ve.wait_ge(hc_ps, 1)
            cp(HC, ps[:, 4, 0:PM])
            ve.wait_ge(e_pe, 9)
            xs_copy(cp, 0).then_inc(e_dve, 1)
            then(tt(pb.rearrange("p (a c) -> p a c", a=4), K("quarter").unsqueeze(2).to_broadcast([128, 4, 32]),
                    W("px").unsqueeze(1).to_broadcast([128, 4, 32]), ALU.mult))
            for t in range(BP):
                a = ts(PSEL[:, 128 * t:128 * t + 128], pb, K("of_pair")[:, t:t + 1], None, ALU.mult)
            a.then_inc(psel_ready, 1)
            for t in range(BP):
                ve.wait_ge(h0_ps, t + 1)
                tt(H[:, t].rearrange("p a b c -> p (a b c)"), ps[:, t % 4, 0:PM], HC, ALU.add).then_inc(h0_sb, 1)
            ve.wait_ge(g_init, 1)
            ve.wait_ge(h0_sb, BP)
            ve.sem_inc(g_add, 1)
            ve.sem_inc(h_add, 1)
            ve.sem_inc(h_whole, 1)

            def z1(n):
                ve.wait_ge(pe_w1, n + 1)
                tt(Z1[:, :, 0].rearrange("p k i x -> p k (i x)"), ps[:, 4, 0:PM].rearrange("p (k m) -> p k m", k=K6),
                   dc[:].rearrange("p k i x -> p k (i x)"), ALU.add).then_inc(z1_re, 1)
                ve.wait_ge(z1_re, n + 1)
                for kyp in range(2):
                    j0, j1 = slice(64 * kyp, 64 * kyp + 32), slice(64 * kyp + 32, 64 * kyp + 64)
                    cp(Z1[j1, :, 1].rearrange("p k i x -> p k (i x)"), Z1[j0, :, 0].rearrange("p k i x -> p k (i x)")).then_inc(z1_im, 1)
                    ts(Z1[j0, :, 1].rearrange("p k i x -> p k (i x)"), Z1[j1, :, 0].rearrange("p k i x -> p k (i x)"),
                       -1.0, None, ALU.mult).then_inc(z1_im, 1)

            def turn_r(n, i):
                if i == 0:
                    ve.wait_ge(r_ready, 4 * n + 4)
                ve.transpose(RT[:, i].rearrange("p a b c d -> p (a b c d)"), R[:, i].rearrange("p a b c d -> p (a b c d)")).then_inc(rt_ready, 1)

            def front_z(n):
                ve.wait_ge(pe_t, n + 1)
                zt_copy(cp, 1).then_inc(zt_1, 1)

            def front_v(n, q):
                for h in range(2):
                    ve.wait_ge(v_first, 4 * n + 2 * q + h + 1)
                    tt(V[HB[1 - h], h, 4 * q:4 * q + 4, :].rearrange("p a b -> p (a b)"), ps[HB[h], 4 + q, :],
                       V[HB[h], h, 4 * q:4 * q + 4, :].rearrange("p a b -> p (a b)"), ALU.subtract).then_inc(v_rest, 1)

            def back_u(n):
                for q in range(2):
                    ve.wait_ge(pe_tu, 2 * n + q + 1)
                    src = ps[:, 6 + q, :].rearrange("p (g h m) -> p g h m", g=4, h=2)
                    dst = U[:].rearrange("p m (g h o) -> p g h o m", g=OG, h=2)
                    for h in range(2):
                        ins = cp(dst[:, 4 * q:4 * q + 4, h], src[:, :, h, 0:48].rearrange("p g (o m) -> p g o m", o=2))
                ins.then_inc(u_ready, 1)

            def back_x(n):
                ve.wait_ge(pe_d, n + 1)
                xs_copy(cp, 0).then_inc(x_re, 1)

            def back_g(n, t):
                ve.wait_ge(pe_g, n + 1)
                gd = G[:, bass.ds(t, 1)].rearrange("p a i x y -> p (a i x y)")
                tt(gd, gd, ps[:, 3, 0:256], ALU.add).then_inc(g_add, 1)

            def back_h(n, t):
                ve.wait_ge(pe_w2, n + 1)
                hd = H[:, bass.ds(t, 1)].rearrange("p a k i x -> p (a k i x)")
                tt(hd, hd, ps[:, 6, 0:PM], ALU.add).then_inc(h_add, 1)

            with ve.Fori(0, L) as l:
                ve.wait_ge(h_whole, l + 1)
                ts(dc[:, 0, :, 0], W("b1")[:, bass.ds(l, 1)].to_broadcast([128, 2]), float(S), None, ALU.mult).then_inc(dc_ready, 1)
                for m in range(1, 18, 2):
                    ve.wait_ge(mix_pe, l * 18 + m + 1)
                    cp(Z[:].rearrange("p a b c d -> p (a b c d)")[:, 512 * m:512 * m + 512], ps[:, m % 4, :]).then_inc(z_dve, 1)
                ve.wait_ge(dc_ready, l + 1)
                z1(l * BP)
                front_z(l * BP)
                front_v(l * BP, 0)
                front_v(l * BP, 1)
                with ve.Fori(0, BP - 1) as t:
                    n = l * BP + t
                    z1(n + 1)
                    turn_r(n, 0)
                    front_z(n + 1)
                    back_u(n)
                    turn_r(n, 1)
                    front_v(n + 1, 0)
                    back_x(n)
                    back_g(n, t)
                    front_v(n + 1, 1)
                    back_h(n, t)
                n = l * BP + (BP - 1)
                turn_r(n, 0)
                turn_r(n, 1)
                back_u(n)
                back_x(n)
                back_g(n, BP - 1)
                back_h(n, BP - 1)
                ve.wait_ge(h_add, l * BP + BP + 1)
                hdc = H[0:32, :, 0, :, 0]
                ve.scalar_tensor_tensor(out=hdc, in0=W("w2b")[0:32, bass.ds(l, 1)].unsqueeze(2).to_broadcast([32, BP, 2]), scalar=float(S), in1=hdc,
                                        op0=ALU.mult, op1=ALU.add).then_inc(h_whole, 1)

            ve.wait_ge(h_whole, L + 1)
            gf = G[:].rearrange("p a b c d -> p (a b c d)")
            ts(fo[:].rearrange("p a b c -> p (a b c)"), K("pick_out"), W("q2"), None, ALU.mult).then_inc(T["fo_rdy"], 1)
            ve.wait_ge(load_xg, 16 * 64)
            for j in range(4):
                c = slice(2048 * j, 2048 * j + 2048)
                ve.scalar_tensor_tensor(out=gf[:, c], in0=Ff[:, c], scalar=comp[:, 0:1], in1=gf[:, c], op0=ALU.mult, op1=ALU.add).then_inc(T["relu_d"], 1)
            ve.wait_ge(pe_g, L * BP)
            ve.memset(wb[:], 0.0)
            ve.memset(wr1[:], 0.0)
            ve.memset(R[:], 0.0)
            then(ve.memset(wr2[:], 0.0))
            for i in range(2):
                r = slice(64 * i, 64 * i + 64)
                cp(wr1[r, 32 * i:32 * i + 32], W("rw1")[r, :])
                cp(wr2[32 * i:32 * i + 32, i, :], W("rw2")[32 * i:32 * i + 32, :])
            ve.wait_ge(T["w_ps"], 1)
            for i in range(2):
                r = slice(64 * i, 64 * i + 64)
                a = cp(wb[r, :, 64 * i:64 * i + 64], ps[r, 0, 0:320].rearrange("p (a b) -> p a b", a=5))
            a.then_inc(T["w_rdy"], 1)
            b8 = [128, 8, 64]
            for j in range(4):
                c = slice(512 * j, 512 * j + 512)
                for w in range(4):
                    dst = (QT, T0, KT, T1)[w][:, c].rearrange("p (a b) -> p a b", b=64)
                    ve.wait_ge(T["qk_ps"], 4 * j + w + 1)
                    tt(dst, ps[:, 4 * (j % 2) + w, :].rearrange("p (a b) -> p a b", b=64),
                       K(("cos_q", "sin_q", "cos_k", "sin_k")[w]).unsqueeze(1).to_broadcast(b8), ALU.mult).then_inc(T["qk_mul"], 1)
            ve.wait_ge(T["qk_sb"], 8)
            for j in range(4):
                c = slice(512 * j, 512 * j + 512)
                t0 = T0[:, c].rearrange("p (a b) -> p a b", b=64)
                ve.wait_ge(T["s_ps"], j + 1)
                then(tt(t0, ps[:, 4 + j, :].rearrange("p (a b) -> p a b", b=64), K("causal").unsqueeze(1).to_broadcast(b8), ALU.add))
                then(ve.reduce_max(st[:, 0, 8 * j:8 * j + 8], t0, AX.X))
                tt(t0, t0, st[:, 0, 8 * j:8 * j + 8].unsqueeze(2).to_broadcast(b8), ALU.subtract).then_inc(T["s_sh"], 1)
            for j in range(4):
                c = slice(512 * j, 512 * j + 512)
                pj = PR[:, c].rearrange("p (a b) -> p a b", b=64)
                ve.wait_ge(T["p_exp"], j + 1)
                then(ve.reduce_sum(st[:, 1, 8 * j:8 * j + 8], pj, AX.X))
                then(ve.reciprocal(st[:, 2, 8 * j:8 * j + 8], st[:, 1, 8 * j:8 * j + 8]))
                tt(pj, pj, st[:, 2, 8 * j:8 * j + 8].unsqueeze(2).to_broadcast(b8), ALU.mult).then_inc(T["p_sb"], 1)
            for j in range(4):
                c = slice(512 * j, 512 * j + 512)
                ve.wait_ge(T["o_ps"], j + 1)
                a = tt(Y1[:, c], ps[:, 4 + j, :], TOK[:, c], ALU.add)
            then(a)
            b32 = [128, 32, 64]

            def layernorm(k, y, n):
                y3, t3, q3, n3 = [v.rearrange("p (a b) -> p a b", b=64) for v in (y, T0, T1, n)]
                then(ve.reduce_sum(st[:, 0, :], y3, AX.X))
                then(ts(st[:, 0, :], st[:, 0, :], 1.0 / D, None, ALU.mult))
                tt(t3, y3, st[:, 0, :].unsqueeze(2).to_broadcast(b32), ALU.subtract).then_inc(T["ln_c"], 1)
                ve.wait_ge(T["ln_sq"], k + 1)
                then(ve.reduce_sum(st[:, 1, :], q3, AX.X))
                ts(st[:, 1, :], st[:, 1, :], 1.0 / D, 1e-5, ALU.mult, ALU.add).then_inc(T["ln_v"], 1)
                ve.wait_ge(T["ln_std"], k + 1)
                then(ve.reciprocal(st[:, 3, :], st[:, 2, :]))
                return tt(n3, t3, st[:, 3, :].unsqueeze(2).to_broadcast(b32), ALU.mult)

            layernorm(0, Y1, N1).then_inc(T["n1_sb"], 1)
            b6 = [128, 32, E]
            lg, ex, pr, sel1, sel2, tmp = [gt[:, i] for i in range(6)]

            def per_token(v):
                return v.unsqueeze(2).to_broadcast(b6)

            rank = K("rank").unsqueeze(1).to_broadcast(b6)
            ve.wait_ge(T["lg_ps"], 1)
            then(tt(lg, ps[:, 0, 0:192].rearrange("p (a b) -> p a b", b=E), W("rb2").unsqueeze(1).to_broadcast(b6), ALU.add))
            then(ve.reduce_max(gm[:, 0], lg, AX.X))
            tt(lg, lg, per_token(gm[:, 0]), ALU.subtract).then_inc(T["lg_sh"], 1)
            ve.wait_ge(T["lg_exp"], 1)
            then(ve.reduce_sum(gm[:, 0], ex, AX.X))
            then(ve.reciprocal(gm[:, 1], gm[:, 0]))
            then(tt(pr, ex, per_token(gm[:, 1]), ALU.mult))

            def pick(p, best, sel):
                then(ve.reduce_max(best, p, AX.X))
                then(tt(tmp, p, per_token(best), ALU.is_equal))
                then(tt(tmp, tmp, rank, ALU.mult))
                then(ve.reduce_max(gm[:, 5], tmp, AX.X))
                then(tt(sel, tmp, per_token(gm[:, 5]), ALU.is_equal))

            pick(pr, gm[:, 0], sel1)
            then(ve.scalar_tensor_tensor(out=pr, in0=sel1, scalar=-2.0, in1=pr, op0=ALU.mult, op1=ALU.add))
            pick(pr, gm[:, 1], sel2)
            tt(gm[:, 2], gm[:, 1], gm[:, 0], ALU.subtract).then_inc(T["g_dif"], 1)
            ve.wait_ge(T["g_exp"], 1)
            then(ts(gm[:, 4], gm[:, 3], 1.0, None, ALU.add))
            then(ve.reciprocal(gm[:, 4], gm[:, 4]))
            then(tt(gm[:, 5], gm[:, 3], gm[:, 4], ALU.mult))
            then(tt(sel1, sel1, per_token(gm[:, 4]), ALU.mult))
            then(tt(sel2, sel2, per_token(gm[:, 5]), ALU.mult))
            tt(lg, sel1, sel2, ALU.add).then_inc(T["gate"], 1)
            ve.wait_ge(T["gate"], 1)
            gate = lg.rearrange("p (h i) e -> p h i e", i=2)
            n1v = N1.rearrange("p (h i d) -> p h i d", i=2, d=D)
            y1v = Y1.rearrange("p (h i d) -> p h i d", i=2, d=D)
            gp = GP.rearrange("p (e h d) -> p e h d", e=E, h=4)
            for n in range(8):
                i, j = n // 4, n % 4
                for p in range(3):
                    ve.wait_ge(T["l3_ps"], 3 * n + p + 1)
                    pv = ps[:, 4 + p, :].rearrange("p (h e d) -> p e h d", e=2, d=D)
                    for e in range(2):
                        a = tt(gp[:, 2 * p + e], pv[:, e], gate[:, 4 * j:4 * j + 4, i, 2 * p + e].unsqueeze(2).to_broadcast([128, 4, 64]), ALU.mult)
                    a.then_inc(T["l3_rd"], 1)
                ve.wait_ge(T["l3_rd"], 3 * n + 3)
                yv = y1v[:, 4 * j:4 * j + 4, i]
                then(ve.reduce_sum(yv, gp.rearrange("p e h d -> p h d e"), AX.X))
                then(tt(yv, yv, n1v[:, 4 * j:4 * j + 4, i], ALU.add))
            layernorm(1, Y1, N1).then_inc(T["y_sb"], 1)

        @block.gpsimd
        def _(po):
            po.memset(w1c[:], 0.0)
            po.memset(w2c[:], 0.0)
            po.memset(pbd[:], 0.0).then_inc(wr_zero, 1)
            po.wait_ge(wr_zero, 1)

            def layer_w1_q(l):
                po.wait_ge(load_w12, l * 128 + 128)
                po.sem_inc(waited, 1)
                for kyp in range(2):
                    r = slice(64 * kyp + 32, 64 * kyp + 64)
                    po.tensor_scalar(w1c[r, :], w1c[r, :], -1.0, None, ALU.mult).then_inc(w1_neg, 1)
                    po.wait_ge(w1_neg, l * 2 + kyp + 1)
                    po.sem_inc(waited, 1)
                po.wait_ge(h_whole, l + 1)
                po.sem_inc(waited, 1)
                po.tensor_copy(qs[:].rearrange("p a b c -> p (a b c)"), qs_all[:, bass.ds(l, 1)].rearrange("p a b c d -> p (a b c d)")).then_inc(q_cur, 1)
                po.wait_ge(q_cur, l + 1)
                po.sem_inc(waited, 1)

            layer_w1_q(0)
            with po.Fori(1, L) as l:
                po.wait_ge(load_fw, l * 16 + 16)
                po.sem_inc(waited, 1)
                for kyp in range(2):
                    r = slice(64 * kyp + 32, 64 * kyp + 64)
                    po.tensor_scalar(fws[r, :, 0, :], fws[r, :, 0, :], -1.0, None, ALU.mult).then_inc(w_neg, 1)
                    po.wait_ge(w_neg, l * 2 + kyp + 1)
                    po.sem_inc(waited, 1)
                layer_w1_q(l)
            for j in range(4):
                c = slice(512 * j, 512 * j + 512)
                po.wait_ge(T["qk_mul"], 4 * j + 2)
                po.tensor_tensor(QT[:, c], QT[:, c], T0[:, c], ALU.add).then_inc(T["qk_sb"], 1)
                po.wait_ge(T["qk_mul"], 4 * j + 4)
                po.tensor_tensor(KT[:, c], KT[:, c], T1[:, c], ALU.add).then_inc(T["qk_sb"], 1)


def kernel(**inputs):
    import concourse.bacc as bacc
    from concourse.bass_utils import run_bass_kernel_spmd as run

    a = {k: np.asarray(v) for k, v in inputs.items()}
    t = {k[7:]: v for k, v in a.items() if k.startswith("L0_tok_")}
    at = {k[8:]: v for k, v in a.items() if k.startswith("L0_attn_")}
    ff = {k[7:]: v for k, v in a.items() if k.startswith("L0_ffn_")}
    w = t["fw"].transpose(0, 5, 2, 1, 4, 6, 3).reshape(L, 2, K6, C, 2 * 12, 2, C)
    w = w.transpose(0, 1, 3, 2, 4, 5, 6)
    fw = np.stack([w, w[:, :, :, :, :, ::-1]], 2).reshape(L, 128, K6 * NKX * 2 * C)
    w12 = np.stack([t["w1_w"].transpose(0, 2, 1), t["w2_w"].transpose(0, 2, 1)], 1)
    pT = np.concatenate([t["p_w"].T[1:], t["p_b"][None]], 0)
    small = np.zeros((128, NSMALL), np.float32)

    def put(name, v, r0=0):
        c, width = SAT[name]
        v = np.asarray(v).reshape(-1, width)
        small[r0:r0 + v.shape[0], c:c + width] = v

    put("px", np.tile(t["p_w"][:, 0], (128, 1)))
    put("q1T", t["q1_w"].T)
    put("w2n", t["w2_w"].transpose(1, 0, 2))
    put("comps", np.concatenate([t["p_w"], t["p_b"][:, None], t["w2_b"].T], 1))
    put("q1b", np.tile(t["q1_b"], 32))
    put("q2", np.tile(t["q2_w"][0], 32))
    put("q2b", np.tile(t["q2_b"], 128))
    put("b1", t["w1_b"].T)
    put("w2b", t["w2_b"].T)
    put("WqcT", at["Wq_comp"].T)
    put("WkvcT", at["Wkv_comp"].T)
    swap = np.arange(HR) ^ 1
    for n in "qk":
        put("W" + n, np.concatenate([at[f"W{n}c"], at[f"W{n}r"]], 1))
        put("W" + n + "s", np.concatenate([at[f"W{n}c"], at[f"W{n}r"][:, swap]], 1))
    put("Wv", at["Wv"])
    for i in range(2):
        put("rw1", ff["router_w1"], 64 * i)
        put("rw2", ff["router_w2"], 32 * i)
        put("rb1", ff["router_b1"], 32 * i)
    put("rb2", np.tile(ff["router_b2"], (128, 1)))
    put("eb1", ff["expert_b1"].reshape(3, 128).T)
    put("eb2", ff["expert_b2"].reshape(3, 128).T)
    put("eb3", ff["expert_b3"].reshape(1, 384))
    e1 = np.tile(ff["expert_w1"].transpose(1, 0, 2).reshape(D, E * HID), (2, 1))
    e2 = ff["expert_w2"].reshape(3, 128, HID).transpose(1, 0, 2).reshape(128, 192)
    e3 = ff["expert_w3"].reshape(3, 128, D).transpose(1, 0, 2).reshape(128, 192)
    arrays = {"x": a["x"], "fw": fw, "w12": w12, "pT": pT, "small": small,
              "ew": np.concatenate([e1, e2, e3], 1), "const": constants()}
    nc = bacc.Bacc("TRN2", target_bir_lowering=False, num_devices=1)
    maps, args = {}, []
    for name, v in arrays.items():
        v = np.ascontiguousarray(v)
        maps["in_" + name] = v
        args.append(nc.dram_tensor("in_" + name, v.shape, mybir.dt.from_np(v.dtype), kind="ExternalInput").ap())
    o = nc.dram_tensor("out_0", (B, S, S), F32, kind="ExternalOutput").ap()
    program(nc, *args, o)
    r = run(nc, [maps], core_ids=[0])
    return r.results[0]["out_0"]
```

```python
from contextlib import ExitStack

import numpy as np

import concourse.bass as bass
from concourse import mybir

F32 = mybir.dt.float32
F32R = mybir.dt.float32r
ALU = mybir.AluOpType
ACT = mybir.ActivationFunctionType
AX = mybir.AxisListType

B, S, C, L, NQ = 64, 64, 32, 4, 4
NKX, NKY = 24, 12
BP = B // 2
OG = C // 4
K6 = NKY // 2
PM = K6 * 2 * NKX
D, E, HID, RH = 64, 6, 64, 32
HR = 16
NEG = -3.0e38

LAYOUT = [("ident", 128), ("row_inv", 128), ("col_inv", 128), ("col_fwd", 64), ("row_fwd", 224),
          ("gx_part", 4), ("gy_row", 32), ("same", 16), ("rep", 128), ("pick_out", 128),
          ("gmodes", PM), ("quarter", 4), ("of_pair", BP),
          ("cos_q", 64), ("sin_q", 64), ("cos_k", 64), ("sin_k", 64), ("causal", 64), ("rank", 6), ("own", 16)]
AT = {}
for _name, _width in LAYOUT:
    AT[_name] = (sum(w for n, w in LAYOUT[:len(AT)]), _width)
NCONST = sum(w for _, w in LAYOUT)


def constants():
    f = {n: np.zeros((128, w), np.float64) for n, w in LAYOUT}
    kx = np.array(list(range(12)) + list(range(-12, 0)))
    ky = np.arange(NKY)
    pos = np.arange(S)
    tx = 2 * np.pi * np.outer(kx, pos) / S
    ty = 2 * np.pi * np.outer(ky, pos) / S
    f["ident"][:] = np.eye(128)
    for b in range(2):
        f["row_inv"][b * 24:b * 24 + 24, b * 64:b * 64 + 64] = np.cos(tx) / 8
        f["row_inv"][48 + b * 24:72 + b * 24, b * 64:b * 64 + 64] = -np.sin(tx) / 8
    v = np.zeros((K6, 2, 2, 2, 2, S))
    for k in range(NKY):
        w = (1.0 if k == 0 else 2.0) / 8
        for o in range(2):
            v[k % K6, k // K6, 0, o, o] = w * np.cos(ty[k])
            v[k % K6, k // K6, 1, o, o] = w * np.sin(ty[k])
    f["col_inv"][:48] = f["col_inv"][64:112] = v.reshape(48, 128)
    c = np.zeros((2, S, 2, 2, NKY))
    order = [K6 * (m % 2) + m // 2 for m in range(NKY)]
    for o in range(2):
        c[o, :, o, 0] = np.cos(ty[order]).T / 8
        c[o, :, o, 1] = -np.sin(ty[order]).T / 8
    f["col_fwd"][:, :48] = c.reshape(128, 48)
    d = np.zeros((2, 128, 112))
    for b in range(2):
        r = slice(b * 64, b * 64 + 64)
        re, im = slice(b * 24, b * 24 + 24), slice(64 + b * 24, 88 + b * 24)
        d[0, r, re], d[0, r, im] = np.cos(tx).T / 8, -np.sin(tx).T / 8
        d[1, r, re], d[1, r, im] = np.sin(tx).T / 8, np.cos(tx).T / 8
    f["row_fwd"][:] = d.transpose(1, 0, 2).reshape(128, 224)
    grid = np.linspace(0.0, 1.0, S, dtype=np.float32)
    p = np.arange(128)
    xt, xv, yh, x0 = p // 32, p // 16 % 2, p // 8 % 2, p // 4 % 2
    xr = np.arange(4)
    xg = 32 * (xr // 2) + 2 * (xr % 2) + (8 * xt + 4 * xv + x0)[:, None]
    f["gx_part"][:] = grid[xg]
    f["gy_row"][:] = grid[32 * yh[:, None] + np.arange(32)]
    k_yh, k_x0 = p // 32 % 2, p % 2
    e = np.zeros((128, 2, 2, 2, 2))
    for v in range(2):
        e[p, v, v, k_yh, k_x0] = 1
    f["same"][:] = e.reshape(128, 16)
    r = np.zeros((C, 2, 2, 2, OG, 2))
    for ch in range(C):
        r[ch, ch % 2, :, ch // 2 % 2, ch // 4, :] = 1
    f["rep"][:C] = r.reshape(C, 128)
    fields = np.stack([np.tile(grid[:, None], (1, S)), np.tile(grid[None], (S, 1)), np.ones((S, S))])
    m = np.fft.fft2(fields.astype(np.float64))[:, kx][:, :, ky] / S
    g = np.zeros((2, 2, 3, K6, 2, NKX))
    for kyp in range(2):
        for k in range(K6):
            g[kyp, 0, :, k] = m[:, None, :, K6 * kyp + k].real
            g[kyp, 1, :, k] = m[:, None, :, K6 * kyp + k].imag
    f["gmodes"][:12] = g.reshape(12, PM)
    f["quarter"][:] = (p[:, None] // 32) == np.arange(4)
    f["of_pair"][:] = (p[:, None] % 32) == np.arange(32)
    g = np.zeros((128, 2, 2, 32))
    for xl in range(2):
        g[p, yh, xl, 8 * xt + 4 * xv + 2 * xl + x0] = 1
    f["pick_out"][:] = g.reshape(128, 128)
    half = HR // 2
    theta = (1.0 / (np.float32(10000.0) ** (np.arange(half, dtype=np.float32) / np.float32(half)))).astype(np.float32)
    ang = (pos.astype(np.float32)[:, None] * theta[None]).astype(np.float32)
    cos, sin = np.ones((64, S)), np.zeros((64, S))
    for i in range(half):
        for s in range(2):
            cos[48 + 2 * i + s] = np.cos(ang[:, i])
            sin[48 + 2 * i + s] = (-1, 1)[s] * np.sin(ang[:, i])
    for n, m in (("cos", cos), ("sin", sin)):
        f[n + "_k"][:] = np.tile(m, (2, 1))
        f[n + "_q"][:] = np.tile(m, (2, 1)) / np.sqrt(D)
    f["causal"][:] = np.where(np.arange(64)[None] > (p % 64)[:, None], NEG, 0)
    f["rank"][:] = np.arange(E, 0, -1)
    f["own"][:] = p[:, None] // E == np.arange(16)
    return np.concatenate([f[n] for n, _ in LAYOUT], 1).astype(np.float32)


SMALL = [("px", 32), ("q1T", 4), ("w2n", L * 32), ("comps", 8), ("q1b", 1), ("q2", 1), ("q2b", 1),
         ("b1", L), ("w2b", L), ("WqcT", 64), ("WkvcT", 64), ("Wq", 64), ("Wqs", 64),
         ("Wk", 64), ("Wks", 64), ("Wv", 64), ("rw1", 32), ("rw2", 6), ("rb1", 1), ("rb2", 6),
         ("eb1", 3), ("eb2", 3), ("eb3", D)]
SAT = {}
for _name, _width in SMALL:
    SAT[_name] = (sum(w for n, w in SMALL[:len(SAT)]), _width)
NSMALL = sum(w for _, w in SMALL)


def program(nc, x, fw, w12, pT, small, ew, const, out):
    with ExitStack() as ctx:
        def sb(name, *shape, dtype=F32):
            return ctx.enter_context(nc.sbuf_tensor(name, [128, *shape], dtype))

        def sem(name):
            return ctx.enter_context(nc.semaphore(name))

        ps = ctx.enter_context(nc.psum_tensor("ps", [128, 8, 512], F32))
        cs = sb("cs", NCONST)
        sm = sb("sm", NSMALL)

        def K(name):
            a, w = AT[name]
            return cs[:, a:a + w]

        def W(name):
            a, w = SAT[name]
            return sm[:, a:a + w]

        H = sb("H", BP, K6, 2, NKX)
        Z = sb("Z", K6, NKX, BP, 2)
        G = sb("G", BP, 2, 4, 32)
        fws = sb("fws", K6 * NKX, 2, C)
        w1c = sb("w1c", 128)
        w2c = sb("w2c", 128)
        pbd = sb("pbd", 128)
        dc = sb("dc", K6, 2, NKX)
        qs_all = sb("qs_all", L, 2, 8, NQ)
        qs = sb("qs", 2, 8, NQ)
        Z1 = sb("Z1", K6, 2, 2, NKX)
        Zt = sb("Zt", OG, 2, 32, 2)
        V = sb("V", 2, OG, 128, dtype=F32R)
        ci = sb("ci", 2, 128, dtype=F32R)
        R = sb("R", 2, 32, 2, OG, 2)
        RT = sb("RT", 2, 2, 4, 2, 64)
        US = sb("US", OG, 128)
        U = [sb(name, 2 * NKY, C, dtype=F32R) for name in ("u_first", "u_rest")]
        rf = sb("rf", 2, 224, dtype=F32R)
        XS = sb("XS", NKY, 2, C)
        XT = sb("XT", PM)
        q1w2 = Z1[0:32].rearrange("p a b c d -> p (a b c d)")[:, PM + 128:PM + 128 + L * NQ]
        comp = sb("comp", 12)
        gxp = sb("gxp", 4)
        S0 = sb("S0", 4, 32)
        XN = R[:].rearrange("p a b c d e -> p (a b c d e)")
        UX = XN[:, 0:2 * NKY * BP].rearrange("p (m b) -> p m b", b=BP)
        XNT = RT[:].rearrange("p a b c d e -> p (a b c d e)")
        HC = Z1[:].rearrange("p a b c d -> p (a b c d)")[:, 0:PM]
        pb = Z1[:].rearrange("p a b c d -> p (a b c d)")[:, PM:PM + 128]
        PSEL = Z[:].rearrange("p a b c d -> p (a b c d)")[:, 0:BP * 128]
        load_s = sem("load_s")
        load_fw = sem("load_fw")
        load_w12 = sem("load_w12")
        load_p = sem("load_p")
        load_x = sem("load_x")
        load_xg = sem("load_xg")
        wr_zero = sem("wr_zero")
        w_neg = sem("w_neg")
        w1_neg = sem("w1_neg")
        setup_pe = sem("setup_pe")
        setup_dve = sem("setup_dve")
        q_cur = sem("q_cur")
        e_pe = sem("e_pe")
        e_act = sem("e_act"); e_dve = sem("e_dve")
        hc_ps = sem("hc_ps")
        psel_ready = sem("psel_ready")
        h0_ps = sem("h0_ps"); h0_sb = sem("h0_sb")
        g_init = sem("g_init")
        mix_pe = sem("mix_pe")
        z_act = sem("z_act"); z_dve = sem("z_dve")
        dc_ready = sem("dc_ready")
        pe_w1 = sem("pe_w1")
        z1_re = sem("z1_re"); z1_im = sem("z1_im")
        pe_t = sem("pe_t")
        zt_0 = sem("zt_0"); zt_1 = sem("zt_1")
        pe_a = sem("pe_a")
        v_first = sem("v_first"); v_rest = sem("v_rest")
        ci_first = sem("ci_first"); ci_rest = sem("ci_rest")
        pe_b = sem("pe_b")
        r_ready = sem("r_ready")
        rt_ready = sem("rt_ready")
        pe_c = sem("pe_c")
        us_ready = sem("us_ready")
        pe_tu = sem("pe_tu")
        u_first = sem("u_first"); u_rest = sem("u_rest")
        pe_d = sem("pe_d")
        x_re = sem("x_re"); x_im = sem("x_im")
        pe_t2 = sem("pe_t2"); xt_ready = sem("xt_ready")
        pe_w2 = sem("pe_w2"); h_add = sem("h_add")
        pe_g = sem("pe_g"); g_add = sem("g_add")
        stored = sem("stored")
        waited = sem("waited")

        def r_part(h, q):
            return R[:].rearrange("p i g h o x -> p h o (i g) x")[:, h, 4 * q:4 * q + 4]

        def zt_copy(copy, half):
            src = ps[0:96, 4 + half, 0:384].rearrange("p (a g o) -> p g a o", g=2 * OG, o=2)
            return copy(Zt[0:96].rearrange("p g h a o -> p (g h) a o")[:, :, 12 * half:12 * half + 12, :], src)

        def u_parts(q, h):
            src = ps[:, 6 + q, :].rearrange("p (g h m) -> p g h m", g=4, h=2)[:, :, h, 0:48].rearrange("p g (o m) -> p g o m", o=2)
            return src, [u[:].rearrange("p m (g h o) -> p g h o m", g=OG, h=2)[:, 4 * q:4 * q + 4, h] for u in U]

        HB = (slice(0, 48), slice(64, 112))

        def xs_copy(copy, ri):
            return copy(XS[0:48, :, ri, :], ps[64 * ri:64 * ri + 48, 6, 0:384].rearrange("p (a c) -> p a c", c=C))

        block = ctx.enter_context(nc.Block())
        xg = x.rearrange("b (h t l z) (u y) o -> u z h l t b (y o)", h=2, t=8, l=2, u=2)
        Zf = Z[:].rearrange("p a b c d -> p (a b c d)")
        Hf = H[:].rearrange("p a b c d -> p (a b c d)")
        Ff = fws[:].rearrange("p a b c -> p (a b c)")
        NT = 16 * 128
        TOK, XTT, QT, KT = [Zf[:, NT * i:NT * i + NT] for i in range(4)]
        VT, PR, PT, Y1 = [Hf[:, NT * i:NT * i + NT] for i in range(4)]
        N1, N1T, T0, T1 = [Ff[:, NT * i:NT * i + NT] for i in range(4)]
        RHS = QT
        H1 = [KT[:, 512 * i:512 * i + 512] for i in range(3)]
        H2 = [VT[:, 512 * i:512 * i + 512] for i in range(3)]
        GP = PR[:, 0:1536]
        OUT = T0
        fo = sb("fo", 2, 2, 32)
        wb = sb("wb", 5, 128)
        wr1 = sb("wr1", 64)
        wr2 = sb("wr2", 2, E)
        ew1 = R[:].rearrange("p a b c d e -> p (a b c d e)")[:, 0:384]
        ew2 = Ff[:, 4 * NT:4 * NT + 384]
        ew3 = Ff[:, 4 * NT + 384:4 * NT + 768]
        EB3 = Hf[0:96, 4 * NT:4 * NT + 16 * D]
        gateT = RT[:].rearrange("p a b c d e -> p (a b c d e)")[0:96, 1152:1408]
        st = sb("st", 4, 32)
        so = sb("so", 4, 8, 4)
        gt = RT[:].rearrange("p a b c d e -> p (a b c d e)")[:, 0:6 * 32 * E].rearrange("p (a b c) -> p a b c", a=6, b=32)
        gm = sb("gm", 6, 32)
        names = ["t_load", "prep", "zero", "w_ps", "w_rdy", "eb3_rdy",
                 "relu_x", "relu_p", "relu_d", "relu_a",
                 "h_ps", "h_sb", "xt_ps", "xt_sb",
                 "qk_ps", "qk_mul", "qk_sb", "v_ps", "v_sb",
                 "s_ps", "s_sh", "p_exp", "p_sb", "pt_ps", "pt_sb", "o_ps",
                 "ln_c", "ln_sq", "ln_v", "ln_std", "n1_sb", "nt_ps", "nt_sb",
                 "rh_ps", "rh_sb", "lg_ps", "lg_sh", "lg_exp", "g_dif", "g_exp", "gate",
                 "gt_ps", "gt_sb", "nb_ps", "nb_sb",
                 "l1_ps", "l1_sb", "l2_ps", "l2_sb", "l3_ps", "l3_rd",
                 "lo_v", "lo_std", "y_sb"]
        T = {n: sem("t_" + n) for n in names}

        @block.sync
        def _(sp):
            sp.dma_start(XN.rearrange("p (b y) -> p b y", y=S), x.rearrange("(b i) x y o -> (i x) b (y o)", i=2)).then_inc(load_x, 16)
            sp.dma_start(cs[:], const).then_inc(load_s, 16)
            sp.dma_start(sm[:], small).then_inc(load_s, 16)
            sp.wait_ge(wr_zero, 1)
            for b in range(4):
                sp.dma_start(pbd[3 * b:3 * b + 3, 32 * b:32 * b + 32], pT).then_inc(load_p, 16)

            def layer_w12(l):
                for kyp in range(2):
                    for ri in range(2):
                        r = 64 * kyp + 32 * ri
                        sp.dma_start(w1c[r:r + 32, r:r + 32], w12[bass.ds(l, 1), 0, :, :].rearrange("a i o -> (a i) o")).then_inc(load_w12, 16)
                        sp.dma_start(w2c[r:r + 32, r:r + 32], w12[bass.ds(l, 1), 1, :, :].rearrange("a i o -> (a i) o")).then_inc(load_w12, 16)

            sp.dma_start(fws[:].rearrange("p a b c -> p (a b c)"), fw[0]).then_inc(load_fw, 16)
            layer_w12(0)
            with sp.Fori(0, L - 1) as l:
                sp.wait_ge(mix_pe, (l + 1) * 18)
                sp.dma_start(fws[:].rearrange("p a b c -> p (a b c)"), fw[bass.ds(l + 1, 1)].rearrange("a p n -> (a p) n")).then_inc(load_fw, 16)
                sp.wait_ge(pe_w2, (l + 1) * BP)
                layer_w12(l + 1)
            sp.wait_ge(mix_pe, L * 18)
            XG = fws[:].rearrange("p a b c -> p (a b c)")[:, 0:BP * 256].rearrange("p (b h l y) -> p h l b y", h=2, l=2, y=32)
            for q in range(NQ):
                for u in range(2):
                    for z in range(2):
                        for xh in range(2):
                            for xl in range(2):
                                r = 8 * u + 4 * z + q
                                sp.dma_start(XG[r:r + 113:16, xh, xl], xg[u, z, xh, xl]).then_inc(load_xg, 16)
            sp.wait_ge(T["zero"], 1)
            for e in range(E):
                r, q = slice(64 * (e % 2), 64 * (e % 2) + 64), 128 * (e // 2) + 64 * (e % 2)
                sp.dma_start(ew2[r, q:q + 64], ew[r, 384 + 64 * (e // 2):448 + 64 * (e // 2)]).then_inc(T["t_load"], 16)
                sp.dma_start(ew3[r, q:q + 64], ew[r, 576 + 64 * (e // 2):640 + 64 * (e // 2)]).then_inc(T["t_load"], 16)
            sp.wait_ge(pe_g, L * BP)
            sp.dma_start(ew1, ew[:, 0:384]).then_inc(T["t_load"], 16)
            od = out.rearrange("(h p i) x d -> p i x h d", p=2, i=2)
            ov = OUT.rearrange("p (h i d) -> p i h d", i=2, d=D)
            for n in range(8):
                i, j = n // 4, n % 4
                sp.wait_ge(T["y_sb"], n + 1)
                for p in range(2):
                    sp.dma_start(od[p, i][:, 4 * j:4 * j + 4], ov[64 * p:64 * p + 64, i, 4 * j:4 * j + 4]).then_inc(stored, 16)
            sp.wait_ge(stored, 16 * 16)

        @block.tensor
        def _(pe):
            mm = pe.matmul

            def own_wait():
                pe.sem_inc(waited, 1)

            pe.wait_ge(load_s, 32)
            for l in range(L):
                a = mm(ps[0:32, 0, 4 * l:4 * l + 4], W("w2n")[0:32, 32 * l:32 * l + 32], W("q1T")[0:32, :], start=True, stop=True)
            a.then_inc(setup_pe, 1)
            pe.wait_ge(setup_dve, 1)
            mm(ps[:, 1, 0:16], K("rep")[0:32, :], q1w2, start=True, stop=True)
            mm(ps[:, 2, 0:8], XT[0:32, 0:128], W("comps")[0:32, :], start=True, stop=True).then_inc(setup_pe, 1)

            for w, name in enumerate(("Wq", "Wqs", "Wk", "Wks", "Wv")):
                for i in range(2):
                    a = mm(ps[64 * i:64 * i + 64, 3, 64 * w:64 * w + 64], W("WqcT" if w < 2 else "WkvcT")[0:64, :], W(name)[0:64, :], start=True, stop=True)
            a.then_inc(T["w_ps"], 1)

            pe.wait_ge(load_x, 16)
            pe.wait_ge(setup_dve, 2)
            for j in range(4):
                for k in range(4):
                    c = 512 * j + 128 * k
                    a = pe.transpose(ps[:, j, 128 * k:128 * k + 128], XN[:, c:c + 128], K("ident"))
                a.then_inc(e_pe, 1)
            for j in range(4):
                pe.wait_ge((e_act, e_dve)[j % 2], j // 2 + 1)
                a = mm(ps[64 * (j % 2):64 * (j % 2) + 64, 4 + j // 2, :], K("col_fwd"), XNT[:, 512 * j:512 * j + 512], start=True, stop=True)
                if j % 2:
                    a.then_inc(e_pe, 1)
            for j in range(2):
                pe.wait_ge((e_act, e_dve)[j], 3)
                for k in range(4):
                    a = pe.transpose(ps[:, 6 + j, 128 * k:128 * k + 128], US[:, 4 * j + k, :], K("ident"))
                a.then_inc(e_pe, 1)
            pe.wait_ge(load_p, 64)
            mm(ps[:, 4, 0:PM], pbd[0:12, :], K("gmodes")[0:12, :], start=True, stop=True).then_inc(hc_ps, 1)
            pe.wait_ge(e_dve, 4)
            for j in range(2):
                a = mm(ps[0:112, 6, 0:384], K("row_fwd")[:, 112 * j:112 * j + 112],
                       UX[:, NKY * j:NKY * j + NKY, :].rearrange("p a b -> p (a b)"), start=(j == 0), stop=(j == 1))
            a.then_inc(e_pe, 1)
            pe.wait_ge(e_dve, 5)
            pe.wait_ge(e_act, 4)
            xs = XS[0:48].rearrange("p (k a) b c -> p k (a b c)", a=2)
            for k in range(K6):
                a = pe.transpose(ps[:, 7, 48 * k:48 * k + 48], xs[:, k], K("ident")[0:48, 0:48])
            a.then_inc(e_pe, 1)
            pe.wait_ge(e_act, 5)
            pe.wait_ge(psel_ready, 1)
            for t in range(BP):
                if t >= 4:
                    pe.wait_ge(h0_sb, t - 3)
                mm(ps[:, t % 4, 0:PM], PSEL[:, 128 * t:128 * t + 128], XT[:, :], start=True, stop=True).then_inc(h0_ps, 1)

            def channels_1(n, t):
                src = Z[:, :, :, bass.ds(t, 1), :]
                mm(ps[:, 4, 0:PM], w1c[:, :], src.rearrange("p k x a b -> p k (a b) x"), start=True, stop=True).then_inc(pe_w1, 1)

            def turn_z1(n):
                pe.wait_ge(z1_im, 4 * n + 4)
                for k in range(K6):
                    a = pe.transpose(ps[0:96, 4 + k // 3, 128 * (k % 3):128 * (k % 3) + 128],
                                     Z1[:, k].rearrange("p a b c -> p (a b c)"), K("ident"))
                a.then_inc(pe_t, 1)

            def rows_inverse(n):
                pe.wait_ge(zt_0, n + 1)
                pe.wait_ge(zt_1, n + 1)
                for og in range(OG):
                    a = mm(ps[0:112, 4 + og // 4, 128 * (og % 4):128 * (og % 4) + 128],
                           Zt[0:96, og].rearrange("p h a b -> p (h a b)")[:, 0:112], K("row_inv")[0:96, :], start=True, stop=True)
                    if og % 4 == 3:
                        a.then_inc(pe_a, 1)

            def columns_inverse(n, q):
                for h in range(2):
                    pe.wait_ge(v_rest, 4 * n + 2 * q + h + 1)
                    if q == 1 and h == 1:
                        pe.wait_ge(g_add, n + 1)
                    for part in range(2):
                        a = mm(ps[:, 2 * q + h, :], ci[0:112, part, :],
                               V[0:112, h, 4 * q:4 * q + 4, :].rearrange("p a b -> p (a b)"), start=(part == 0), stop=(part == 1))
                    a.then_inc(pe_b, 1)

            def columns_forward(n):
                pe.wait_ge(h_add, n + 1)
                for q in range(2):
                    pe.wait_ge(r_ready, 4 * n + 2 * q + 2)
                    own_wait()
                    for h in range(2):
                        a = mm(ps[64 * h:64 * h + 64, 6 + q, :], K("col_fwd"),
                               r_part(h, q), start=True, stop=True)
                    a.then_inc(pe_c, 1)

            def turn_us(n):
                for q in range(2):
                    pe.wait_ge(us_ready, 2 * n + q + 1)
                    for og in range(4):
                        a = pe.transpose(ps[:, 6 + q, 128 * og:128 * og + 112], US[0:112, 4 * q + og, :], K("ident")[0:112, 0:112])
                    a.then_inc(pe_tu, 1)

            def rows_forward(n):
                pe.wait_ge(u_rest, 4 * n + 4)
                for j in range(2):
                    for f, u in ((0, 0), (1, 0), (0, 1)):
                        a = mm(ps[0:112, 6, 0:384], rf[:, f, 112 * j:112 * j + 112],
                               U[u][:, NKY * j:NKY * j + NKY, :].rearrange("p a b -> p (a b)"), start=(j == f == u == 0), stop=(j == 1 and u == 1))
                a.then_inc(pe_d, 1)

            def output_share(n, vs=(0, 1)):
                pe.wait_ge(rt_ready, 2 * n + 2)
                for v in vs:
                    for xt in range(4):
                        a = mm(ps[32 * xt:32 * xt + 32, 3, 0:256], qs[:, v].rearrange("p a b -> p (a b)"),
                               RT[:, :, :, xt, v, :], start=(v == 0), stop=(v == 1))
                if v == 1:
                    a.then_inc(pe_g, 1)

            def turn_xs(n):
                pe.wait_ge(x_re, n + 1)
                pe.wait_ge(x_im, n + 1)
                own_wait()
                xs = XS[0:48].rearrange("p (k a) b c -> p k (a b c)", a=2)
                for k in range(K6):
                    a = pe.transpose(ps[:, 7, 48 * k:48 * k + 48], xs[:, k], K("ident")[0:48, 0:48])
                a.then_inc(pe_t2, 1)

            def channels_2(n):
                pe.wait_ge(xt_ready, n + 1)
                mm(ps[:, 6, 0:PM], w2c[:, :], XT[:, :], start=True, stop=True).then_inc(pe_w2, 1)

            with pe.Fori(0, L) as l:
                pe.wait_ge(h_add, l * BP + 1)
                pe.wait_ge(load_fw, l * 16 + 16)
                pe.wait_ge(w_neg, l * 2 + 2)
                for m in range(18):
                    if m == 3:
                        pe.wait_ge(g_add, l * BP + 1)
                    if m >= 4:
                        pe.wait_ge((z_act, z_dve)[m % 2], l * 9 + (m - 4) // 2 + 1)
                    own_wait()
                    for s in range(8):
                        k, kxi = divmod(8 * m + s, NKX)
                        for kyp in range(2):
                            r = slice(64 * kyp, 64 * kyp + 64)
                            a = mm(ps[r, m % 4, 64 * s:64 * s + 64], fws[r, 8 * m + s].rearrange("p a b -> p (a b)"),
                                   H[r, :, k, :, kxi], start=True, stop=True)
                    a.then_inc(mix_pe, 1)
                pe.wait_ge(z_act, l * 9 + 9)
                pe.wait_ge(z_dve, l * 9 + 9)
                pe.wait_ge(q_cur, l + 1)
                pe.wait_ge(ci_rest, 1)
                pe.wait_ge(load_w12, l * 128 + 128)
                pe.wait_ge(w1_neg, l * 2 + 2)
                channels_1(l * BP, 0)
                turn_z1(l * BP)
                rows_inverse(l * BP)
                columns_inverse(l * BP, 0)
                with pe.Fori(0, BP - 1) as t:
                    n = l * BP + t
                    columns_inverse(n, 1)
                    channels_1(n + 1, t + 1)
                    columns_forward(n)
                    turn_z1(n + 1)
                    turn_us(n)
                    rows_inverse(n + 1)
                    rows_forward(n)
                    output_share(n)
                    turn_xs(n)
                    columns_inverse(n + 1, 0)
                    channels_2(n)
                n = l * BP + (BP - 1)
                columns_inverse(n, 1)
                columns_forward(n)
                turn_us(n)
                rows_forward(n)
                output_share(n)
                turn_xs(n)
                channels_2(n)

            pe.wait_ge(h_add, L * BP + 1)
            pe.wait_ge(g_add, L * BP + 1)
            pe.wait_ge(T["prep"], 5)
            g6 = G[:].rearrange("p (h r) i (a b) y -> p h r i a b y", r=2, a=2)
            for j in range(4):
                if j < 3:
                    pe.wait_ge(T["relu_p"], j + 1)
                else:
                    pe.wait_ge(T["relu_a"], 1)
                for bpp in range(2):
                    for xh in range(2):
                        r = 64 * bpp + 32 * xh
                        o = ps[r:r + 32, 4 + j, :].rearrange("p (h i z y) -> p h i z y", h=4, i=2, z=2)
                        for yh in range(2):
                            for xl in range(2):
                                a = mm(o[:, :, :, yh, :], fo[:, yh, xl, :], g6[:, 4 * j:4 * j + 4, bpp, :, xh, xl, :],
                                       start=(xl == 0), stop=(xl == 1))
                a.then_inc(T["h_ps"], 1)

            def turn(j, bank0, src, ready, done):
                pe.wait_ge(ready, j + 1)
                for k in range(4):
                    c = 512 * j + 128 * k
                    a = pe.transpose(ps[:, bank0 + j, 128 * k:128 * k + 128], src[:, c:c + 128], K("ident"))
                a.then_inc(done, 1)

            for j in range(4):
                turn(j, 0, TOK, T["h_sb"], T["xt_ps"])
            pe.wait_ge(T["w_rdy"], 2)
            pe.wait_ge(T["xt_sb"], 4)

            def qk(j):
                for w in range(4):
                    if j:
                        pe.wait_ge(T["qk_mul"], 4 * j - 3 + w)
                    mm(ps[:, w, :], wb[:, w, :], XTT[:, 512 * j:512 * j + 512], start=True, stop=True).then_inc(T["qk_ps"], 1)

            def scores(j):
                pe.wait_ge(T["qk_sb"], 2 * j + 2)
                for k in range(8):
                    c = 512 * j + 64 * k
                    for i in range(2):
                        r = slice(64 * i, 64 * i + 64)
                        a = mm(ps[r, 4 + j, 64 * k:64 * k + 64], QT[r, c:c + 64], KT[r, c:c + 64], start=True, stop=True)
                a.then_inc(T["s_ps"], 1)

            qk(0)
            qk(1)
            scores(0)
            qk(2)
            scores(1)
            qk(3)
            scores(2)
            for j in range(4):
                pe.wait_ge(T["qk_mul"], 13 + j)
                for k in range(4):
                    c = 512 * j + 128 * k
                    a = mm(ps[:, j, 128 * k:128 * k + 128], XTT[:, c:c + 128], wb[:, 4, :], start=True, stop=True)
                a.then_inc(T["v_ps"], 1)
            scores(3)
            pe.wait_ge(T["v_sb"], 4)

            def values(j):
                pe.wait_ge(T["pt_sb"], j + 1)
                for k in range(4):
                    for i in range(2):
                        c = 512 * j + 128 * k + 64 * i
                        for p in range(2):
                            r = slice(64 * p, 64 * p + 64)
                            a = mm(ps[r, 4 + j, 128 * k + 64 * i:128 * k + 64 * i + 64], PT[r, c:c + 64], VT[r, c:c + 64], start=True, stop=True)
                a.then_inc(T["o_ps"], 1)

            turn(0, 0, PR, T["p_sb"], T["pt_ps"])
            for j in range(1, 4):
                turn(j, 0, PR, T["p_sb"], T["pt_ps"])
                values(j - 1)
            values(3)
            turn(0, 0, N1, T["n1_sb"], T["nt_ps"])
            for j in range(4):
                if j < 3:
                    turn(j + 1, 0, N1, T["n1_sb"], T["nt_ps"])
                pe.wait_ge(T["nt_sb"], j + 1)
                mm(ps[0:64, 4 + j, :], wr1[:, :], N1T[:, 512 * j:512 * j + 512], start=True, stop=True).then_inc(T["rh_ps"], 1)
            pe.wait_ge(T["rh_sb"], 4)
            for g in range(16):
                a = mm(ps[:, 7, 12 * g:12 * g + 12], RHS[0:64, 128 * g:128 * g + 128], wr2[0:64].rearrange("p a b -> p (a b)"), start=True, stop=True)
            a.then_inc(T["lg_ps"], 1)
            pe.wait_ge(T["t_load"], 16 * 13)
            for n in range(8):
                i, j = n // 4, n % 4
                r = slice(64 * i, 64 * i + 64)
                for p in range(3):
                    m = 3 * n + p
                    if m >= 2:
                        pe.wait_ge(T["l1_sb"], m - 1)
                    mm(ps[:, m % 2, :], ew1[r, 128 * p:128 * p + 128], N1T[r, 512 * j:512 * j + 512], start=True, stop=True).then_inc(T["l1_ps"], 1)
                for p in range(3):
                    m = 3 * n + p
                    pe.wait_ge(T["l1_sb"], m + 1)
                    if m >= 2:
                        pe.wait_ge(T["l2_sb"], m - 1)
                    mm(ps[:, 2 + m % 2, :], ew2[:, 128 * p:128 * p + 128], H1[p], start=True, stop=True).then_inc(T["l2_ps"], 1)
                if n == 1:
                    pe.wait_ge(T["gate"], 1)
                    for k in range(2):
                        a = pe.transpose(ps[0:96, 7, 128 * k:128 * k + 128], gt[:, 0].rearrange("p a b -> p (a b)")[:, 96 * k:96 * k + 96], K("ident"))
                    a.then_inc(T["gt_ps"], 1)
                    pe.wait_ge(T["gt_sb"], 1)
                    pe.wait_ge(T["eb3_rdy"], 1)
                    for k in range(4):
                        if k:
                            pe.wait_ge(T["nb_sb"], k)
                        mm(ps[:, 7, :], gateT[:, 128 * (k // 2):128 * (k // 2) + 128], EB3[:, 512 * (k % 2):512 * (k % 2) + 512],
                           start=True, stop=True).then_inc(T["nb_ps"], 1)
                for p in range(3):
                    pe.wait_ge(T["l2_sb"], 3 * n + p + 1)
                    if n:
                        pe.wait_ge(T["l3_rd"], 3 * n - 2 + p)
                    for k in range(4):
                        a = mm(ps[:, 4 + p, 128 * k:128 * k + 128], H2[p][:, 128 * k:128 * k + 128], ew3[:, 128 * p:128 * p + 128],
                               start=True, stop=True)
                    a.then_inc(T["l3_ps"], 1)

        @block.scalar
        def _(act):
            cp = act.copy
            act.wait_ge(load_s, 32)
            cp(ci[:, 0, :], K("col_inv"))
            cp(rf[:, 0, :], K("row_fwd")).then_inc(ci_first, 1)
            for j in range(2):
                act.wait_ge(e_pe, 2 * j + 1)
                cp(XNT[:, 1024 * j:1024 * j + 512], ps[:, 2 * j, :]).then_inc(e_act, 1)
            act.wait_ge(e_pe, 5)
            cp(US[:, 0:4, :].rearrange("p a b -> p (a b)"), ps[:, 4, :]).then_inc(e_act, 1)
            act.wait_ge(e_pe, 9)
            xs_copy(act.copy, 1).then_inc(e_act, 1)
            act.wait_ge(e_pe, 10)
            cp(XT[:, :], ps[:, 7, 0:PM]).then_inc(e_act, 1)
            act.wait_ge(setup_dve, 2)
            cp(G[:].rearrange("p b i x y -> p (b i) (x y)"), S0[:].rearrange("p x y -> p (x y)").unsqueeze(1).to_broadcast([128, 2 * BP, 128])).then_inc(g_init, 1)
            act.wait_ge(load_fw, 16)
            for kyp in range(2):
                r = slice(64 * kyp + 32, 64 * kyp + 64)
                act.mul(fws[r, :, 0, :], fws[r, :, 0, :], -1.0).then_inc(w_neg, 1)

            def relu(n):
                for q in range(2):
                    for h in range(2):
                        act.wait_ge(pe_b, 4 * n + 2 * q + h + 1)
                        act.activation(r_part(h, q), ps[:, 2 * q + h, :].rearrange("p (g a x) -> p g a x", g=4, x=2), ACT.Relu).then_inc(r_ready, 1)

            def copy_us(n):
                for q in range(2):
                    act.wait_ge(pe_c, 2 * n + q + 1)
                    cp(US[:, 4 * q:4 * q + 4, :].rearrange("p a b -> p (a b)"), ps[:, 6 + q, :]).then_inc(us_ready, 1)

            def copy_zt(n):
                act.wait_ge(pe_t, n + 1)
                zt_copy(act.copy, 0).then_inc(zt_0, 1)

            def split_u(n):
                for q in range(2):
                    act.wait_ge(pe_tu, 2 * n + q + 1)
                    for h in range(2):
                        src, (first, rest) = u_parts(q, h)
                        cp(first, src).then_inc(u_first, 1)

            def split_v(n):
                for q in range(2):
                    act.wait_ge(pe_a, 2 * n + q + 1)
                    for h in range(2):
                        cp(V[HB[h], h, 4 * q:4 * q + 4, :].rearrange("p a b -> p (a b)"), ps[HB[h], 4 + q, :]).then_inc(v_first, 1)

            def copy_x(n):
                act.wait_ge(pe_d, n + 1)
                xs_copy(act.copy, 1).then_inc(x_im, 1)
                act.wait_ge(pe_t2, n + 1)
                cp(XT[:, :], ps[:, 7, 0:PM]).then_inc(xt_ready, 1)

            with act.Fori(0, L) as l:
                for m in range(0, 18, 2):
                    act.wait_ge(mix_pe, l * 18 + m + 1)
                    cp(Z[:].rearrange("p a b c d -> p (a b c d)")[:, 512 * m:512 * m + 512], ps[:, m % 4, :]).then_inc(z_act, 1)
                copy_zt(l * BP)
                split_v(l * BP)
                with act.Fori(0, BP - 1) as t:
                    n = l * BP + t
                    relu(n)
                    copy_us(n)
                    copy_zt(n + 1)
                    split_u(n)
                    split_v(n + 1)
                    copy_x(n)
                n = l * BP + (BP - 1)
                relu(n)
                copy_us(n)
                split_u(n)
                copy_x(n)

            act.wait_ge(h_add, L * BP + 1)
            act.wait_ge(g_add, L * BP + 1)
            gf = G[:].rearrange("p a b c d -> p (a b c d)")
            act.wait_ge(T["relu_d"], 1)
            act.activation(gf[:, 6144:8192], gf[:, 6144:8192], ACT.Relu).then_inc(T["relu_a"], 1)
            for j in range(4):
                act.wait_ge(T["h_ps"], j + 1)
                act.activation(TOK[:, 512 * j:512 * j + 512], ps[:, 4 + j, :], ACT.Identity, bias=W("q2b")).then_inc(T["h_sb"], 1)
            for j in range(4):
                act.wait_ge(T["xt_ps"], j + 1)
                cp(XTT[:, 512 * j:512 * j + 512], ps[:, j, :]).then_inc(T["xt_sb"], 1)

            def exponentials(j):
                act.wait_ge(T["s_sh"], j + 1)
                c = slice(512 * j, 512 * j + 512)
                act.activation(PR[:, c], T0[:, c], ACT.Exp).then_inc(T["p_exp"], 1)

            for j in range(3):
                exponentials(j)
            for j in range(4):
                act.wait_ge(T["v_ps"], j + 1)
                cp(VT[:, 512 * j:512 * j + 512], ps[:, j, :]).then_inc(T["v_sb"], 1)
            exponentials(3)
            for j in range(4):
                act.wait_ge(T["pt_ps"], j + 1)
                cp(PT[:, 512 * j:512 * j + 512], ps[:, j, :]).then_inc(T["pt_sb"], 1)

            def ln_square(j):
                c = slice(512 * j, 512 * j + 512)
                act.wait_ge(T["ln_c"], j + 1)
                act.activation(T1[:, c], T0[:, c], ACT.Square).then_inc(T["ln_sq"], 1)

            def ln_root(j):
                g = slice(8 * j, 8 * j + 8)
                act.wait_ge(T["ln_v"], j + 1)
                act.activation(st[:, 2, g], st[:, 1, g], ACT.Sqrt).then_inc(T["ln_std"], 1)

            ln_square(0)
            for j in range(1, 4):
                ln_square(j)
                ln_root(j - 1)
            ln_root(3)
            for j in range(4):
                act.wait_ge(T["nt_ps"], j + 1)
                cp(N1T[:, 512 * j:512 * j + 512], ps[:, j, :]).then_inc(T["nt_sb"], 1)
            for j in range(4):
                act.wait_ge(T["rh_ps"], j + 1)
                act.activation(RHS[0:64, 512 * j:512 * j + 512], ps[0:64, 4 + j, :], ACT.Relu, bias=W("rb1")[0:64, :]).then_inc(T["rh_sb"], 1)

            def hidden(n):
                for p in range(3):
                    act.wait_ge(T["l1_ps"], 3 * n + p + 1)
                    act.activation(H1[p], ps[:, (3 * n + p) % 2, :], ACT.Relu, bias=W("eb1")[:, p:p + 1]).then_inc(T["l1_sb"], 1)
                for p in range(3):
                    act.wait_ge(T["l2_ps"], 3 * n + p + 1)
                    act.activation(H2[p], ps[:, 2 + (3 * n + p) % 2, :], ACT.Relu, bias=W("eb2")[:, p:p + 1]).then_inc(T["l2_sb"], 1)

            act.wait_ge(T["lg_sh"], 1)
            act.activation(gt[:, 1], gt[:, 0], ACT.Exp).then_inc(T["lg_exp"], 1)
            hidden(0)
            act.wait_ge(T["g_dif"], 1)
            act.activation(gm[:, 3], gm[:, 2], ACT.Exp).then_inc(T["g_exp"], 1)
            hidden(1)
            act.wait_ge(T["gt_ps"], 1)
            cp(gateT, ps[0:96, 7, 0:256]).then_inc(T["gt_sb"], 1)
            for n in range(2, 8):
                hidden(n)
                act.wait_ge(T["lo_v"], n - 1)
                act.activation(so[:, 2, n - 2], so[:, 1, n - 2], ACT.Sqrt).then_inc(T["lo_std"], 1)
            for n in range(6, 8):
                act.wait_ge(T["lo_v"], n + 1)
                act.activation(so[:, 2, n], so[:, 1, n], ACT.Sqrt).then_inc(T["lo_std"], 1)

        @block.vector
        def _(ve):
            chain = [0]
            step = sem("ve_step")

            def then(ins):
                chain[0] += 1
                ins.then_inc(step, 1)
                ve.wait_ge(step, chain[0])

            tt, ts, cp = ve.tensor_tensor, ve.tensor_scalar, ve.tensor_copy
            ve.memset(dc[:], 0.0)
            ve.memset(Zt[:], 0.0)
            ve.memset(V[:].bitcast(F32), 0.0)
            ve.wait_ge(load_s, 32)
            cp(XT[0:32, 0:128].rearrange("p (a q) -> p a q", q=4), W("q1T")[0:32, :].unsqueeze(1).to_broadcast([32, 32, 4]))
            ve.wait_ge(ci_first, 1)
            tt(ci[:, 1, :], K("col_inv"), ci[:, 0, :], ALU.subtract)
            tt(rf[:, 1, :], K("row_fwd"), rf[:, 0, :], ALU.subtract).then_inc(ci_rest, 1)
            ve.wait_ge(setup_pe, 1)
            cp(q1w2, ps[0:32, 0, 0:16]).then_inc(setup_dve, 1)
            ve.wait_ge(setup_pe, 2)
            for l in range(L):
                tt(qs_all[:, l].rearrange("p v m q -> p (v m) q"), ps[:, 1, 4 * l:4 * l + 4].unsqueeze(1).to_broadcast([128, 16, 4]),
                   K("same").unsqueeze(2).to_broadcast([128, 16, 4]), ALU.mult)
            ve.wait_ge(T["w_ps"], 1)
            ve.wait_ge(wr_zero, 1)
            for i in range(2):
                r = slice(64 * i, 64 * i + 64)
                cp(wb[r, :, 64 * i:64 * i + 64], ps[r, 3, 0:320].rearrange("p (a b) -> p a b", a=5)).then_inc(T["w_rdy"], 1)
            then(cp(comp[:, 0:8], ps[:, 2, 0:8]))
            then(ve.reduce_sum(comp[:, 8:9], comp[:, 3:8], AX.X))
            then(tt(comp[:, 9:10], comp[:, 8:9], W("q1b"), ALU.add))
            then(ts(gxp[:, :], K("gx_part"), comp[:, 1:2], comp[:, 9:10], ALU.mult, ALU.add))
            for xr in range(4):
                a = ts(S0[:, xr, :], K("gy_row"), comp[:, 2:3], gxp[:, xr:xr + 1], ALU.mult, ALU.add)
            a.then_inc(setup_dve, 1)
            for j in range(2):
                ve.wait_ge(e_pe, 2 * j + 2)
                cp(XNT[:, 1024 * j + 512:1024 * j + 1024], ps[:, 2 * j + 1, :]).then_inc(e_dve, 1)
            ve.wait_ge(e_pe, 6)
            cp(US[:, 4:8, :].rearrange("p a b -> p (a b)"), ps[:, 5, :]).then_inc(e_dve, 1)
            dst = UX.rearrange("p m (j h k o) -> p j h k o m", j=2, h=2, o=2)
            for j in range(2):
                ve.wait_ge(e_pe, 7 + j)
                src = ps[:, 6 + j, :].rearrange("p (k h m) -> p k h m", k=4, h=2)
                for h in range(2):
                    a = cp(dst[:, j, h], src[:, :, h, 0:48].rearrange("p k (o m) -> p k o m", o=2))
            a.then_inc(e_dve, 1)
            ve.wait_ge(hc_ps, 1)
            cp(HC, ps[:, 4, 0:PM])
            ve.wait_ge(e_pe, 9)
            xs_copy(cp, 0).then_inc(e_dve, 1)
            then(tt(pb.rearrange("p (a c) -> p a c", a=4), K("quarter").unsqueeze(2).to_broadcast([128, 4, 32]),
                    W("px").unsqueeze(1).to_broadcast([128, 4, 32]), ALU.mult))
            for t in range(BP):
                a = ts(PSEL[:, 128 * t:128 * t + 128], pb, K("of_pair")[:, t:t + 1], None, ALU.mult)
            a.then_inc(psel_ready, 1)
            for t in range(BP):
                ve.wait_ge(h0_ps, t + 1)
                tt(H[:, t].rearrange("p a b c -> p (a b c)"), ps[:, t % 4, 0:PM], HC, ALU.add).then_inc(h0_sb, 1)
            ve.wait_ge(g_init, 1)
            ve.wait_ge(h0_sb, BP)
            ve.sem_inc(g_add, 1)
            ve.sem_inc(h_add, 1)

            def z1(n):
                ve.wait_ge(pe_w1, n + 1)
                tt(Z1[:, :, 0].rearrange("p k i x -> p k (i x)"), ps[:, 4, 0:PM].rearrange("p (k m) -> p k m", k=K6),
                   dc[:].rearrange("p k i x -> p k (i x)"), ALU.add).then_inc(z1_re, 1)
                ve.wait_ge(z1_re, n + 1)
                for kyp in range(2):
                    j0, j1 = slice(64 * kyp, 64 * kyp + 32), slice(64 * kyp + 32, 64 * kyp + 64)
                    cp(Z1[j1, :, 1].rearrange("p k i x -> p k (i x)"), Z1[j0, :, 0].rearrange("p k i x -> p k (i x)")).then_inc(z1_im, 1)
                    ts(Z1[j0, :, 1].rearrange("p k i x -> p k (i x)"), Z1[j1, :, 0].rearrange("p k i x -> p k (i x)"),
                       -1.0, None, ALU.mult).then_inc(z1_im, 1)

            def turn_r(n, i):
                if i == 0:
                    ve.wait_ge(r_ready, 4 * n + 4)
                ve.transpose(RT[:, i].rearrange("p a b c d -> p (a b c d)"), R[:, i].rearrange("p a b c d -> p (a b c d)")).then_inc(rt_ready, 1)

            def copy_zt(n):
                ve.wait_ge(pe_t, n + 1)
                zt_copy(cp, 1).then_inc(zt_1, 1)

            def split_v(n, q, hs=(0, 1)):
                for h in hs:
                    ve.wait_ge(v_first, 4 * n + 2 * q + h + 1)
                    tt(V[HB[1 - h], h, 4 * q:4 * q + 4, :].rearrange("p a b -> p (a b)"), ps[HB[h], 4 + q, :],
                       V[HB[h], h, 4 * q:4 * q + 4, :].rearrange("p a b -> p (a b)"), ALU.subtract).then_inc(v_rest, 1)

            def split_u(n):
                for q in range(2):
                    ve.wait_ge(u_first, 4 * n + 2 * q + 2)
                    for h in range(2):
                        src, (first, rest) = u_parts(q, h)
                        tt(rest, src, first, ALU.subtract).then_inc(u_rest, 1)

            def copy_xs(n):
                ve.wait_ge(pe_d, n + 1)
                xs_copy(cp, 0).then_inc(x_re, 1)

            def add_g(n, t):
                ve.wait_ge(pe_g, n + 1)
                gd = G[:, bass.ds(t, 1)].rearrange("p a i x y -> p (a i x y)")
                tt(gd, gd, ps[:, 3, 0:256], ALU.add).then_inc(g_add, 1)

            def add_h(n, t):
                ve.wait_ge(pe_w2, n + 1)
                hd = H[:, bass.ds(t, 1)].rearrange("p a k i x -> p (a k i x)")
                tt(hd, hd, ps[:, 6, 0:PM], ALU.add).then_inc(h_add, 1)

            with ve.Fori(0, L) as l:
                ve.wait_ge(h_add, l * BP + 1)
                ts(dc[:, 0, :, 0], W("b1")[:, bass.ds(l, 1)].to_broadcast([128, 2]), float(S), None, ALU.mult).then_inc(dc_ready, 1)
                for m in range(1, 18, 2):
                    ve.wait_ge(mix_pe, l * 18 + m + 1)
                    cp(Z[:].rearrange("p a b c d -> p (a b c d)")[:, 512 * m:512 * m + 512], ps[:, m % 4, :]).then_inc(z_dve, 1)
                hdc = H[0:32, :, 0, :, 0]
                ve.scalar_tensor_tensor(out=hdc, in0=W("w2b")[0:32, bass.ds(l, 1)].unsqueeze(2).to_broadcast([32, BP, 2]), scalar=float(S), in1=hdc,
                                        op0=ALU.mult, op1=ALU.add).then_inc(dc_ready, 1)
                ve.wait_ge(dc_ready, 2 * l + 2)
                z1(l * BP)
                copy_zt(l * BP)
                split_v(l * BP, 0)
                split_v(l * BP, 1)
                with ve.Fori(0, BP - 1) as t:
                    n = l * BP + t
                    z1(n + 1)
                    turn_r(n, 0)
                    copy_zt(n + 1)
                    split_u(n)
                    turn_r(n, 1)
                    split_v(n + 1, 0, (0,))
                    copy_xs(n)
                    split_v(n + 1, 0, (1,))
                    add_g(n, t)
                    split_v(n + 1, 1)
                    add_h(n, t)
                n = l * BP + (BP - 1)
                turn_r(n, 0)
                turn_r(n, 1)
                split_u(n)
                copy_xs(n)
                add_h(n, BP - 1)
                add_g(n, BP - 1)

            ve.wait_ge(h_add, L * BP + 1)
            ve.wait_ge(g_add, L * BP + 1)
            gf = G[:].rearrange("p a b c d -> p (a b c d)")
            ve.wait_ge(load_xg, 16 * 64)
            c = slice(6144, 8192)
            ve.scalar_tensor_tensor(out=gf[:, c], in0=Ff[:, c], scalar=comp[:, 0:1], in1=gf[:, c], op0=ALU.mult, op1=ALU.add).then_inc(T["relu_d"], 1)
            b8 = [128, 8, 64]

            def rotate(j):
                c = slice(512 * j, 512 * j + 512)
                for w in range(4):
                    dst = (QT, T0, KT, T1)[w][:, c].rearrange("p (a b) -> p a b", b=64)
                    ve.wait_ge(T["qk_ps"], 4 * j + w + 1)
                    tt(dst, ps[:, w, :].rearrange("p (a b) -> p a b", b=64),
                       K(("cos_q", "sin_q", "cos_k", "sin_k")[w]).unsqueeze(1).to_broadcast(b8), ALU.mult).then_inc(T["qk_mul"], 1)

            def softmax_1(j):
                c = slice(512 * j, 512 * j + 512)
                t0 = T0[:, c].rearrange("p (a b) -> p a b", b=64)
                ve.wait_ge(T["qk_sb"], 2 * j + 2)
                ve.wait_ge(T["s_ps"], j + 1)
                then(tt(t0, ps[:, 4 + j, :].rearrange("p (a b) -> p a b", b=64), K("causal").unsqueeze(1).to_broadcast(b8), ALU.add))
                then(ve.reduce_max(st[:, 0, 8 * j:8 * j + 8], t0, AX.X))
                tt(t0, t0, st[:, 0, 8 * j:8 * j + 8].unsqueeze(2).to_broadcast(b8), ALU.subtract).then_inc(T["s_sh"], 1)

            def softmax_2(j):
                c = slice(512 * j, 512 * j + 512)
                pj = PR[:, c].rearrange("p (a b) -> p a b", b=64)
                ve.wait_ge(T["p_exp"], j + 1)
                then(ve.reduce_sum(st[:, 1, 8 * j:8 * j + 8], pj, AX.X))
                then(ve.reciprocal(st[:, 2, 8 * j:8 * j + 8], st[:, 1, 8 * j:8 * j + 8]))
                tt(pj, pj, st[:, 2, 8 * j:8 * j + 8].unsqueeze(2).to_broadcast(b8), ALU.mult).then_inc(T["p_sb"], 1)

            rotate(0)
            rotate(1)
            softmax_1(0)
            rotate(2)
            softmax_1(1)
            rotate(3)
            softmax_2(0)
            softmax_1(2)
            softmax_2(1)
            softmax_1(3)
            softmax_2(2)
            softmax_2(3)

            def norm_1(j):
                c, g = slice(512 * j, 512 * j + 512), slice(8 * j, 8 * j + 8)
                y3, t3 = [v[:, c].rearrange("p (a b) -> p a b", b=64) for v in (Y1, T0)]
                ve.wait_ge(T["o_ps"], j + 1)
                then(tt(Y1[:, c], ps[:, 4 + j, :], TOK[:, c], ALU.add))
                then(ve.reduce_sum(st[:, 0, g], y3, AX.X))
                then(ts(st[:, 0, g], st[:, 0, g], 1.0 / D, None, ALU.mult))
                tt(t3, y3, st[:, 0, g].unsqueeze(2).to_broadcast(b8), ALU.subtract).then_inc(T["ln_c"], 1)

            def norm_2(j):
                g = slice(8 * j, 8 * j + 8)
                ve.wait_ge(T["ln_sq"], j + 1)
                then(ve.reduce_sum(st[:, 1, g], T1[:, 512 * j:512 * j + 512].rearrange("p (a b) -> p a b", b=64), AX.X))
                ts(st[:, 1, g], st[:, 1, g], 1.0 / D, 1e-5, ALU.mult, ALU.add).then_inc(T["ln_v"], 1)

            def norm_3(j):
                c, g = slice(512 * j, 512 * j + 512), slice(8 * j, 8 * j + 8)
                n3, t3 = [v[:, c].rearrange("p (a b) -> p a b", b=64) for v in (N1, T0)]
                ve.wait_ge(T["ln_std"], j + 1)
                then(ve.reciprocal(st[:, 3, g], st[:, 2, g]))
                tt(n3, t3, st[:, 3, g].unsqueeze(2).to_broadcast(b8), ALU.mult).then_inc(T["n1_sb"], 1)

            norm_1(0)
            norm_1(1)
            norm_2(0)
            norm_1(2)
            norm_2(1)
            norm_3(0)
            norm_1(3)
            norm_2(2)
            norm_3(1)
            norm_2(3)
            norm_3(2)
            norm_3(3)
            b6 = [128, 32, E]
            lg, ex, pr, sel1, sel2, tmp = [gt[:, i] for i in range(6)]

            def per_token(v):
                return v.unsqueeze(2).to_broadcast(b6)

            rank = K("rank").unsqueeze(1).to_broadcast(b6)
            ve.wait_ge(T["lg_ps"], 1)
            then(tt(lg, ps[:, 7, 0:192].rearrange("p (a b) -> p a b", b=E), W("rb2").unsqueeze(1).to_broadcast(b6), ALU.add))
            then(ve.reduce_max(gm[:, 0], lg, AX.X))
            tt(lg, lg, per_token(gm[:, 0]), ALU.subtract).then_inc(T["lg_sh"], 1)
            ve.wait_ge(T["lg_exp"], 1)
            then(ve.reduce_sum(gm[:, 0], ex, AX.X))
            then(ve.reciprocal(gm[:, 1], gm[:, 0]))
            then(tt(pr, ex, per_token(gm[:, 1]), ALU.mult))

            def pick(p, best, sel):
                then(ve.reduce_max(best, p, AX.X))
                then(tt(tmp, p, per_token(best), ALU.is_equal))
                then(tt(tmp, tmp, rank, ALU.mult))
                then(ve.reduce_max(gm[:, 5], tmp, AX.X))
                then(tt(sel, tmp, per_token(gm[:, 5]), ALU.is_equal))

            pick(pr, gm[:, 0], sel1)
            then(ve.scalar_tensor_tensor(out=pr, in0=sel1, scalar=-2.0, in1=pr, op0=ALU.mult, op1=ALU.add))
            pick(pr, gm[:, 1], sel2)
            tt(gm[:, 2], gm[:, 1], gm[:, 0], ALU.subtract).then_inc(T["g_dif"], 1)
            ve.wait_ge(T["g_exp"], 1)
            then(ts(gm[:, 4], gm[:, 3], 1.0, None, ALU.add))
            then(ve.reciprocal(gm[:, 4], gm[:, 4]))
            then(tt(gm[:, 5], gm[:, 3], gm[:, 4], ALU.mult))
            then(tt(sel1, sel1, per_token(gm[:, 4]), ALU.mult))
            then(tt(sel2, sel2, per_token(gm[:, 5]), ALU.mult))
            tt(lg, sel1, sel2, ALU.add).then_inc(T["gate"], 1)
            ve.wait_ge(T["gate"], 1)
            gate = lg.rearrange("p (h i) e -> p h i e", i=2)
            for k in range(4):
                c = slice(512 * k, 512 * k + 512)
                ve.wait_ge(T["nb_ps"], k + 1)
                a = tt(N1[:, c], N1[:, c], ps[:, 7, :], ALU.add).then_inc(T["nb_sb"], 1)
            n1v = N1.rearrange("p (h i d) -> p h i d", i=2, d=D)
            y1v = Y1.rearrange("p (h i d) -> p h i d", i=2, d=D)
            ov = OUT.rearrange("p (h i d) -> p h i d", i=2, d=D)
            gp = GP.rearrange("p (e h d) -> p e h d", e=E, h=4)
            b4 = [128, 4, 64]

            def out_3(n):
                i, j = n // 4, n % 4
                ve.wait_ge(T["lo_std"], n + 1)
                then(ve.reciprocal(so[:, 3, n], so[:, 2, n]))
                tt(ov[:, 4 * j:4 * j + 4, i], y1v[:, 4 * j:4 * j + 4, i], so[:, 3, n].unsqueeze(2).to_broadcast(b4), ALU.mult).then_inc(T["y_sb"], 1)

            for n in range(8):
                i, j = n // 4, n % 4
                for p in range(3):
                    ve.wait_ge(T["l3_ps"], 3 * n + p + 1)
                    pv = ps[:, 4 + p, :].rearrange("p (h e d) -> p e h d", e=2, d=D)
                    for e in range(2):
                        a = tt(gp[:, 2 * p + e], pv[:, e], gate[:, 4 * j:4 * j + 4, i, 2 * p + e].unsqueeze(2).to_broadcast([128, 4, 64]), ALU.mult)
                    a.then_inc(T["l3_rd"], 1)
                ve.wait_ge(T["l3_rd"], 3 * n + 3)
                ve.wait_ge(T["nb_sb"], 4)
                yv = y1v[:, 4 * j:4 * j + 4, i]
                sq = T1[:, 0:256].rearrange("p (h d) -> p h d", d=D)
                then(ve.reduce_sum(yv, gp.rearrange("p e h d -> p h d e"), AX.X))
                then(tt(yv, yv, n1v[:, 4 * j:4 * j + 4, i], ALU.add))
                then(ve.reduce_sum(so[:, 0, n], yv, AX.X))
                then(ts(so[:, 0, n], so[:, 0, n], 1.0 / D, None, ALU.mult))
                then(tt(yv, yv, so[:, 0, n].unsqueeze(2).to_broadcast(b4), ALU.subtract))
                then(tt(sq, yv, yv, ALU.mult))
                then(ve.reduce_sum(so[:, 1, n], sq, AX.X))
                ts(so[:, 1, n], so[:, 1, n], 1.0 / D, 1e-5, ALU.mult, ALU.add).then_inc(T["lo_v"], 1)
                if n >= 2:
                    out_3(n - 2)
            out_3(6)
            out_3(7)

        @block.gpsimd
        def _(po):
            po.memset(w1c[:], 0.0)
            po.memset(w2c[:], 0.0)
            po.memset(wb[:], 0.0)
            po.memset(wr1[:], 0.0)
            po.memset(wr2[:], 0.0)
            po.memset(pbd[:], 0.0).then_inc(wr_zero, 1)
            po.wait_ge(wr_zero, 1)
            po.wait_ge(load_s, 32)
            po.tensor_scalar(fo[:].rearrange("p a b c -> p (a b c)"), K("pick_out"), W("q2"), None, ALU.mult).then_inc(T["prep"], 1)
            for i in range(2):
                r = slice(64 * i, 64 * i + 64)
                po.wait_ge(T["prep"], 2 * i + 1)
                po.tensor_copy(wr1[r, 32 * i:32 * i + 32], W("rw1")[r, :]).then_inc(T["prep"], 1)
                po.wait_ge(T["prep"], 2 * i + 2)
                po.tensor_copy(wr2[32 * i:32 * i + 32, i, :], W("rw2")[32 * i:32 * i + 32, :]).then_inc(T["prep"], 1)
            po.wait_ge(T["prep"], 5)

            def layer_w1_q(l):
                po.wait_ge(load_w12, l * 128 + 128)
                po.sem_inc(waited, 1)
                for kyp in range(2):
                    r = slice(64 * kyp + 32, 64 * kyp + 64)
                    po.tensor_scalar(w1c[r, :], w1c[r, :], -1.0, None, ALU.mult).then_inc(w1_neg, 1)
                    po.wait_ge(w1_neg, l * 2 + kyp + 1)
                    po.sem_inc(waited, 1)
                po.wait_ge(g_add, l * BP + 1)
                po.sem_inc(waited, 1)
                po.tensor_copy(qs[:].rearrange("p a b c -> p (a b c)"), qs_all[:, bass.ds(l, 1)].rearrange("p a b c d -> p (a b c d)")).then_inc(q_cur, 1)
                po.wait_ge(q_cur, l + 1)
                po.sem_inc(waited, 1)

            layer_w1_q(0)
            with po.Fori(1, L) as l:
                po.wait_ge(load_fw, l * 16 + 16)
                po.sem_inc(waited, 1)
                for kyp in range(2):
                    r = slice(64 * kyp + 32, 64 * kyp + 64)
                    po.tensor_scalar(fws[r, :, 0, :], fws[r, :, 0, :], -1.0, None, ALU.mult).then_inc(w_neg, 1)
                    po.wait_ge(w_neg, l * 2 + kyp + 1)
                    po.sem_inc(waited, 1)
                layer_w1_q(l)
            po.wait_ge(mix_pe, L * 18)
            po.memset(Ff[:, 4 * NT:4 * NT + 768], 0.0).then_inc(T["zero"], 1)
            gf = G[:].rearrange("p a b c d -> p (a b c d)")
            po.wait_ge(load_xg, 16 * 64)
            for j in range(3):
                c = slice(2048 * j, 2048 * j + 2048)
                po.tensor_scalar(Ff[:, c], Ff[:, c], comp[:, 0:1], None, ALU.mult).then_inc(T["relu_x"], 1)
                po.wait_ge(T["relu_x"], 2 * j + 1)
                po.wait_ge(g_add, (L - 1) * BP + 8 * (j + 1) + 1)
                po.tensor_tensor(gf[:, c], gf[:, c], Ff[:, c], ALU.add).then_inc(T["relu_x"], 1)
                po.wait_ge(T["relu_x"], 2 * j + 2)
                po.tensor_scalar(gf[:, c], gf[:, c], 0.0, None, ALU.max).then_inc(T["relu_p"], 1)
            po.wait_ge(h_add, L * BP + 1)
            po.tensor_tensor(EB3.rearrange("p (g d) -> p g d", d=D), W("eb3")[0:96, :].unsqueeze(1).to_broadcast([96, 16, D]),
                             K("own")[0:96, :].unsqueeze(2).to_broadcast([96, 16, D]), ALU.mult).then_inc(T["eb3_rdy"], 1)
            po.wait_ge(T["eb3_rdy"], 1)
            for j in range(4):
                c = slice(512 * j, 512 * j + 512)
                po.wait_ge(T["qk_mul"], 4 * j + 2)
                po.tensor_tensor(QT[:, c], QT[:, c], T0[:, c], ALU.add).then_inc(T["qk_sb"], 1)
                po.wait_ge(T["qk_mul"], 4 * j + 4)
                po.tensor_tensor(KT[:, c], KT[:, c], T1[:, c], ALU.add).then_inc(T["qk_sb"], 1)


def kernel(**inputs):
    import concourse.bacc as bacc
    from concourse.bass_utils import run_bass_kernel_spmd as run

    a = {k: np.asarray(v) for k, v in inputs.items()}
    t = {k[7:]: v for k, v in a.items() if k.startswith("L0_tok_")}
    at = {k[8:]: v for k, v in a.items() if k.startswith("L0_attn_")}
    ff = {k[7:]: v for k, v in a.items() if k.startswith("L0_ffn_")}
    w = t["fw"].transpose(0, 5, 2, 1, 4, 6, 3).reshape(L, 2, K6, C, 2 * 12, 2, C)
    w = w.transpose(0, 1, 3, 2, 4, 5, 6)
    fw = np.stack([w, w[:, :, :, :, :, ::-1]], 2).reshape(L, 128, K6 * NKX * 2 * C)
    w12 = np.stack([t["w1_w"].transpose(0, 2, 1), t["w2_w"].transpose(0, 2, 1)], 1)
    pT = np.concatenate([t["p_w"].T[1:], t["p_b"][None]], 0)
    small = np.zeros((128, NSMALL), np.float32)

    def put(name, v, r0=0):
        c, width = SAT[name]
        v = np.asarray(v).reshape(-1, width)
        small[r0:r0 + v.shape[0], c:c + width] = v

    put("px", np.tile(t["p_w"][:, 0], (128, 1)))
    put("q1T", t["q1_w"].T)
    put("w2n", t["w2_w"].transpose(1, 0, 2))
    put("comps", np.concatenate([t["p_w"], t["p_b"][:, None], t["w2_b"].T], 1))
    put("q1b", np.tile(t["q1_b"], 32))
    put("q2", np.tile(t["q2_w"][0], 32))
    put("q2b", np.tile(t["q2_b"], 128))
    put("b1", t["w1_b"].T)
    put("w2b", t["w2_b"].T)
    put("WqcT", at["Wq_comp"].T)
    put("WkvcT", at["Wkv_comp"].T)
    swap = np.arange(HR) ^ 1
    for n in "qk":
        put("W" + n, np.concatenate([at[f"W{n}c"], at[f"W{n}r"]], 1))
        put("W" + n + "s", np.concatenate([at[f"W{n}c"], at[f"W{n}r"][:, swap]], 1))
    put("Wv", at["Wv"])
    for i in range(2):
        put("rw1", ff["router_w1"], 64 * i)
        put("rw2", ff["router_w2"], 32 * i)
        put("rb1", ff["router_b1"], 32 * i)
    put("rb2", np.tile(ff["router_b2"], (128, 1)))
    put("eb1", ff["expert_b1"].reshape(3, 128).T)
    put("eb2", ff["expert_b2"].reshape(3, 128).T)
    put("eb3", np.tile(ff["expert_b3"], (16, 1)))
    e1 = np.tile(ff["expert_w1"].transpose(1, 0, 2).reshape(D, E * HID), (2, 1))
    e2 = ff["expert_w2"].reshape(3, 128, HID).transpose(1, 0, 2).reshape(128, 192)
    e3 = ff["expert_w3"].reshape(3, 128, D).transpose(1, 0, 2).reshape(128, 192)
    arrays = {"x": a["x"], "fw": fw, "w12": w12, "pT": pT, "small": small,
              "ew": np.concatenate([e1, e2, e3], 1), "const": constants()}
    nc = bacc.Bacc("TRN2", target_bir_lowering=False, num_devices=1)
    maps, args = {}, []
    for name, v in arrays.items():
        v = np.ascontiguousarray(v)
        maps["in_" + name] = v
        args.append(nc.dram_tensor("in_" + name, v.shape, mybir.dt.from_np(v.dtype), kind="ExternalInput").ap())
    o = nc.dram_tensor("out_0", (B, S, S), F32, kind="ExternalOutput").ap()
    program(nc, *args, o)
    r = run(nc, [maps], core_ids=[0])
    return r.results[0]["out_0"]
```
